# Optimizing a Trainium2 kernel written in Bass

```python
import numpy as np
import jax
import jax.numpy as jnp

def _softmax(x, axis=-1):
    return jax.nn.softmax(x, axis=axis)

def _gelu(x):
    return jax.nn.gelu(x, approximate=True)

def _silu(x):
    return jax.nn.silu(x)

def _sigmoid(x):
    return jax.nn.sigmoid(x)

def _layernorm(x, axis=-1, eps=1e-05):
    m = jnp.mean(x, axis=axis, keepdims=True)
    v = jnp.var(x, axis=axis, keepdims=True)
    return (x - m) / jnp.sqrt(v + eps)

def _scatter_add(tgt, idx, src, axis=0):
    return tgt.at[idx].add(src)

def _segment_sum(src, seg, n):
    return jax.ops.segment_sum(src, seg, n)
kernel_name = 'mk_gnn_ffn_d1_gnn_r8_cb0268'

def setup_inputs(seed: int=0):
    np.random.seed(seed)
    _w = jnp.asarray

    def _rec_inputs():
        import jax
        import jax.numpy as jnp
        _gk = jax.random.key(seed)
        x = -0.0003713 + 1 * jax.random.normal(jax.random.fold_in(_gk, 1), (6250, 256), jnp.float32)
        _s = jax.random.randint(jax.random.fold_in(_gk, 2), (100000,), 0, 6250, jnp.int32)
        _d = jax.random.randint(jax.random.fold_in(_gk, 3), (100000,), 0, 6250, jnp.int32)
        _loop = jnp.arange(6250, dtype=jnp.int32)
        src = jnp.concatenate([_s, _d, _loop])
        dst = jnp.concatenate([_d, _s, _loop])
        _o = jnp.argsort(dst, stable=True)
        src = src[_o]
        dst = dst[_o]
        return (x, src, dst)
    x, src, dst = _rec_inputs()

    def _L0_gnn_setup():
        import jax, jax.numpy as jnp
        import numpy as np
        N_NODES = 6250

        def _sage_conv(x, src, dst, W_l, b_l, W_r):
            gathered = jnp.take(x, src, axis=0)
            summed = jax.ops.segment_sum(gathered, dst, num_segments=N_NODES)
            deg = jax.ops.segment_sum(jnp.ones_like(dst, dtype=x.dtype), dst, num_segments=N_NODES)
            mean_nb = summed / jnp.maximum(deg, 1.0)[:, None]
            return mean_nb @ W_l + b_l + x @ W_r
        key = jax.random.key(seed)
        ks = jax.random.split(key, 8)
        d = 256
        E = 100000
        s = 1.0 / np.sqrt(d)
        x = jax.random.normal(ks[0], (N_NODES, d), dtype=jnp.float32)
        ei = jax.random.randint(ks[1], (2, E), 0, N_NODES, dtype=jnp.int64)
        W1_l = jax.random.normal(ks[2], (d, d), dtype=jnp.float32) * s
        b1 = jnp.zeros((d,), dtype=jnp.float32)
        W1_r = jax.random.normal(ks[3], (d, d), dtype=jnp.float32) * s
        W2_l = jax.random.normal(ks[4], (d, d), dtype=jnp.float32) * s
        b2 = jnp.zeros((d,), dtype=jnp.float32)
        W2_r = jax.random.normal(ks[5], (d, d), dtype=jnp.float32) * s
        return {'x': x, 'ei': ei, 'W1_l': W1_l, 'b1': b1, 'W1_r': W1_r, 'W2_l': W2_l, 'b2': b2, 'W2_r': W2_r}
    _L0_gnn_all = _L0_gnn_setup()
    _L0_gnn_in = {k: v for k, v in _L0_gnn_all.items() if k in ('W1_l', 'b1', 'W1_r', 'W2_l', 'b2', 'W2_r')}
    del _L0_gnn_all

    def _L0_ffn_setup():
        import jax, jax.numpy as jnp
        import numpy as np
        TOP_K = 2
        key = jax.random.key(seed)
        ks = jax.random.split(key, 4)
        B, L, D, H, E = (8, 512, 256, 1024, 8)
        s = 0.02
        return {'x': jax.random.normal(ks[0], (B, L, D), jnp.float32), 'Wg': jax.random.normal(ks[1], (D, E), jnp.float32) * s, 'bg': jnp.zeros((E,), jnp.float32), 'W1': jax.random.normal(ks[2], (E, D, H), jnp.float32) * s, 'b1': jnp.zeros((E, H), jnp.float32), 'W2': jax.random.normal(ks[3], (E, H, D), jnp.float32) * s, 'b2': jnp.zeros((E, D), jnp.float32)}
    _L0_ffn_all = _L0_ffn_setup()
    _L0_ffn_in = {k: v for k, v in _L0_ffn_all.items() if k in ('Wg', 'bg', 'W1', 'b1', 'W2', 'b2')}
    del _L0_ffn_all
    return {'x': x, 'src': src, 'dst': dst, 'L0_gnn_W1_l': _L0_gnn_in['W1_l'], 'L0_gnn_b1': _L0_gnn_in['b1'], 'L0_gnn_W1_r': _L0_gnn_in['W1_r'], 'L0_gnn_W2_l': _L0_gnn_in['W2_l'], 'L0_gnn_b2': _L0_gnn_in['b2'], 'L0_gnn_W2_r': _L0_gnn_in['W2_r'], 'L0_ffn_Wg': _L0_ffn_in['Wg'], 'L0_ffn_bg': _L0_ffn_in['bg'], 'L0_ffn_W1': _L0_ffn_in['W1'], 'L0_ffn_b1': _L0_ffn_in['b1'], 'L0_ffn_W2': _L0_ffn_in['W2'], 'L0_ffn_b2': _L0_ffn_in['b2']}

def reference(x, src, dst, L0_gnn_W1_l, L0_gnn_b1, L0_gnn_W1_r, L0_gnn_W2_l, L0_gnn_b2, L0_gnn_W2_r, L0_ffn_Wg, L0_ffn_bg, L0_ffn_W1, L0_ffn_b1, L0_ffn_W2, L0_ffn_b2):
    import jax
    import jax.numpy as jnp

    def _L0_gnn_ref(x, ei, W1_l, b1, W1_r, W2_l, b2, W2_r):
        import jax, jax.numpy as jnp
        import numpy as np
        N_NODES = 6250

        def _sage_conv(x, src, dst, W_l, b_l, W_r):
            gathered = jnp.take(x, src, axis=0)
            summed = jax.ops.segment_sum(gathered, dst, num_segments=N_NODES)
            deg = jax.ops.segment_sum(jnp.ones_like(dst, dtype=x.dtype), dst, num_segments=N_NODES)
            mean_nb = summed / jnp.maximum(deg, 1.0)[:, None]
            return mean_nb @ W_l + b_l + x @ W_r
        src, dst = (ei[0], ei[1])
        h = jax.nn.relu(_sage_conv(x, src, dst, W1_l, b1, W1_r))
        h = _sage_conv(h, src, dst, W2_l, b2, W2_r)
        return h

    def _L0_ffn_ref(x, Wg, bg, W1, b1, W2, b2):
        import jax, jax.numpy as jnp
        import numpy as np
        TOP_K = 2
        B, L, D = x.shape
        E = W1.shape[0]
        xf = x.reshape(-1, D)
        gate_logits = xf @ Wg + bg
        top_w, top_i = jax.lax.top_k(gate_logits, TOP_K)
        top_w = jax.nn.softmax(top_w, axis=-1)
        w_dense = jnp.sum(jax.nn.one_hot(top_i, E, dtype=xf.dtype) * top_w[..., None], axis=1)
        out = jnp.zeros_like(xf)
        for e in range(E):
            h = jax.nn.gelu(xf @ W1[e] + b1[e], approximate=False)
            out = out + w_dense[:, e:e + 1] * (h @ W2[e] + b2[e])
        return out.reshape(B, L, D)
    edge_index = jnp.stack([src, dst])
    x = x + _L0_gnn_ref(_layernorm(x, axis=-1), edge_index, L0_gnn_W1_l, L0_gnn_b1, L0_gnn_W1_r, L0_gnn_W2_l, L0_gnn_b2, L0_gnn_W2_r)
    x = x + _L0_ffn_ref(_layernorm(x, axis=-1)[None], L0_ffn_Wg, L0_ffn_bg, L0_ffn_W1, L0_ffn_b1, L0_ffn_W2, L0_ffn_b2)[0]
    return x

_drawn_inputs = setup_inputs


def setup_inputs(seed=0):
    import zlib

    import numpy as np

    out = dict(_drawn_inputs(seed))
    spreads = {'L0_gnn_b1': (0.0, 0.1),
     'L0_gnn_b2': (0.0, 0.1),
     'L0_ffn_bg': (0.0, 0.1),
     'L0_ffn_b1': (0.0, 0.394),
     'L0_ffn_b2': (0.0, 0.1)}
    factors = {}
    for name, (base, spread) in spreads.items():
        noise = np.random.default_rng([zlib.crc32(name.encode()), seed]).standard_normal(out[name].shape)
        drawn = base * np.exp(spread * noise) if base else spread * noise
        out[name] = jnp.asarray(drawn.astype(out[name].dtype))
    for name, factor in factors.items():
        out[name] = (out[name] * factor).astype(out[name].dtype)
    return out
```

```python
from contextlib import ExitStack

import concourse.bass as bass
from concourse import mybir

F32 = mybir.dt.float32
F16 = mybir.dt.float16
I32 = mybir.dt.int32
U32 = mybir.dt.uint32
ALU = mybir.AluOpType
ACT = mybir.ActivationFunctionType
AX_X = mybir.AxisListType.X
RADD = bass.bass_isa.ReduceOp.add

P = 128
N_NODES = 6250
D = 256
KB = D // P
N_EDGES = 206250
NT = -(-N_NODES // P)
NPAD = NT * P
GRP = 8
GPT = P // GRP
NG = NT * GPT
NQ = 7
GP = NG // NQ
WIN = 3 * P
NC = WIN // P
WINX = WIN + 8
KW = GRP * NT
COARSE = -(-(N_EDGES + WINX) // P)
E_ROWS = COARSE + 8
EPAD = E_ROWS * P
ECH = -(-N_EDGES // P)
DST_PAD = 8191
RING = 4
XSCALE = 1024.0
EPS = 1e-5

NE = 8
H = 1024
HC = H // P
FT = 256
CAPR = NPAD + FT
NF = NPAD * 2 // FT + NE
QT = 7
NX = NT // QT
EARLY = 3
T_AT, D_AT, M_AT, H_AT = 6, 9, 3, 12
T2_AT, D2_AT, X2_AT, G2_AT = 7, 15, 31, 41
XT_AT, YT_AT = 4, 1
WE = 4 * 2048
NW = 4 * NE

S_W1, S_W2, S_WG, S_E1, S_E2, S_H, S_G = range(7)


class Chain:

    def __init__(self, eng, sem):
        self.eng, self.sem, self.start, self.n = eng, sem, 0, 0

    def link(self, ins):
        ins.then_inc(self.sem, 1)
        self.n += 1
        self.eng.wait_ge(self.sem, self.start + self.n)

    def at(self, start):
        self.start, self.n = start, 0


def build(nc, x, src, dst, W1l, b1, W1r, W2l, b2, W2r, Wg, bg, E1, eb1, E2, eb2, out):
    def dram(name, shape, dt):
        return nc.dram_tensor(name, shape, dt, kind="Internal").ap()

    adj_d = dram("adj_d", (NT, P, NT * P), F16)
    coarse_d = dram("coarse_d", (COARSE,), I32)
    deg_d = dram("deg_d", (NPAD,), F32)
    split_d = dram("split_d", (NE, P, WE), F16)
    table_d = dram("table_d", (NPAD, 2 * D), F16)
    xs_d = dram("xs_d", (NE * CAPR, 2 * D), F16)
    y_d = dram("y_d", (NF * FT, D), F32)
    x1_d = dram("x1_d", (NPAD, D), F32)

    with ExitStack() as ctx:
        def sb(name, shape, dt):
            return ctx.enter_context(nc.sbuf_tensor(name, shape, dt))

        def pb(name, shape, dt=F32):
            return ctx.enter_context(nc.psum_tensor(name, shape, dt))

        def sem(name):
            return ctx.enter_context(nc.semaphore(name))

        arena = sb("arena", [P, NE * WE], F16)

        def part(base, first, size, dt=F16, parts=P):
            n = size if dt == F16 else 2 * size
            v = base[0:parts, first:first + n]
            return v if dt == F16 else v.bitcast(dt)

        xs = part(arena, 0, NT * 512).rearrange("p (t c) -> p t c", c=512)
        hs = part(arena, NT * 512, NT * 512).rearrange("p (t c) -> p t c", c=512)
        A0 = 2 * NT * 512
        adj = [part(arena, A0 + i * NT * P, NT * P) for i in range(2)]
        wts = arena[:, :].rearrange("p (e w) -> p e w", w=WE)
        o = NT * 512
        xraw = [part(arena, o + i * 2 * QT * D, QT * D, F32).rearrange("p (t c) -> p t c", c=D) for i in range(2)]
        o += 4 * QT * D
        wd = part(arena, o, NQ * WINX, I32, GP).rearrange("p (q w) -> p q w", w=WINX)
        dl = part(arena, o, NQ * WINX, F32, GP).rearrange("p (q w) -> p q w", w=WINX)
        o += 2 * NQ * WINX
        ws = part(arena, o, NQ * WINX, I32, GP).rearrange("p (q w) -> p q w", w=WINX)
        o += 2 * NQ * WINX
        crow = part(arena, o, COARSE, I32, GP)
        sblk = part(arena, o, NQ * WIN, I32, GP).rearrange("p (q w) -> p q w", w=WIN)
        wfine = part(arena, o + 2 * COARSE, NQ * P, I32, GP).rearrange("p (q w) -> p q w", w=P)
        assert o + 2 * NQ * WIN <= A0 and o + 2 * COARSE + 2 * NQ * P <= A0
        o = A0
        erow = [part(arena, o + 2 * i * E_ROWS, E_ROWS, I32) for i in range(2)]
        o += 4 * E_ROWS
        wraw = [part(arena, o + i * 2048, 1024, F32) for i in range(2)]
        o += 4096
        wsage = part(arena, o, 4 * KB * D, F32).rearrange("p (m k c) -> p m k c", m=4, k=KB)
        assert o + 8 * KB * D <= NE * WE and EARLY * WE <= NT * 512

        work = sb("work", [P, 2 * 6656], F16)
        w_in = [part(work, i * 2048, 1024, F32) for i in range(2)]
        w_sc = part(work, 4096, 1024, F32)
        w_hl = [part(work, 6144 + i * 2048, 2048) for i in range(2)]
        xl = [part(work, i * 1024, 1024).rearrange("p (h c) -> p h c", h=2) for i in range(2)]
        xT = [part(work, 2048 + i * 1024, 1024).rearrange("p (b n) -> p b n", b=4) for i in range(2)]
        gel = [part(work, 4096 + i * 512, FT, F32) for i in range(2)]
        ghl = [part(work, 5120 + i * 512, 2 * FT).rearrange("p (b n) -> p b n", b=2) for i in range(4)]
        yt = [part(work, 7168 + i * 1024, 2 * D, F32).rearrange("p (h c) -> p h c", h=2) for i in range(2)]
        eb2b = part(work, 9216, NE * D, F32).rearrange("p (e c) -> p e c", e=NE)
        zrow = part(work, 0, 2 * D)
        yg = [[part(arena, (2 * i + k) * 512, D, F32) for k in range(2)] for i in range(4)]
        xf = [part(arena, 4096 + i * 512, D, F32) for i in range(4)]
        of = [part(arena, 6144 + i * 512, D, F32) for i in range(4)]

        onehots = sb("onehots", [P, RING * NC * (P + KW)], F16)
        oh1 = part(onehots, 0, RING * NC * P).rearrange("p (r c n) -> p r c n", r=RING, c=NC)
        oh2 = part(onehots, RING * NC * P, RING * NC * KW).rearrange("p (r c n) -> p r c n", r=RING, c=NC)
        key = [part(onehots, k * NQ * WIN, NQ * WIN, F16, GP).rearrange("p (q w) -> p q w", w=WIN) for k in range(2)]
        xres = [part(onehots, i * 512, D, F32) for i in range(2)]
        x1t = [part(onehots, 1024 + i * 512, D, F32) for i in range(2)]
        x2s = part(onehots, 2048, D, F32)
        x2 = [part(onehots, 2560 + i * 512, 512) for i in range(2)]
        x2T = part(onehots, 3584, 512).rearrange("p (b n) -> p b n", b=4)
        grow = part(onehots, 4096, 512)
        goh = part(onehots, 4608, P)

        keys = sb("keys", [P, 2, NC, NG], F16)
        keyt = [sb(f"keyt{i}", [P, 2, NC, GPT], F32) for i in range(2)]
        iota = sb("iota", [P, KW], F16)
        ident = sb("ident", [P, P], F16)
        ones = sb("ones", [P, P], F16)
        ltri = sb("ltri", [P, P], F16)
        bnd_i = sb("bnd_i", [GP, NQ], I32)
        bnd = sb("bnd", [GP, NQ], F32)
        cnt = sb("cnt", [GP, 4, NQ], F32)
        row_i = sb("row_i", [GP, NQ], I32)
        lo_i = sb("lo_i", [GP, NQ], I32)
        junk = sb("junk", [P, E_ROWS + 1], F16)
        iota_i = part(junk, 0, KW, I32)
        deg8 = sb("deg8", [GP, NQ, GRP], F32)
        deg = sb("deg", [P, NT], F32)
        rdeg = sb("rdeg", [P, NT], F32)
        viol = sb("viol", [P, 2], F32)
        violr = sb("violr", [P, 2], F32)
        flag = sb("flag", [P, 1], I32)
        stats = sb("stats", [P, QT, 6], F32)
        mv = sb("mv", [P, NT, 2], F32)
        sd = sb("sd", [P, NT], F32)
        rs = sb("rs", [P, NT], F32)
        nmr = sb("nmr", [P, NT], F32)
        epst = sb("epst", [P, 1], F32)
        wsplit = sb("wsplit", [P, 4, KB, 2, D], F16)
        wgate = sb("wgate", [P, KB, NE], F32)
        wgs = sb("wgs", [P, KB, 2, NE], F16)
        biasb = sb("biasb", [P, 2, D], F32)
        bgb = sb("bgb", [P, NE], F32)
        eb1T = sb("eb1T", [P, NE, HC], F32)
        sq = sb("sq", [P, 1024], F16)
        ss = sb("ss", [P, 7 + NW], F32)
        ssum = sb("ssum", [P, 7], F32)
        ssall = sb("ssall", [P, 7], F32)
        bound = sb("bound", [P, 7], F32)
        p2 = sb("p2", [P, 7], I32)
        ip2 = sb("ip2", [P, 7], I32)
        scl = sb("scl", [P, 7], F32)
        inv = sb("inv", [P, 7], F32)
        cc = sb("cc", [P, 5], F32)
        meanhl = [sb(f"meanhl{i}", [P, 512], F16) for i in range(2)]
        mT = sb("mT", [P, 4, P], F16)
        nT = sb("nT", [P, 4, P], F16)
        tmp = sb("tmp", [P, D], F32)
        st2 = sb("st2", [P, 6], F32)
        mv2 = sb("mv2", [P, 2], F32)
        sd2 = sb("sd2", [P, 1], F32)
        rs2 = sb("rs2", [P, 1], F32)
        lg = sb("lg", [P, NE], F32)
        m8 = sb("m8", [P, 8], F32)
        i8 = sb("i8", [P, 8], U32)
        e01 = sb("e01", [P, 2], F32)
        ecap_i = sb("ecap_i", [P, NE], I32)
        ecap = sb("ecap", [P, NE], F32)
        sel = sb("sel", [P, 2, NE], F32)
        mask = sb("mask", [P, NE], F16)
        msum = sb("msum", [P, NE], F16)
        rk = sb("rk", [P, NE], F32)
        jk = sb("jk", [P, 2, NE], F32)
        posf = sb("posf", [P, 2], F32)
        posi = [[sb(f"posi{i}{k}", [P, 1], I32) for k in range(2)] for i in range(2)]
        posall = sb("posall", [P, NT, 2], F32)
        eall = sb("eall", [P, NT, 2], F16)
        posg = [[sb(f"posg{i}{k}", [P, 1], I32) for k in range(2)] for i in range(4)]
        diff = sb("diff", [P, NT], F32)
        zz = sb("zz", [P, NT], F32)
        zp = sb("zp", [P, NT], F32)
        past = part(onehots, 5120, 2 * NT, F32).rearrange("p (t k) -> p t k", k=2)
        wt = sb("wt", [P, 2, NT], F32)
        cntb = sb("cntb", [P, NE], F32)
        cti = sb("cti", [P, 2, NE], I32)
        nte = sb("nte", [P, NE], F32)
        cend = sb("cend", [P, NE], F32)
        pad_b = sb("pad_b", [P, 2, NE], I32)
        pad_bf = sb("pad_bf", [P, 2, NE], F32)
        pad_f = sb("pad_f", [P, 2, NE], F32)
        pad_i = sb("pad_i", [P, 2, NE], I32)
        fi_i = sb("fi_i", [1, NF], I32)
        ftab = sb("ftab", [1, 7, NF], F32)
        tab = sb("tab", [1, 3, NF], I32)
        gsrc = sb("gsrc", [P, 1], I32)
        gdst = sb("gdst", [P, 1], I32)
        gkey = sb("gkey", [P, 2], F32)
        gtile = sb("gtile", [P, 1], F32)
        zeros = sb("zeros", [P, D], F16)

        bank = [pb(f"bank{i}", [P, 512]) for i in range(8)]
        cps = bank[0:2]
        acc = bank[2:4]
        tpm, tpx, dps, gps = bank[4:8]
        lgp, rkp, cnp, dgp = gps[:, 0:8], gps[:, 8:16], gps[:, 16:24], gps[:, 24:25]
        hps = bank[0:4]
        yps = [b.rearrange("p (h c) -> p h c", h=2) for b in bank[4:6]]
        xtp = [b.rearrange("p (b n) -> p b n", b=2) for b in bank[6:8]]

        s_const = sem("s_const")
        s_coarse_raw = sem("s_coarse_raw")
        s_coarse = sem("s_coarse")
        s_x = [sem(f"s_xin{i}") for i in range(2)]
        s_erow = sem("s_erow")
        s_small = sem("s_small")
        s_wraw = [sem(f"s_wraw{i}") for i in range(2)]
        s_wraw_used = sem("s_wraw_used")
        s_row = sem("s_row")
        s_fine = sem("s_fine")
        s_lo = sem("s_lo")
        s_win = sem("s_win")
        s_key = sem("s_key")
        s_keyT = sem("s_keyT")
        s_keyc = sem("s_keyc")
        s_iota = sem("s_iota")
        s_dve = sem("s_dve")
        s_act = sem("s_act")
        s_pool = sem("s_pool")
        s_stats = sem("s_stats")
        s_sd = sem("s_sd")
        s_norm = sem("s_norm")
        s_xn = sem("s_xn")
        s_xs = sem("s_xs")
        s_ss = sem("s_ss")
        s_ssum = sem("s_ssum")
        s_ssall = sem("s_ssall")
        s_bound = sem("s_bound")
        s_scales = sem("s_scales")
        s_wsplit = sem("s_wsplit")
        s_viol = sem("s_viol")
        s_violr = sem("s_violr")
        s_flag = sem("s_flag")
        s_deg = sem("s_deg")
        s_deg_out = sem("s_deg_out")
        s_deg_in = sem("s_deg_in")
        s_oh = sem("s_oh")
        s_cnt = sem("s_cnt")
        s_evac = sem("s_evac")
        s_acc = [sem(f"s_acc_l{i}") for i in range(2)]
        s_mean = [sem(f"s_mean_l{i}") for i in range(2)]
        s_t = [sem(f"s_t_l{i}") for i in range(2)]
        s_tc = [sem(f"s_tc_l{i}") for i in range(2)]
        s_dense = [sem(f"s_dense_l{i}") for i in range(2)]
        s_h = sem("s_h")
        s_adj_out = [sem(f"s_adj_out{i}") for i in range(2)]
        s_adj_in = [sem(f"s_adj_in{i}") for i in range(2)]
        s_xres = [sem(f"s_xres{i}") for i in range(2)]
        s_x1 = sem("s_x1")
        s_x1_out = [sem(f"s_x1_out{i}") for i in range(2)]
        s_var2 = sem("s_var2")
        s_sd2 = sem("s_sd2")
        s_x2 = sem("s_x2")
        s_x2t = sem("s_x2t")
        s_x2tc = sem("s_x2tc")
        s_logits = sem("s_logits")
        s_mask = sem("s_mask")
        s_rank = sem("s_rank")
        s_pos = sem("s_pos")
        s_scat = [sem(f"s_scat{i}") for i in range(2)]
        s_cntp = sem("s_cntp")
        s_pads = sem("s_pads")
        s_pads_out = sem("s_pads_out")
        s_tab = sem("s_tab")
        s_z = sem("s_z")
        s_win_w = [sem(f"s_win_w{i}") for i in range(2)]
        s_whl_out = [sem(f"s_whl_out{i}") for i in range(2)]
        s_late = sem("s_late")
        s_eb2 = sem("s_eb2")
        s_rows = [sem(f"s_rows{i}") for i in range(2)]
        s_xt = sem("s_xt")
        s_xtc = sem("s_xtc")
        s_hid = sem("s_hid")
        s_gel = sem("s_gel")
        s_g = sem("s_g")
        s_mm2 = sem("s_mm2")
        s_y = sem("s_y")
        s_y_out = [sem(f"s_y_out{i}") for i in range(2)]
        s_ready = sem("s_ready")
        s_idx = sem("s_idx")
        s_yg = [sem(f"s_yg{i}") for i in range(4)]
        s_xf = [sem(f"s_xf{i}") for i in range(4)]
        s_fin = sem("s_fin")
        s_out = [sem(f"s_out{i}") for i in range(4)]
        s_table = sem("s_table")
        s_alone_dve = sem("s_alone_dve")
        s_alone_pool = sem("s_alone_pool")
        s_dve2 = sem("s_dve2")
        s_dve3 = sem("s_dve3")
        s_gh = sem("s_gh")
        s_half = sem("s_half")
        s_gkey = sem("s_gkey")
        s_gedge = sem("s_gedge")
        s_goh = sem("s_goh")
        s_grow = sem("s_grow")
        s_gmm = sem("s_gmm")
        block = ctx.enter_context(nc.Block())

        def even(n):
            return [(n + 1) // 2, n // 2]

        def wchunk(e, w):
            if w < 2:
                return E1[bass.ds(e, 1), w * P:(w + 1) * P, :].rearrange("a p n -> (a p) n")
            return E2[bass.ds(e, 1), (w - 2) * 512:(w - 1) * 512, :].rearrange("a (c p) n -> p (a c) n", p=P)

        def wview(buf, w):
            return buf if w < 2 else buf.rearrange("p (c n) -> p c n", n=D)

        tables = [xs, hs]

        @block.sync
        def _(sp):
            with nc.allow_non_contiguous_dma(reason="every 128th destination"):
                sp.dma_start(coarse_d.rearrange("(n a) -> n a", a=1),
                             dst[0:COARSE * P].rearrange("(n a) -> n a", a=P)[:, 0:1]).then_inc(s_coarse_raw, 16)

            def load_x(q):
                sp.dma_start(xraw[q % 2], x[q * QT * P:(q + 1) * QT * P, :].rearrange("(t p) c -> p t c", p=P)
                             ).then_inc(s_x[q % 2], 16)

            def load_w(e, w, first=False):
                if not first:
                    sp.wait_ge(s_wraw_used, 4 * e + w - 1)
                sp.dma_start(wview(wraw[w % 2], w), wchunk(e, w)).then_inc(s_wraw[w % 2], 16)
            load_x(0)
            load_x(1)
            sp.wait_ge(s_coarse_raw, 16)
            sp.dma_start(crow, coarse_d.rearrange("(a n) -> a n", a=1).to_broadcast([GP, COARSE])
                         ).then_inc(s_coarse, 16)
            for i in range(2):
                sp.dma_start(erow[i], dst[i:EPAD + i].rearrange("(p n) -> p n", p=P)).then_inc(s_erow, 16)
            for m, w in enumerate((W1l, W1r, W2l, W2r)):
                sp.dma_start(wsage[:, m], w.rearrange("(k p) c -> p k c", p=P)).then_inc(s_small, 16)
            for i, b in enumerate((b1, b2)):
                sp.dma_start(biasb[:, i, :], b.rearrange("(a c) -> a c", a=1).to_broadcast([P, D])
                             ).then_inc(s_small, 16)
            sp.dma_start(bgb[:, :], bg.rearrange("(a c) -> a c", a=1).to_broadcast([P, NE])).then_inc(s_small, 16)
            sp.dma_start(wgate[:, :, :], Wg.rearrange("(k p) e -> p k e", p=P)).then_inc(s_small, 16)
            with nc.allow_non_contiguous_dma(reason="hidden units onto partitions"):
                sp.dma_start(eb1T[:, :, :], eb1.rearrange("e (c p) -> p e c", p=P)).then_inc(s_small, 16)
            load_w(0, 0, True)
            load_w(0, 1, True)
            load_w(0, 2)
            load_w(0, 3)
            for q in range(2, NX):
                sp.wait_ge(s_xs, q - 1)
                load_x(q)
                for w in range(4):
                    load_w(q - 1, w)
            with sp.Fori(NX - 1, NE) as e:
                for w in range(4):
                    load_w(e, w)
            sp.wait_ge(s_deg, 1)
            sp.dma_start(deg_d.rearrange("(q p d) -> p q d", p=GP, d=GRP), deg8[:, :, :]).then_inc(s_deg_out, 16)
            sp.wait_ge(s_deg_out, 16)
            with nc.allow_non_contiguous_dma(reason="nodes onto partitions"):
                sp.dma_start(deg[:, :], deg_d.rearrange("(t p) -> p t", p=P)).then_inc(s_deg_in, 16)

            def general(layer):
                sp.wait_ge(s_h if layer else s_xs, NT if layer else NX)
                with sp.Fori(0, NT) as t:
                    sp.dma_start(table_d[bass.ds(t * P, P), :], tables[layer][:, bass.ds(t, 1), :].rearrange(
                        "p a c -> p (a c)")).then_inc(s_table, 16)
                sp.wait_ge(s_table, 16 * NT * (layer + 1))

                def tile(t, slot, first=False):
                    if layer:
                        load_res(t, slot, first)
                    with sp.Fori(0, ECH) as c:
                        n = (t + layer * NT) * ECH + c
                        sp.wait_ge(s_gmm, n + 1)
                        for chunk, edges in ((gsrc, src), (gdst, dst)):
                            sp.dma_start(chunk[:, :], edges[bass.ds(c * P, P)].rearrange("(p a) -> p a", a=1)
                                         ).then_inc(s_gedge, 16)
                tile(0, 0, True)
                tile(1, 1, True)
                with sp.Fori(1, NT // 2) as i:
                    tile(2 * i, 0)
                    tile(2 * i + 1, 1)
                tile(NT - 1, 0)

            def load_res(t, slot, first):
                if not first:
                    sp.wait_ge(s_x1, t - 1)
                sp.dma_start(xres[slot], x[bass.ds(t * P, P), :]).then_inc(s_xres[slot], 16)

            sp.wait_ge(s_flag, 1)
            bad = sp.value_load(flag[0:1, 0:1], min_val=0, max_val=1)
            with sp.If(bad < 1):
                def store_adj(u, slot):
                    sp.wait_ge(s_evac, GPT * u + GPT)
                    sp.dma_start(adj_d[bass.ds(u, 1), :, :].rearrange("a p n -> (a p) n"), adj[slot]
                                 ).then_inc(s_adj_out[slot], 16)
                with sp.Fori(0, NT // 2) as i:
                    store_adj(2 * i, 0)
                    store_adj(2 * i + 1, 1)
                store_adj(NT - 1, 0)
            with sp.Else():
                general(0)
            sp.wait_ge(s_t[0], NT)
            for i in range(2):
                sp.wait_ge(s_whl_out[i], 16 * NW // 2)
            sp.dma_start(wts[:, 0:EARLY, :], split_d[0:EARLY].rearrange("e p w -> p e w")).then_inc(s_late, 16)
            with sp.If(bad < 1):
                for i in range(2):
                    sp.wait_ge(s_adj_out[i], 16 * even(NT)[i])

                def load_adj(t, slot, first=False):
                    if not first:
                        sp.wait_ge(s_acc[1], t - 1)
                    sp.dma_start(adj[slot], adj_d[bass.ds(t, 1), :, :].rearrange("a p n -> (a p) n")
                                 ).then_inc(s_adj_in[slot], 16)
                    load_res(t, slot, first)
                sp.wait_ge(s_acc[0], NT)
                load_adj(0, 0, True)
                load_adj(1, 1, True)
                with sp.Fori(1, NT // 2) as i:
                    load_adj(2 * i, 0)
                    load_adj(2 * i + 1, 1)
                load_adj(NT - 1, 0)
            with sp.Else():
                general(1)

            sp.wait_ge(s_t[1], NT)
            sp.wait_ge(s_acc[1], NT)
            sp.wait_ge(s_late, 16)
            sp.dma_start(eb2b, eb2.rearrange("e c -> (e c)").rearrange("(a n) -> a n", a=1).to_broadcast(
                [P, NE * D])).then_inc(s_eb2, 16)

            def load_rows(f, slot):
                r = sp.value_load(tab[0:1, 1, bass.ds(f, 1)], min_val=0, max_val=NE * CAPR - FT)
                sp.dma_start(xl[slot], xs_d[bass.ds(r, FT), :].rearrange("(h p) c -> p h c", p=P)
                             ).then_inc(s_rows[slot], 16)
            for e in range(EARLY, NE):
                sp.dma_start(wts[:, e, :], split_d[e]).then_inc(s_late, 16)
                sp.wait_ge(s_late, 16 * (e - EARLY + 2))
                if e == EARLY:
                    sp.wait_ge(s_tab, 1)
                    for i in range(2):
                        sp.wait_ge(s_scat[i], 32 * even(NT)[i])
                    sp.wait_ge(s_pads_out, 16 * 2 * NE)
                    load_rows(0, 0)
                    load_rows(1, 1)

            def step(f, slot, load=True):
                if load:
                    sp.wait_ge(s_xt, f)
                    load_rows(f + 1, 1 - slot)
                sp.wait_ge(s_y, f)
                sp.dma_start(y_d[bass.ds((f - 1) * FT, FT), :].rearrange("(h p) c -> p h c", p=P), yt[1 - slot]
                             ).then_inc(s_y_out[1 - slot], 16)
            step(1, 1)
            with sp.Fori(1, (NF - 1) // 2) as i:
                step(2 * i, 0)
                step(2 * i + 1, 1)
            step(NF - 1, 0, load=False)
            step(NF, 1, load=False)
            for i in range(2):
                sp.wait_ge(s_y_out[i], 16 * even(NF)[i])
                sp.wait_ge(s_x1_out[i], 16 * even(NT)[i])
            sp.wait_ge(s_mm2, NF * HC)
            sp.nop().then_inc(s_ready, 1)

            def load_x1(t, slot):
                sp.wait_ge(s_idx, t + 1)
                sp.dma_start(xf[slot], x1_d[bass.ds(t * P, P), :]).then_inc(s_xf[slot], 16)
            with sp.Fori(0, NT // 4) as i:
                for slot in range(4):
                    load_x1(4 * i + slot, slot)
            load_x1(NT - 1, 0)

        @block.gpsimd
        def _(pool):
            ch = Chain(pool, s_pool)
            pool.iota(iota_i[:, :], pattern=[[1, KW]], base=0, channel_multiplier=0)
            pool.iota(bnd_i[:, :], pattern=[[GRP * GP, NQ]], base=0, channel_multiplier=GRP)
            pool.iota(ecap_i[:, :], pattern=[[CAPR, NE]], base=0, channel_multiplier=0)
            pool.iota(pad_b[:, :, :], pattern=[[P, 2], [CAPR, NE]], base=0, channel_multiplier=1)
            pool.iota(fi_i[:, :], pattern=[[1, NF]], base=0, channel_multiplier=0)
            pool.memset(epst[:, :], EPS / XSCALE ** 2)
            pool.memset(ones[:, :], 1.0).then_inc(s_const, 1)
            ch.link(pool.memset(ident[:, :], 0.0))
            pool.affine_select(out=ident[:, :], in_=ident[:, :], compare_op=ALU.not_equal, fill=1.0, base=0,
                               pattern=[[-1, P]], channel_multiplier=1).then_inc(s_const, 1)
            pool.affine_select(out=ltri[:, :], in_=ones[:, :], compare_op=ALU.is_gt, fill=0.0, base=0,
                               pattern=[[1, P]], channel_multiplier=-1).then_inc(s_const, 1)
            pool.memset(msum[:, :], 0.0).then_inc(s_const, 1)

            def low_x(q):
                pool.wait_ge(s_xn, q + 1)
                t = slice(q * QT, (q + 1) * QT)
                pool.tensor_tensor(xs[:, t, D:2 * D], xraw[q % 2], xs[:, t, 0:D], ALU.subtract).then_inc(s_xs, 1)
            low_x(0)
            low_x(1)
            pool.wait_ge(s_row, 1)
            for q in range(NQ):
                pool.indirect_dma_start(wfine[:, q, :], None, dst[0:EPAD].rearrange("(n a) -> n a", a=P),
                                        bass.IndirectOffsetOnAxis(ap=row_i[:, q:q + 1], axis=0)
                                        ).then_inc(s_fine, 16)
            low_x(2)
            pool.wait_ge(s_lo, 1)
            for q in range(NQ):
                for win, a in ((wd, dst), (ws, src)):
                    pool.indirect_dma_start(win[:, q, :], None, a[0:EPAD].rearrange("(n a) -> n a", a=1),
                                            bass.IndirectOffsetOnAxis(ap=lo_i[:, q:q + 1], axis=0)
                                            ).then_inc(s_win, 16)
            for q in range(3, NX):
                low_x(q)
            pool.wait_ge(s_viol, 1)
            pool.partition_all_reduce(violr[:, :], viol[:, :], P, RADD).then_inc(s_violr, 1)
            pool.wait_ge(s_ssum, 1)
            pool.partition_all_reduce(ssall[:, :], ssum[:, :], P, RADD).then_inc(s_ssall, 1)

            def load_w(e, w):
                pool.dma_start(wview(w_in[w % 2], w), wchunk(e, w)).then_inc(s_win_w[w % 2], 16)

            def split_w(e, w, first=False, last=False):
                n = 4 * e + w
                pool.wait_ge(s_win_w[w % 2], 32 * e + 16 * (w // 2) + 16)
                pool.nop().then_inc(s_alone_pool, 1)
                scale = scl[:, S_E1:S_E1 + 1] if w < 2 else scl[:, S_E2:S_E2 + 1]
                ch.link(pool.tensor_scalar(w_sc, w_in[w % 2], scale, None, ALU.mult))
                if not last:
                    load_w(e + w // 2, (w + 2) % 4)
                if not first:
                    pool.wait_ge(s_whl_out[w % 2], 32 * e + 16 * (w // 2))
                pool.nop().then_inc(s_alone_pool, 1)
                ch.link(pool.tensor_copy(w_hl[w % 2][:, 0:1024], w_sc))
                ch.link(pool.tensor_tensor(w_hl[w % 2][:, 1024:2048], w_sc, w_hl[w % 2][:, 0:1024], ALU.subtract))
                pool.dma_start(split_d[bass.ds(e, 1), :, w * 2048:(w + 1) * 2048].rearrange("a p n -> (a p) n"),
                               w_hl[w % 2]).then_inc(s_whl_out[w % 2], 16)

            pool.wait_ge(s_scales, 1)
            load_w(0, 0)
            load_w(0, 1)
            for w in range(4):
                split_w(0, w, first=w < 2)
            base = ch.n
            with pool.Fori(1, NE - 1) as e:
                ch.at(base + 12 * (e - 1))
                for w in range(4):
                    split_w(e, w)
            ch.at(base + 12 * (NE - 2))
            for w in range(4):
                split_w(NE - 1, w, last=w >= 2)

            pool.wait_ge(s_flag, 1)
            bad = pool.value_load(flag[0:1, 0:1], min_val=0, max_val=1)

            def gathers(t, layer):
                with pool.Fori(0, ECH) as c:
                    n = (t + layer * NT) * ECH + c
                    pool.wait_ge(s_gedge, 32 * n + 32)
                    pool.nop().then_inc(s_alone_pool, 1)
                    pool.indirect_dma_start(grow, None, table_d, bass.IndirectOffsetOnAxis(ap=gsrc[:, 0:1], axis=0)
                                            ).then_inc(s_grow, 16)
                    pool.wait_ge(s_grow, 16 * n + 16)

            def scatter(p, slot):
                pool.wait_ge(s_pos, p + 1)
                pool.nop().then_inc(s_alone_pool, 1)
                for k in range(2):
                    pool.indirect_dma_start(xs_d, bass.IndirectOffsetOnAxis(ap=posi[slot][k][:, 0:1], axis=0),
                                            x2[slot], None).then_inc(s_scat[slot], 16)

            with pool.If(bad < 1):
                with pool.Fori(0, NT // 2) as i:
                    scatter(2 * i, 0)
                    scatter(2 * i + 1, 1)
                scatter(NT - 1, 0)
            with pool.Else():
                pool.wait_ge(s_table, 16 * NT)
                with pool.Fori(0, NT) as t:
                    gathers(t, 0)
                pool.wait_ge(s_table, 32 * NT)
                with pool.Fori(0, NT // 2) as i:
                    for slot in range(2):
                        gathers(2 * i + slot, 1)
                        scatter(2 * i + slot, slot)
                gathers(NT - 1, 1)
                scatter(NT - 1, 0)
            ch.link(pool.memset(zrow, 0.0))
            pool.wait_ge(s_pads, 1)
            for k in range(2):
                for e in range(NE):
                    pool.indirect_dma_start(xs_d, bass.IndirectOffsetOnAxis(ap=pad_i[:, k, e:e + 1], axis=0),
                                            zrow, None).then_inc(s_pads_out, 16)

            pool.wait_ge(s_ready, 1)
            base = ch.start + ch.n

            def gather(t, slot):
                for k in range(2):
                    ch.link(pool.tensor_copy(posg[slot][k][:, 0:1], posall[:, bass.ds(t, 1), k]))
                pool.nop().then_inc(s_idx, 1)
                for k in range(2):
                    pool.indirect_dma_start(yg[slot][k], None, y_d,
                                            bass.IndirectOffsetOnAxis(ap=posg[slot][k][:, 0:1], axis=0)
                                            ).then_inc(s_yg[slot], 16)
            for slot in range(4):
                gather(slot, slot)
            with pool.Fori(1, NT // 4) as i:
                ch.at(base + 8 * i)
                for slot in range(4):
                    pool.wait_ge(s_out[slot], 16 * i)
                    gather(4 * i + slot, slot)
            ch.at(base + 8 * (NT // 4))
            pool.wait_ge(s_out[0], 16 * (NT // 4))
            gather(NT - 1, 0)

        @block.scalar
        def _(act):
            ch = Chain(act, s_act)
            act.wait_ge(s_const, 4)
            act.activation(iota[:, :], iota_i[:, :], ACT.Copy).then_inc(s_iota, 1)
            act.activation(bnd[:, :], bnd_i[:, :], ACT.Copy).then_inc(s_iota, 1)
            act.activation(ecap[:, :], ecap_i[:, :], ACT.Copy).then_inc(s_iota, 1)
            act.activation(pad_bf[:, :, :], pad_b[:, :, :], ACT.Copy).then_inc(s_iota, 1)
            act.activation(ftab[:, 0, :], fi_i[:, :], ACT.Copy).then_inc(s_iota, 1)

            def norm_x(q):
                t = slice(q * QT, (q + 1) * QT)
                act.wait_ge(s_stats, q + 1)
                act.activation(sd[:, t], mv[:, t, 1], ACT.Sqrt, bias=epst[:, 0:1], scale=XSCALE ** -2
                               ).then_inc(s_sd, 1)
                act.wait_ge(s_norm, q + 1)
                for j in range(QT):
                    u = q * QT + j
                    last = act.activation(xraw[q % 2][:, j, :], xraw[q % 2][:, j, :], ACT.Identity,
                                          bias=nmr[:, u:u + 1], scale=rs[:, u:u + 1])
                ch.link(last)
                act.activation(xs[:, t, 0:D], xraw[q % 2], ACT.Copy).then_inc(s_xn, 1)

            def square(view, col):
                n = view.shape[1] * (view.shape[2] if len(view.shape) == 3 else 1)
                v = sq[:, 0:n].rearrange("p (a b) -> p a b", a=view.shape[1]) if len(view.shape) == 3 else sq[:, 0:n]
                ch.link(act.activation(v, view, ACT.Square, accum_out=ss[:, col:col + 1]))

            def square_w(e, w):
                act.wait_ge(s_wraw[w % 2], 32 * e + 16 * (w // 2) + 16)
                col = ss[:, 7 + w:8 + w] if isinstance(e, int) and e == 0 else ss[:, bass.ds(4 * e + w + 7, 1)]
                act.activation(sq[:, :], wraw[w % 2], ACT.Square, accum_out=col).then_inc(s_wraw_used, 1)
                act.wait_ge(s_wraw_used, 4 * e + w + 1)

            norm_x(0)
            norm_x(1)
            act.wait_ge(s_small, 16 * 9)
            for m in range(4):
                square(wsage[:, m], m)
            square(wgate[:, :, :], 4)
            square(biasb[:, 0, :], 5)
            square(eb1T[:, :, :], 6)
            for w in range(4):
                square_w(0, w)
            for q in range(2, NX):
                norm_x(q)
                for w in range(4):
                    square_w(q - 1, w)
            with act.Fori(NX - 1, NE) as e:
                for w in range(4):
                    square_w(e, w)
            act.nop().then_inc(s_ss, 1)
            for q in range(NQ):
                act.wait_ge(s_keyT, q + 1)
                for k in range(2):
                    act.activation(keys[:, k, :, q * GP:(q + 1) * GP],
                                   bank[2 * (q % 2) + k][:, 0:NC * GP].rearrange("p (c g) -> p c g", c=NC), ACT.Copy
                                   ).then_inc(s_keyc, 1)
            act.wait_ge(s_ssall, 1)
            act.activation(bound[:, :], ssall[:, :], ACT.Sqrt).then_inc(s_bound, 1)

            def t_copy(p, layer):
                act.wait_ge(s_t[layer], p + 1)
                act.activation(mT[:, :, :], tpm[:, :].rearrange("p (b n) -> p b n", b=4), ACT.Copy
                               ).then_inc(s_tc[layer], 1)
                act.activation(nT[:, :, :], tpx[:, :].rearrange("p (b n) -> p b n", b=4), ACT.Copy
                               ).then_inc(s_tc[layer], 1)

            def evac(u, slot, j):
                act.wait_ge(s_cnt, GPT * u + j + 1)
                view = adj[slot].rearrange("p (a n) -> p n a", a=NT)[:, GRP * j:GRP * (j + 1), :]
                act.activation(view, cps[j % 2][:, 0:KW].rearrange("p (n a) -> p n a", n=GRP), ACT.Copy
                               ).then_inc(s_evac, 1)

            def step1(t, slot, build=True, post=True):
                for j in range(GPT):
                    if build:
                        evac(t + 1, 1 - slot, j)
                    if post and j == T_AT:
                        t_copy(t - 1, 0)

            act.wait_ge(s_flag, 1)
            bad = act.value_load(flag[0:1, 0:1], min_val=0, max_val=1)
            with act.If(bad < 1):
                act.wait_ge(s_wsplit, 1)
                for j in range(GPT):
                    evac(0, 0, j)
                step1(0, 0, post=False)
                act.wait_ge(s_acc[0], 1)
                act.wait_ge(s_adj_out[0], 16)
                step1(1, 1)
                with act.Fori(1, (NT - 1) // 2) as i:
                    for k in range(2):
                        act.wait_ge(s_acc[0], 2 * i + k)
                        act.wait_ge(s_adj_out[1 - k], 16 * (i + k))
                        step1(2 * i + k, k)
                step1(NT - 1, 0, build=False)
                t_copy(NT - 1, 0)
            with act.Else():
                with act.Fori(0, NT) as t:
                    t_copy(t, 0)

            def post2(p):
                t_copy(p, 1)
                act.wait_ge(s_var2, p + 1)
                act.activation(sd2[:, :], mv2[:, 1:2], ACT.Sqrt, bias=epst[:, 0:1], scale=XSCALE ** -2
                               ).then_inc(s_sd2, 1)
                act.wait_ge(s_x2t, p + 1)
                act.activation(x2T, tpm[:, :].rearrange("p (b n) -> p b n", b=4), ACT.Copy).then_inc(s_x2tc, 1)

            def store_x1(p, slot):
                act.wait_ge(s_x1, p + 1)
                act.dma_start(x1_d[bass.ds(p * P, P), :], x1t[slot]).then_inc(s_x1_out[slot], 16)
            with act.Fori(0, NT // 2) as i:
                for slot in range(2):
                    post2(2 * i + slot)
                    store_x1(2 * i + slot, slot)
            post2(NT - 1)
            store_x1(NT - 1, 0)
            act.wait_ge(s_z, 1)
            act.activation(zz[:, :], diff[:, :], ACT.Exp).then_inc(s_z, 1)

            act.wait_ge(s_tab, 1)

            def xt_copy(f, slot):
                act.wait_ge(s_xt, f + 1)
                act.activation(xT[slot][:, 0:2, :], xtp[0], ACT.Copy).then_inc(s_xtc, 1)

            def step(f, slot, nxt=True, first=False):
                e = act.value_load(tab[0:1, 0, bass.ds(f, 1)], min_val=0, max_val=NE - 1)
                for c in range(HC):
                    act.wait_ge(s_hid, HC * f + c + 1)
                    if not (first and c < 2):
                        act.wait_ge(s_g, HC * f + c - 1)
                    act.activation(gel[c % 2], hps[c % 4][:, 0:FT], ACT.Gelu,
                                   bias=eb1T[:, bass.ds(e, 1), c], scale=cc[:, 3:4]).then_inc(s_gel, 1)
                    if nxt and c == XT_AT:
                        xt_copy(f + 1, 1 - slot)
            xt_copy(0, 0)
            step(0, 0, first=True)
            with act.Fori(0, (NF - 3) // 2) as i:
                step(2 * i + 1, 1)
                step(2 * i + 2, 0)
            step(NF - 2, 1)
            step(NF - 1, 0, nxt=False)

            def leave(t, slot):
                act.wait_ge(s_fin, t + 1)
                act.dma_start(out[bass.ds(t * P, P), :], of[slot]).then_inc(s_out[slot], 16)
            with act.Fori(0, NT // 4) as i:
                for slot in range(4):
                    leave(4 * i + slot, slot)
            leave(NT - 1, 0)
            for slot in range(4):
                act.wait_ge(s_out[slot], 16 * len(range(slot, NT, 4)))

        @block.tensor
        def _(pe):
            pe.wait_ge(s_const, 4)
            pe.wait_ge(s_key, 1)
            for q in range(NQ):
                if q >= 2:
                    pe.wait_ge(s_keyc, 2 * (q - 1))
                for k in range(2):
                    for c in range(NC):
                        last = pe.matmul(bank[2 * (q % 2) + k][:, c * GP:(c + 1) * GP],
                                         key[k][:, q, c * P:(c + 1) * P], ident[0:GP, 0:GP], start=True, stop=True)
                last.then_inc(s_keyT, 1)

            def count(u, j, first=False):
                n = GPT * u + j
                pe.wait_ge(s_oh, n + 1)
                if not first:
                    pe.wait_ge(s_evac, n - 1)
                for c in range(NC):
                    last = pe.matmul(cps[j % 2][:, 0:KW], oh1[:, j % RING, c, :], oh2[:, j % RING, c, :],
                                     start=(c == 0), stop=(c == NC - 1))
                last.then_inc(s_cnt, 1)

            def sums(slot, table, a0, a1):
                for a in range(a0, a1):
                    for h in range(2):
                        last = pe.matmul(acc[slot][:, 0:D], adj[slot][:, a * P:(a + 1) * P],
                                         table[:, a, h * D:(h + 1) * D],
                                         start=(a == 0 and h == 0), stop=(a == NT - 1 and h == 1))
                return last

            def turn(p, slot, layer):
                pe.wait_ge(s_mean[layer], p + 1)
                for b in range(4):
                    pe.matmul(tpm[:, b * P:(b + 1) * P], meanhl[slot][:, b * P:(b + 1) * P], ident[:, :],
                              start=True, stop=True)
                for b in range(4):
                    last = pe.matmul(tpx[:, b * P:(b + 1) * P],
                                     tables[layer][:, bass.ds(p, 1), b * P:(b + 1) * P].rearrange("p a c -> p (a c)"),
                                     ident[:, :], start=True, stop=True)
                last.then_inc(s_t[layer], 1)

            def dense(p, layer):
                pe.wait_ge(s_tc[layer], 2 * p + 2)
                n = 0
                for m, rows in enumerate((mT, nT)):
                    for k in range(KB):
                        for ra, wb in ((0, 0), (0, 1), (1, 0)):
                            last = pe.matmul(dps[:, 0:D], rows[:, 2 * ra + k, :], wsplit[:, 2 * layer + m, k, wb, :],
                                             start=(n == 0), stop=(n == 11))
                            n += 1
                last.then_inc(s_dense[layer], 1)

            def step1(t, slot, build=True, post=True, reuse=True):
                pe.wait_ge(s_evac, GPT * t + GPT)
                if reuse:
                    pe.wait_ge(s_mean[0], t - 1)
                for j in range(GPT):
                    if build:
                        count(t + 1, j)
                    last = sums(slot, xs, 3 * j, 3 * j + 3 if j < GPT - 1 else NT)
                    if post and j == T_AT:
                        turn(t - 1, 1 - slot, 0)
                    if post and j == D_AT:
                        if reuse:
                            pe.wait_ge(s_h, t - 1)
                        dense(t - 1, 0)
                last.then_inc(s_acc[0], 1)

            pe.nop().then_inc(s_gmm, 1)
            pe.wait_ge(s_flag, 1)
            pe.wait_ge(s_xs, NX)
            pe.wait_ge(s_wsplit, 1)
            bad = pe.value_load(flag[0:1, 0:1], min_val=0, max_val=1)

            def general(t, slot, layer):
                pe.matmul(acc[slot][:, 0:D], zeros[:, 0:P], zeros[:, 0:D], start=True, stop=False)
                if not layer:
                    pe.matmul(dgp, zeros[:, 0:P], zeros[:, 0:1], start=True, stop=False)
                with pe.Fori(0, ECH) as c:
                    n = (t + layer * NT) * ECH + c
                    pe.wait_ge(s_goh, n + 1)
                    pe.wait_ge(s_grow, 16 * n + 16)
                    if not layer:
                        pe.matmul(dgp, goh, ones[:, 0:1], start=False, stop=False)
                    pe.matmul(acc[slot][:, 0:D], goh, grow[:, 0:D], start=False, stop=False)
                    pe.matmul(acc[slot][:, 0:D], goh, grow[:, D:2 * D], start=False, stop=False).then_inc(s_gmm, 1)
                if not layer:
                    pe.matmul(dgp, zeros[:, 0:P], zeros[:, 0:1], start=False, stop=True)
                pe.matmul(acc[slot][:, 0:D], zeros[:, 0:P], zeros[:, 0:D], start=False, stop=True
                          ).then_inc(s_acc[layer], 1)

            with pe.If(bad < 1):
                for j in range(GPT):
                    count(0, j, first=j < 2)
                step1(0, 0, post=False, reuse=False)
                step1(1, 1, reuse=False)
                with pe.Fori(1, (NT - 1) // 2) as i:
                    step1(2 * i, 0)
                    step1(2 * i + 1, 1)
                step1(NT - 1, 0, build=False)
                turn(NT - 1, 0, 0)
                pe.wait_ge(s_h, NT - 1)
                dense(NT - 1, 0)
            with pe.Else():
                def tile(t, slot, first=False):
                    general(t, slot, 0)
                    turn(t, slot, 0)
                    if not first:
                        pe.wait_ge(s_h, t)
                    dense(t, 0)
                tile(0, 0, True)
                tile(1, 1)
                with pe.Fori(1, NT // 2) as i:
                    tile(2 * i, 0)
                    tile(2 * i + 1, 1)
                tile(NT - 1, 0)

            pe.wait_ge(s_h, NT)

            def turn_x2(p, slot):
                pe.wait_ge(s_x2, p + 1)
                for b in range(4):
                    last = pe.matmul(tpm[:, b * P:(b + 1) * P], x2[slot][:, b * P:(b + 1) * P], ident[:, :],
                                     start=True, stop=True)
                last.then_inc(s_x2t, 1)

            def gate(p, first=False):
                pe.wait_ge(s_x2tc, p + 1)
                if not first:
                    pe.wait_ge(s_pos, p)
                n = 0
                for k in range(KB):
                    for ra, wb in ((0, 0), (0, 1), (1, 0)):
                        last = pe.matmul(lgp, x2T[:, 2 * ra + k, :], wgs[:, k, wb, :], start=(n == 0), stop=(n == 5))
                        n += 1
                last.then_inc(s_logits, 1)

            def rank(p):
                pe.wait_ge(s_mask, p + 1)
                pe.matmul(rkp, ones[:, :], msum[:, :], start=True, stop=False)
                pe.matmul(rkp, ltri[:, :], mask[:, :], start=False, stop=True).then_inc(s_rank, 1)

            def free_dense(p, first):
                if not first:
                    pe.wait_ge(s_x1, p)

            def step2(t, slot, loads, post=True, reuse=True, first=False):
                pe.wait_ge(s_adj_in[slot], loads)
                if reuse:
                    pe.wait_ge(s_mean[1], t - 1)
                a = 0
                if post:
                    for stop, what in ((T2_AT, "turn"), (D2_AT, "dense"), (X2_AT, "x2"), (G2_AT, "gate")):
                        sums(slot, hs, a, stop)
                        a = stop
                        if what == "turn":
                            turn(t - 1, 1 - slot, 1)
                        elif what == "dense":
                            free_dense(t - 1, first)
                            dense(t - 1, 1)
                        elif what == "x2":
                            turn_x2(t - 1, 1 - slot)
                        else:
                            gate(t - 1, first)
                sums(slot, hs, a, NT).then_inc(s_acc[1], 1)
                if post:
                    rank(t - 1)

            def whole_post(p, slot, first=False):
                turn(p, slot, 1)
                free_dense(p, first)
                dense(p, 1)
                turn_x2(p, slot)
                gate(p, first)
                rank(p)

            with pe.If(bad < 1):
                step2(0, 0, 16, post=False, reuse=False)
                step2(1, 1, 16, reuse=False, first=True)
                with pe.Fori(1, (NT - 1) // 2) as i:
                    step2(2 * i, 0, 16 * i + 16)
                    step2(2 * i + 1, 1, 16 * i + 16)
                step2(NT - 1, 0, 16 * ((NT + 1) // 2))
                whole_post(NT - 1, 0)
            with pe.Else():
                def tile(t, slot, first=False):
                    general(t, slot, 1)
                    whole_post(t, slot, first)
                tile(0, 0, True)
                tile(1, 1)
                with pe.Fori(1, NT // 2) as i:
                    tile(2 * i, 0)
                    tile(2 * i + 1, 1)
                tile(NT - 1, 0)
            pe.wait_ge(s_pos, NT)
            pe.matmul(cnp, ones[:, :], msum[:, :], start=True, stop=True).then_inc(s_cntp, 1)

            pe.wait_ge(s_tab, 1)

            def turn_rows(f, slot, loads, first=False):
                pe.wait_ge(s_rows[slot], loads)
                if not first:
                    pe.wait_ge(s_xtc, 2 * f)
                for b in range(4):
                    for h in range(2):
                        last = pe.matmul(xtp[b // 2][:, b % 2, h * P:(h + 1) * P], xl[slot][:, h, b * P:(b + 1) * P],
                                         ident[:, :], start=True, stop=True)
                last.then_inc(s_xt, 1)

            def hidden(f, c, slot, e, first=False):
                if not first:
                    pe.wait_ge(s_gel, HC * f + c - 3)
                n = 0
                for k in range(KB):
                    for wa, rb in ((0, 0), (0, 1), (1, 0)):
                        o = k * 2048 + wa * 1024 + c * P
                        last = pe.matmul(hps[c % 4][:, 0:FT], wts[:, bass.ds(e, 1), o:o + P].rearrange(
                            "p a n -> p (a n)"), xT[slot][:, 2 * rb + k, :], start=(n == 0), stop=(n == 5))
                        n += 1
                last.then_inc(s_hid, 1)

            def output(f, c, slot, e, first=False):
                if c == 0 and not first:
                    pe.wait_ge(s_y, f - 1)
                pe.wait_ge(s_g, HC * f + c + 1)
                for h in range(2):
                    for ga, wb in ((0, 0), (0, 1), (1, 0)):
                        o = (2 + c // 4) * 2048 + wb * 1024 + (c % 4) * D
                        last = pe.matmul(yps[slot][:, h, :], ghl[c % 4][:, ga, h * P:(h + 1) * P],
                                         wts[:, bass.ds(e, 1), o:o + D].rearrange("p a n -> p (a n)"),
                                         start=(c == 0 and h == 0 and (ga, wb) == (0, 0)),
                                         stop=(c == HC - 1 and (ga, wb) == (1, 0)), skip_group_check=True)
                last.then_inc(s_mm2, 1)

            def expert_of(f):
                return pe.value_load(tab[0:1, 0, bass.ds(f, 1)], min_val=0, max_val=NE - 1)

            def step(f, slot, loads=None, nxt=True, prev=True, first=False, second=False):
                e = expert_of(f)
                ep = expert_of(f - 1) if prev else None
                need = pe.value_load(tab[0:1, 2, bass.ds(f, 1)], min_val=16, max_val=16 * NE)
                pe.wait_ge(s_late, need)
                pe.wait_ge(s_xtc, 2 * f + 2)
                for c in range(HC):
                    hidden(f, c, slot, e, first=first and c < 4)
                    if c >= 2:
                        output(f, c - 2, slot, e, first=first or second)
                    elif prev:
                        output(f - 1, HC - 2 + c, 1 - slot, ep)
                    if nxt and c == XT_AT - 1:
                        turn_rows(f + 1, 1 - slot, loads)
            turn_rows(0, 0, 16, first=True)
            step(0, 0, 16, prev=False, first=True)
            step(1, 1, 32, second=True)
            with pe.Fori(1, (NF - 1) // 2) as i:
                step(2 * i, 0, 16 * i + 16)
                step(2 * i + 1, 1, 16 * i + 32)
            step(NF - 1, 0, nxt=False)
            e = expert_of(NF - 1)
            for c in (HC - 2, HC - 1):
                output(NF - 1, c, 0, e)

        @block.vector
        def _(dve):
            ch = Chain(dve, s_dve)

            def norm_x(q):
                dve.wait_ge(s_x[q % 2], 16 * (q // 2 + 1))
                t = slice(q * QT, (q + 1) * QT)
                for j in range(QT):
                    last = dve.bn_stats(stats[:, j, :], xraw[q % 2][:, j, :])
                ch.link(last)
                for j in range(QT):
                    last = dve.bn_aggr(mv[:, q * QT + j, :], stats[:, j, :])
                last.then_inc(s_stats, 1)
                dve.wait_ge(s_sd, q + 1)
                ch.link(dve.reciprocal(rs[:, t], sd[:, t]))
                dve.scalar_tensor_tensor(out=nmr[:, t], in0=mv[:, t, 0], scalar=-1.0, in1=rs[:, t],
                                         op0=ALU.mult, op1=ALU.mult).then_inc(s_norm, 1)

            dve.memset(zeros[:, :], 0.0)
            norm_x(0)
            norm_x(1)
            dve.wait_ge(s_iota, 5)
            dve.wait_ge(s_coarse, 16)
            for q in range(NQ):
                ch.link(dve.tensor_scalar(junk[0:GP, 0:COARSE], crow, bnd[:, q:q + 1], 0.0, ALU.is_lt, ALU.add,
                                          accum_out=cnt[:, 0, q:q + 1]))
            ch.link(dve.tensor_scalar(cnt[:, 1, :], cnt[:, 0, :], -1.0, 0.0, ALU.add, ALU.max))
            dve.tensor_copy(row_i[:, :], cnt[:, 1, :]).then_inc(s_row, 1)
            dve.wait_ge(s_erow, 32)
            ch.link(dve.tensor_tensor_reduce(out=junk[:, 0:E_ROWS], in0=erow[0], in1=erow[1], scale=1.0, scalar=0.0,
                                             op0=ALU.subtract, op1=ALU.max, accum_out=viol[:, 0:1]))
            norm_x(2)
            dve.wait_ge(s_fine, 16 * NQ)
            for q in range(NQ):
                ch.link(dve.tensor_scalar(junk[0:GP, 0:P], wfine[:, q, :], bnd[:, q:q + 1], 0.0, ALU.is_lt, ALU.add,
                                          accum_out=cnt[:, 2, q:q + 1]))
            ch.link(dve.scalar_tensor_tensor(out=cnt[:, 3, :], in0=cnt[:, 1, :], scalar=float(P), in1=cnt[:, 2, :],
                                             op0=ALU.mult, op1=ALU.add))
            dve.tensor_copy(lo_i[:, :], cnt[:, 3, :]).then_inc(s_lo, 1)
            for q in range(3, NX):
                norm_x(q)
            dve.wait_ge(s_win, 32 * NQ)
            for q in range(NQ):
                last = dve.tensor_scalar(dl[:, q, :], wd[:, q, :], bnd[:, q:q + 1], 64.0, ALU.subtract, ALU.min)
            ch.link(last)
            ch.link(dve.tensor_scalar(sblk, ws[:, :, 0:WIN], 7, None, ALU.logical_shift_right))
            for q in range(NQ):
                dve.scalar_tensor_tensor(out=key[0][:, q, :], in0=sblk[:, q, :], scalar=-float(P),
                                         in1=ws[:, q, 0:WIN], op0=ALU.mult, op1=ALU.add)
                last = dve.scalar_tensor_tensor(out=key[1][:, q, :], in0=dl[:, q, 0:WIN], scalar=float(NT),
                                                in1=sblk[:, q, :], op0=ALU.mult, op1=ALU.add)
            last.then_inc(s_key, 1)
            ch.link(dve.memset(viol[:, 1:2], 0.0))
            ch.link(dve.tensor_scalar(cnt[:, 0, :], dl[:, :, WIN], float(GRP), 0.0, ALU.is_lt, ALU.add,
                                      accum_out=viol[0:GP, 1:2]))
            dve.nop().then_inc(s_viol, 1)
            for q in range(NQ):
                for d in range(GRP):
                    i = (q * GRP + d) % 4
                    last = dve.tensor_scalar(junk[0:GP, i * WIN:(i + 1) * WIN], dl[:, q, 0:WIN], float(d), 0.0,
                                             ALU.is_equal, ALU.add, accum_out=deg8[:, q, d:d + 1])
                    if i == 3:
                        ch.link(last)
            dve.nop().then_inc(s_deg, 1)
            dve.wait_ge(s_ss, 1)
            ch.link(dve.tensor_copy(ssum[:, 2:7], ss[:, 2:7]))
            dve.tensor_tensor(ssum[:, 0:1], ss[:, 0:1], ss[:, 1:2], ALU.add)
            dve.tensor_tensor(ssum[:, 1:2], ss[:, 2:3], ss[:, 3:4], ALU.add)
            dve.tensor_copy(ssum[:, 2:3], ss[:, 4:5])
            sw = ss[:, 7:7 + NW].rearrange("p (e k w) -> p k e w", k=2, w=2)
            for k in range(2):
                last = dve.tensor_reduce(ssum[:, 3 + k:4 + k], sw[:, k], mybir.AxisListType.XY, ALU.add)
            ch.link(last)
            dve.nop().then_inc(s_ssum, 1)
            dve.wait_ge(s_violr, 1)
            ch.link(dve.tensor_tensor(viol[:, 0:1], violr[:, 0:1], violr[:, 1:2], ALU.add))
            dve.tensor_scalar(flag[:, :], viol[:, 0:1], 1.0, None, ALU.min).then_inc(s_flag, 1)

            dve.wait_ge(s_bound, 1)
            ch.link(dve.tensor_scalar(bound[:, :], bound[:, :], 1.01, 1e-15, ALU.mult, ALU.max))
            ch.link(dve.scalar_tensor_tensor(out=bound[:, S_H:S_H + 1], in0=bound[:, S_W1:S_W1 + 1], scalar=23.0,
                                             in1=bound[:, S_H:S_H + 1], op0=ALU.mult, op1=ALU.add))
            ch.link(dve.scalar_tensor_tensor(out=bound[:, S_G:S_G + 1], in0=bound[:, S_E1:S_E1 + 1], scalar=16.1,
                                             in1=bound[:, S_G:S_G + 1], op0=ALU.mult, op1=ALU.add))
            ch.link(dve.tensor_scalar(p2[:, :], bound[:, :].bitcast(I32), 0x7F800000, None, ALU.bitwise_and))
            ch.link(dve.tensor_scalar(ip2[:, :], p2[:, :], -1.0, float(0x7F000000), ALU.mult, ALU.add))
            ch.link(dve.tensor_scalar(scl[:, :], ip2[:, :].bitcast(F32), 8192.0, None, ALU.mult))
            ch.link(dve.tensor_scalar(inv[:, :], p2[:, :].bitcast(F32), 1.0 / 8192.0, None, ALU.mult))

            def factor(i, a, b, k):
                ch.link(dve.scalar_tensor_tensor(out=cc[:, i:i + 1], in0=a, scalar=k, in1=b,
                                                 op0=ALU.mult, op1=ALU.mult))
            factor(0, scl[:, S_H:S_H + 1], inv[:, S_W1:S_W1 + 1], 1.0 / XSCALE)
            factor(1, inv[:, S_H:S_H + 1], inv[:, S_W2:S_W2 + 1], 1.0)
            ch.link(dve.tensor_scalar(cc[:, 2:3], inv[:, S_WG:S_WG + 1], 1.0 / XSCALE, None, ALU.mult))
            ch.link(dve.tensor_scalar(cc[:, 3:4], inv[:, S_E1:S_E1 + 1], 1.0 / XSCALE, None, ALU.mult))
            factor(4, inv[:, S_G:S_G + 1], inv[:, S_E2:S_E2 + 1], 1.0)
            ch.link(dve.tensor_scalar(biasb[:, 0, :], biasb[:, 0, :], scl[:, S_H:S_H + 1], None, ALU.mult))
            dve.nop().then_inc(s_scales, 1)
            for m in range(4):
                sc = scl[:, S_W1 + m // 2:S_W1 + m // 2 + 1]
                ch.link(dve.tensor_scalar(wsplit[:, m, :, 0, :], wsage[:, m], sc, None, ALU.mult))
                dve.scalar_tensor_tensor(out=wsplit[:, m, :, 1, :], in0=wsage[:, m], scalar=sc,
                                         in1=wsplit[:, m, :, 0, :], op0=ALU.mult, op1=ALU.subtract)
            sc = scl[:, S_WG:S_WG + 1]
            ch.link(dve.tensor_scalar(wgs[:, :, 0, :], wgate[:, :, :], sc, None, ALU.mult))
            ch.link(dve.scalar_tensor_tensor(out=wgs[:, :, 1, :], in0=wgate[:, :, :], scalar=sc, in1=wgs[:, :, 0, :],
                                             op0=ALU.mult, op1=ALU.subtract))
            dve.nop().then_inc(s_wsplit, 1)
            dve.wait_ge(s_deg_in, 16)
            ch.link(dve.tensor_scalar(deg[:, :], deg[:, :], 1.0, None, ALU.max))
            ch.link(dve.reciprocal(rdeg[:, :], deg[:, :]))
            dve.wait_ge(s_keyc, 2 * NQ)

            def start_tile(u, slot):
                ch.link(dve.tensor_copy(keyt[slot][:, :, :, :], keys[:, :, :, bass.ds(u * GPT, GPT)]))

            def onehots_of(u, slot, j, first=False):
                if not first:
                    dve.wait_ge(s_cnt, GPT * u + j - RING + 1)
                for c in range(NC):
                    dve.tensor_scalar(oh1[:, j % RING, c, :], iota[:, 0:P], keyt[slot][:, 0, c, j:j + 1], None,
                                      ALU.is_equal)
                    last = dve.tensor_scalar(oh2[:, j % RING, c, :], iota[:, :], keyt[slot][:, 1, c, j:j + 1], None,
                                             ALU.is_equal)
                last.then_inc(s_oh, 1)

            def mean(p, slot, layer):
                dve.wait_ge(s_acc[layer], p + 1)
                r = rdeg[:, bass.ds(p, 1)]
                ch.link(dve.tensor_scalar(meanhl[slot][:, 0:D], acc[slot][:, 0:D], r, None, ALU.mult))
                dve.scalar_tensor_tensor(out=meanhl[slot][:, D:2 * D], in0=acc[slot][:, 0:D], scalar=r,
                                         in1=meanhl[slot][:, 0:D], op0=ALU.mult, op1=ALU.subtract
                                         ).then_inc(s_mean[layer], 1)

            def relu(p):
                dve.wait_ge(s_dense[0], p + 1)
                ch.link(dve.scalar_tensor_tensor(out=tmp[:, :], in0=dps[:, 0:D], scalar=cc[:, 0:1],
                                                 in1=biasb[:, 0, :], op0=ALU.mult, op1=ALU.add))
                hi = hs[:, bass.ds(p, 1), 0:D].rearrange("p a c -> p (a c)")
                lo = hs[:, bass.ds(p, 1), D:2 * D].rearrange("p a c -> p (a c)")
                ch.link(dve.tensor_scalar(hi, tmp[:, :], 0.0, None, ALU.max))
                dve.scalar_tensor_tensor(out=lo, in0=tmp[:, :], scalar=0.0, in1=hi, op0=ALU.max,
                                         op1=ALU.subtract).then_inc(s_h, 1)

            def step1(t, slot, build=True, post=True):
                if build:
                    start_tile(t + 1, 1 - slot)
                for j in range(GPT):
                    if build:
                        onehots_of(t + 1, 1 - slot, j)
                    if post and j == M_AT:
                        mean(t - 1, 1 - slot, 0)
                    if post and j == H_AT:
                        relu(t - 1)

            def general(t, layer):
                gbase = (t + layer * NT) * ECH
                dve.nop().then_inc(s_alone_dve, 1)
                with dve.Fori(0, ECH) as c:
                    n = gbase + c
                    dve.wait_ge(s_gedge, 32 * n + 32)
                    dve.tensor_scalar(gkey[:, 0:1], gdst[:, :], gtile[:, 0:1], None, ALU.subtract).then_inc(s_gkey, 1)
                    dve.wait_ge(s_gkey, n + 1)
                    dve.tensor_scalar(goh, iota[:, 0:P], gkey[:, 0:1], None, ALU.is_equal).then_inc(s_goh, 1)
                dve.wait_ge(s_acc[layer], t + 1)

            def next_tile():
                ch.link(dve.tensor_scalar(gtile[:, 0:1], gtile[:, 0:1], float(P), None, ALU.add))

            def degree(t):
                ch.link(dve.tensor_scalar(gkey[:, 1:2], dgp, 1.0, None, ALU.max))
                ch.link(dve.reciprocal(rdeg[:, bass.ds(t, 1)], gkey[:, 1:2]))

            bad = dve.value_load(flag[0:1, 0:1], min_val=0, max_val=1)
            base = ch.n
            with dve.If(bad < 1):
                start_tile(0, 0)
                for j in range(GPT):
                    onehots_of(0, 0, j, first=j < RING)
                step1(0, 0, post=False)
                step1(1, 1)
                m = ch.n
                with dve.Fori(1, (NT - 1) // 2) as i:
                    ch.at(m + 8 * (i - 1))
                    step1(2 * i, 0)
                    step1(2 * i + 1, 1)
                    assert ch.n == 8
                ch.at(m + 8 * ((NT - 1) // 2 - 1))
                step1(NT - 1, 0, build=False)
                mean(NT - 1, 0, 0)
                relu(NT - 1)
                fast_n = ch.start + ch.n
            with dve.Else():
                ch.at(base)
                ch.link(dve.memset(gtile[:, :], 0.0))

                def tile(t, slot):
                    general(t, 0)
                    degree(t)
                    mean(t, slot, 0)
                    relu(t)
                    next_tile()
                m = ch.start + ch.n
                with dve.Fori(0, NT // 2) as i:
                    ch.at(m + 12 * i)
                    tile(2 * i, 0)
                    tile(2 * i + 1, 1)
                    assert ch.n == 12
                ch.at(m + 12 * (NT // 2))
                tile(NT - 1, 0)
                ch.link(dve.memset(gtile[:, :], 0.0))

            ch2 = Chain(dve, s_dve2)

            def post2(p, slot, first=False):
                link = ch2.link
                dve.wait_ge(s_acc[1], p + 1)
                r = rdeg[:, bass.ds(p, 1)]
                link(dve.tensor_scalar(meanhl[slot][:, 0:D], acc[slot][:, 0:D], r, None, ALU.mult))
                dve.scalar_tensor_tensor(out=meanhl[slot][:, D:2 * D], in0=acc[slot][:, 0:D], scalar=r,
                                         in1=meanhl[slot][:, 0:D], op0=ALU.mult, op1=ALU.subtract
                                         ).then_inc(s_mean[1], 1)
                dve.wait_ge(s_dense[1], p + 1)
                if not first:
                    dve.wait_ge(s_x1_out[slot], 8 * (p - slot))
                link(dve.scalar_tensor_tensor(out=tmp[:, :], in0=dps[:, 0:D], scalar=cc[:, 1:2],
                                              in1=biasb[:, 1, :], op0=ALU.mult, op1=ALU.add))
                dve.wait_ge(s_xres[slot], 8 * (p - slot) + 16)
                dve.tensor_tensor(x1t[slot], tmp[:, :], xres[slot], ALU.add).then_inc(s_x1, 1)
                dve.wait_ge(s_x1, p + 1)
                link(dve.bn_stats(st2[:, :], x1t[slot]))
                dve.nop().then_inc(s_alone_dve, 1)
                dve.bn_aggr(mv2[:, :], st2[:, :]).then_inc(s_var2, 1)
                dve.wait_ge(s_sd2, p + 1)
                link(dve.reciprocal(rs2[:, :], sd2[:, :]))
                link(dve.tensor_scalar(x2s, x1t[slot], mv2[:, 0:1], rs2[:, 0:1], ALU.subtract, ALU.mult))
                if not first:
                    dve.wait_ge(s_scat[slot], 16 * (p - slot))
                link(dve.tensor_copy(x2[slot][:, 0:D], x2s))
                dve.tensor_tensor(x2[slot][:, D:2 * D], x2s, x2[slot][:, 0:D], ALU.subtract).then_inc(s_x2, 1)
                dve.wait_ge(s_logits, p + 1)
                link(dve.scalar_tensor_tensor(out=lg[:, :], in0=lgp, scalar=cc[:, 2:3], in1=bgb[:, :],
                                              op0=ALU.mult, op1=ALU.add))
                dve.nop().then_inc(s_alone_dve, 1)
                link(dve.max(m8[:, :], lg[:, :]))
                dve.nop().then_inc(s_alone_dve, 1)
                link(dve.max_index(i8[:, :], m8[:, :], lg[:, :]))
                dve.tensor_tensor(diff[:, bass.ds(p, 1)], m8[:, 1:2], m8[:, 0:1], ALU.subtract)
                link(dve.tensor_copy(e01[:, :], i8[:, 0:2]))
                for k in range(2):
                    last = dve.tensor_scalar(sel[:, k, :], iota[:, 0:NE], e01[:, k:k + 1], None, ALU.is_equal)
                link(last)
                dve.tensor_tensor(mask[:, :], sel[:, 0, :], sel[:, 1, :], ALU.add).then_inc(s_mask, 1)
                dve.wait_ge(s_rank, p + 1)
                link(dve.tensor_tensor(rk[:, :], rkp, ecap[:, :], ALU.add))
                for k in range(2):
                    last = dve.tensor_tensor_reduce(out=jk[:, k, :], in0=sel[:, k, :], in1=rk[:, :], scale=1.0,
                                                    scalar=0.0, op0=ALU.mult, op1=ALU.add,
                                                    accum_out=posf[:, k:k + 1])
                link(last)
                for k in range(2):
                    dve.tensor_copy(posi[slot][k][:, :], posf[:, k:k + 1])
                dve.tensor_copy(posall[:, bass.ds(p, 1), :], posf[:, :])
                dve.tensor_copy(eall[:, bass.ds(p, 1), :], e01[:, :])
                dve.tensor_tensor(msum[:, :], msum[:, :], mask[:, :], ALU.add).then_inc(s_pos, 1)
                dve.wait_ge(s_pos, p + 1)

            def layer2(tile):
                tile(0, 0, True)
                tile(1, 1, True)
                m = ch2.n
                per = m // 2
                with dve.Fori(1, NT // 2) as i:
                    ch2.at(m + 2 * per * (i - 1))
                    tile(2 * i, 0)
                    tile(2 * i + 1, 1)
                    assert ch2.n == 2 * per
                ch2.at(m + 2 * per * (NT // 2 - 1))
                tile(NT - 1, 0)
            with dve.If(bad < 1):
                layer2(post2)
            with dve.Else():
                ch2.at(0)

                def tile2(t, slot, first=False):
                    general(t, 1)
                    post2(t, slot, first)
                    ch2.link(dve.tensor_scalar(gtile[:, 0:1], gtile[:, 0:1], float(P), None, ALU.add))
                layer2(tile2)

            ch = Chain(dve, s_dve3)
            link = ch.link
            dve.nop().then_inc(s_z, 1)
            dve.wait_ge(s_cntp, 1)
            link(dve.tensor_copy(cntb[:, :], cnp))
            for k in range(2):
                last = dve.tensor_tensor(pad_f[:, k, :], pad_bf[:, k, :], cntb[:, :], ALU.add)
            link(last)
            dve.tensor_copy(pad_i[:, :, :], pad_f[:, :, :]).then_inc(s_pads, 1)
            link(dve.tensor_scalar(cti[:, 0, :], cntb[:, :], float(FT - 1), None, ALU.add))
            link(dve.tensor_scalar(cti[:, 1, :], cti[:, 0, :], FT.bit_length() - 1, None, ALU.logical_shift_right))
            link(dve.tensor_copy(nte[:, :], cti[:, 1, :]))
            link(dve.tensor_copy(cend[:, 0:1], nte[:, 0:1]))
            for e in range(1, NE):
                link(dve.tensor_tensor(cend[:, e:e + 1], cend[:, e - 1:e], nte[:, e:e + 1], ALU.add))
            tile_i, ge, ex, st, loc, rowf, lastf = (ftab[:, k, :] for k in range(7))
            link(dve.memset(ftab[:, 2:4, :], 0.0))
            for e in range(NE - 1):
                link(dve.tensor_scalar(ge, tile_i, cend[0:1, e:e + 1], None, ALU.is_ge))
                dve.tensor_tensor(ex, ex, ge, ALU.add)
                link(dve.scalar_tensor_tensor(out=st, in0=ge, scalar=nte[0:1, e:e + 1], in1=st, op0=ALU.mult,
                                              op1=ALU.add))
            link(dve.tensor_scalar(ge, tile_i, cend[0:1, NE - 1:NE], None, ALU.is_ge))
            link(dve.tensor_tensor(loc, tile_i, st, ALU.subtract))
            link(dve.tensor_scalar(loc, loc, float(FT), None, ALU.mult))
            link(dve.scalar_tensor_tensor(out=rowf, in0=ex, scalar=float(CAPR), in1=loc, op0=ALU.mult, op1=ALU.add))
            dve.tensor_copy(tab[:, 0, :], ex)
            link(dve.tensor_tensor(lastf, ge, loc, ALU.mult))
            link(dve.tensor_tensor(tab[:, 1, :], rowf, lastf, ALU.subtract))
            link(dve.tensor_scalar(lastf, ex, float(1 - EARLY), 0.0, ALU.add, ALU.max))
            link(dve.tensor_scalar(tab[:, 2, :], lastf, 16.0, 16.0, ALU.mult, ALU.add))
            dve.nop().then_inc(s_tab, 1)
            link(dve.tensor_scalar(nte[:, :], nte[:, :], float(FT), -float(CAPR), ALU.mult, ALU.add))
            for e in range(1, NE):
                link(dve.tensor_scalar(past[:, :, :], eall[:, :, :], float(e), nte[:, e - 1:e], ALU.is_ge, ALU.mult))
                link(dve.tensor_tensor(posall[:, :, :], posall[:, :, :], past[:, :, :], ALU.add))
            dve.wait_ge(s_z, 2)
            link(dve.tensor_scalar(zp[:, :], zz[:, :], 1.0, None, ALU.add))
            link(dve.reciprocal(wt[:, 0, :], zp[:, :]))
            link(dve.tensor_tensor(wt[:, 1, :], wt[:, 0, :], zz[:, :], ALU.mult))

            def xt_copy(f, slot):
                dve.wait_ge(s_xt, f + 1)
                dve.tensor_copy(xT[slot][:, 2:4, :], xtp[1]).then_inc(s_xtc, 1)

            def y_out(f, slot, stored):
                dve.wait_ge(s_mm2, HC * f + HC)
                if stored is not None:
                    dve.wait_ge(s_y_out[slot], stored)
                e = dve.value_load(tab[0:1, 0, bass.ds(f, 1)], min_val=0, max_val=NE - 1)
                for h in range(2):
                    last = dve.scalar_tensor_tensor(out=yt[slot][:, h, :], in0=yps[slot][:, h, :], scalar=cc[:, 4:5],
                                                    in1=eb2b[:, bass.ds(e, 1), :].rearrange("p a c -> p (a c)"),
                                                    op0=ALU.mult, op1=ALU.add)
                last.then_inc(s_y, 1)

            def step(f, slot, nxt=True, prev=True, first=False, stored=None):
                for c in range(HC):
                    n = HC * f + c
                    dve.wait_ge(s_gel, n + 1)
                    if not (first and c < 4):
                        dve.wait_ge(s_mm2, n - 3)
                    dve.tensor_scalar(ghl[c % 4][:, 0, :], gel[c % 2], scl[:, S_G:S_G + 1], None, ALU.mult
                                      ).then_inc(s_gh, 1)
                    dve.wait_ge(s_gh, n + 1)
                    dve.scalar_tensor_tensor(out=ghl[c % 4][:, 1, :], in0=gel[c % 2], scalar=scl[:, S_G:S_G + 1],
                                             in1=ghl[c % 4][:, 0, :], op0=ALU.mult, op1=ALU.subtract
                                             ).then_inc(s_g, 1)
                    if nxt and c == XT_AT:
                        xt_copy(f + 1, 1 - slot)
                    if prev and c == YT_AT + 1:
                        y_out(f - 1, 1 - slot, stored)
            dve.wait_ge(s_eb2, 16)
            xt_copy(0, 0)
            step(0, 0, prev=False, first=True)
            step(1, 1)
            step(2, 0)
            step(3, 1, stored=16)
            with dve.Fori(2, (NF - 1) // 2) as i:
                step(2 * i, 0, stored=16 * i - 16)
                step(2 * i + 1, 1, stored=16 * i)
            step(NF - 1, 0, nxt=False, stored=16 * ((NF - 1) // 2) - 16)
            y_out(NF - 1, 0, 16 * ((NF - 1) // 2))

            def final(t, slot, loads, left):
                dve.wait_ge(s_xf[slot], loads)
                dve.wait_ge(s_yg[slot], 2 * loads)
                if left is not None:
                    dve.wait_ge(s_out[slot], left)
                dve.scalar_tensor_tensor(out=xf[slot], in0=yg[slot][0], scalar=wt[:, 0, bass.ds(t, 1)], in1=xf[slot],
                                         op0=ALU.mult, op1=ALU.add).then_inc(s_half, 1)
                dve.wait_ge(s_half, t + 1)
                dve.scalar_tensor_tensor(out=of[slot], in0=yg[slot][1], scalar=wt[:, 1, bass.ds(t, 1)], in1=xf[slot],
                                         op0=ALU.mult, op1=ALU.add).then_inc(s_fin, 1)
            for slot in range(4):
                final(slot, slot, 16, None)
            with dve.Fori(1, NT // 4) as i:
                for slot in range(4):
                    final(4 * i + slot, slot, 16 * i + 16, 16 * i)
            final(NT - 1, 0, 16 * (NT // 4) + 16, 16 * (NT // 4))


_INS = ['x', 'src', 'dst', 'L0_gnn_W1_l', 'L0_gnn_b1', 'L0_gnn_W1_r', 'L0_gnn_W2_l', 'L0_gnn_b2', 'L0_gnn_W2_r',
        'L0_ffn_Wg', 'L0_ffn_bg', 'L0_ffn_W1', 'L0_ffn_b1', 'L0_ffn_W2', 'L0_ffn_b2']


def kernel(**inputs):
    import numpy as np
    import concourse.bacc as bacc
    from concourse.bass_utils import run_bass_kernel_spmd

    nc = bacc.Bacc("TRN2", target_bir_lowering=False, num_devices=1)
    arrays, args = {}, []
    for name in _INS:
        a = np.ascontiguousarray(inputs[name])
        if name == 'x':
            a = np.pad(a, ((0, NPAD - N_NODES), (0, 0)))
        elif name == 'src':
            a = np.pad(a, (0, EPAD + P - N_EDGES))
        elif name == 'dst':
            a = np.pad(a, (0, EPAD + P - N_EDGES), constant_values=DST_PAD)
        arrays["in_" + name] = a
        args.append(nc.dram_tensor("in_" + name, a.shape, mybir.dt.from_np(a.dtype), kind="ExternalInput").ap())
    out = nc.dram_tensor("out_nodes", (NPAD, D), F32, kind="ExternalOutput").ap()
    build(nc, *args, out)
    r = run_bass_kernel_spmd(nc, [arrays], core_ids=[0])
    return r.results[0]["out_nodes"][:N_NODES]
```

```python
from contextlib import ExitStack

import concourse.bass as bass
from concourse import mybir

F32 = mybir.dt.float32
F16 = mybir.dt.float16
I32 = mybir.dt.int32
U32 = mybir.dt.uint32
ALU = mybir.AluOpType
ACT = mybir.ActivationFunctionType
AX_X = mybir.AxisListType.X
RADD = bass.bass_isa.ReduceOp.add

P = 128
N_NODES = 6250
D = 256
KB = D // P
N_EDGES = 206250
NT = -(-N_NODES // P)
NPAD = NT * P
GRP = 2
SUB = 4
BATCH = GRP * SUB
BPT = P // BATCH
GPT = P // GRP
NG = NT * GPT
NQ = 7
GP = NT * BPT // NQ
WIN = P
WINX = WIN + 1
FW = 448
KW = GRP * NT
COARSE = -(-(N_EDGES + WINX) // P)
E_ROWS = COARSE + 8
EPAD = E_ROWS * P
ECH = -(-N_EDGES // P)
DST_PAD = 8191
RING = 4
XSCALE = 1024.0
EPS = 1e-5

NE = 8
H = 1024
HC = H // P
FT = 256
CAPR = NPAD + FT
NF = NPAD * 2 // FT + NE
QT = 7
NX = NT // QT
EARLY = 3
T_AT, D_AT, M_AT, H_AT = 6, 9, 3, 12
T2_AT, D2_AT, X2_AT, G2_AT = 7, 15, 31, 41
SQ_EACH = 4
DEG_AT = 20
XT_AT, YT_AT = 4, 1
WE = 4 * 2048
NW = 4 * NE

S_W1, S_W2, S_WG, S_H, S_E1, S_E2, S_G = range(7)


class Chain:

    def __init__(self, eng, sem):
        self.eng, self.sem, self.start, self.n = eng, sem, 0, 0

    def link(self, ins):
        ins.then_inc(self.sem, 1)
        self.n += 1
        self.eng.wait_ge(self.sem, self.start + self.n)

    def at(self, start):
        self.start, self.n = start, 0


def build(nc, x, edges, W1l, b1, W1r, W2l, b2, W2r, Wg, bg, E1, eb1, E2, eb2, out):
    def dram(name, shape, dt):
        return nc.dram_tensor(name, shape, dt, kind="Internal").ap()

    adj_d = dram("adj_d", (NT, P, NT * P), F16)
    coarse_d = dram("coarse_d", (COARSE,), I32)
    deg_d = dram("deg_d", (NPAD,), F32)
    split_d = dram("split_d", (NE, P, WE), F16)
    table_d = dram("table_d", (NPAD, 2 * D), F16)
    xs_d = dram("xs_d", (NE * CAPR, 2 * D), F16)
    y_d = dram("y_d", (NF * FT, D), F32)
    x1_d = dram("x1_d", (NPAD, D), F32)

    with ExitStack() as ctx:
        def sb(name, shape, dt):
            return ctx.enter_context(nc.sbuf_tensor(name, shape, dt))

        def pb(name, shape, dt=F32):
            return ctx.enter_context(nc.psum_tensor(name, shape, dt))

        def sem(name):
            return ctx.enter_context(nc.semaphore(name))

        arena = sb("arena", [P, NE * WE], F16)

        def part(base, first, size, dt=F16, parts=P):
            n = size if dt == F16 else 2 * size
            v = base[0:parts, first:first + n]
            return v if dt == F16 else v.bitcast(dt)

        xs = part(arena, 0, NT * 512).rearrange("p (t c) -> p t c", c=512)
        hs = part(arena, NT * 512, NT * 512).rearrange("p (t c) -> p t c", c=512)
        A0 = 2 * NT * 512
        adj = [part(arena, A0 + i * NT * P, NT * P) for i in range(2)]
        wts = arena[:, :].rearrange("p (e w) -> p e w", w=WE)
        o = NT * 512
        wd = part(arena, o, NQ * SUB * WINX * 2, I32, GP).rearrange("p (q s w e) -> p q s w e", q=NQ, s=SUB, e=2)
        wfine = part(arena, o, NQ * FW * 2, I32, GP).rearrange("p (q w e) -> p q w e", q=NQ, e=2)
        o += 4 * NQ * SUB * WINX
        assert NQ * FW <= NQ * SUB * WINX
        wraw = [part(arena, o + i * 2048, 1024, F32) for i in range(2)]
        o += 4096
        wsage = part(arena, o, 4 * KB * D, F32).rearrange("p (m k c) -> p m k c", m=4, k=KB)
        assert o + 8 * KB * D <= A0
        o = A0
        xraw = [part(arena, o + i * 2 * QT * D, QT * D, F32).rearrange("p (t c) -> p t c", c=D) for i in range(2)]
        o += 4 * QT * D
        erow = part(arena, o, 2 * (E_ROWS + 1), I32).rearrange("p (n e) -> p n e", e=2)
        assert o + 4 * (E_ROWS + 1) <= NE * WE and EARLY * WE <= NT * 512

        work = sb("work", [P, 2 * 6656], F16)
        w_in = [part(work, i * 2048, 1024, F32) for i in range(2)]
        w_sc = part(work, 4096, 1024, F32)
        w_hl = [part(work, 6144 + i * 2048, 2048) for i in range(2)]
        xl = [part(work, i * 1024, 1024).rearrange("p (h c) -> p h c", h=2) for i in range(2)]
        xT = [part(work, 2048 + i * 1024, 1024).rearrange("p (b n) -> p b n", b=4) for i in range(2)]
        gel = [part(work, 4096 + i * 512, FT, F32) for i in range(2)]
        ghl = [part(work, 5120 + i * 512, 2 * FT).rearrange("p (b n) -> p b n", b=2) for i in range(4)]
        yt = [part(work, 7168 + i * 1024, 2 * D, F32).rearrange("p (h c) -> p h c", h=2) for i in range(2)]
        eb2b = part(work, 9216, NE * D, F32).rearrange("p (e c) -> p e c", e=NE)
        zrow = part(work, 0, 2 * D)
        crow = part(work, 0, COARSE, I32, GP)
        sblk = part(work, 0, NQ * SUB * WIN, I32, GP).rearrange("p (q s w) -> p q s w", q=NQ, s=SUB)
        dl = part(work, 2 * NQ * SUB * WIN, NQ * SUB * WINX, F16, GP).rearrange("p (q s w) -> p q s w", q=NQ, s=SUB)
        junk = part(work, NQ * SUB * (2 * WIN + WINX), E_ROWS)
        iota_i = part(work, NQ * SUB * (2 * WIN + WINX), P, I32)
        assert NQ * SUB * (2 * WIN + WINX) + E_ROWS <= 2 * 6656 and COARSE <= NQ * SUB * WIN
        yg = [[part(arena, (2 * i + k) * 512, D, F32) for k in range(2)] for i in range(4)]
        xf = [part(arena, 4096 + i * 512, D, F32) for i in range(4)]
        of = [part(arena, 6144 + i * 512, D, F32) for i in range(4)]

        onehots = sb("onehots", [P, 2 * NQ * SUB * WIN], F16)
        oh1 = part(onehots, 0, RING * SUB * P).rearrange("p (r s n) -> p r s n", r=RING, s=SUB)
        oh2 = part(onehots, RING * SUB * P, RING * SUB * KW).rearrange("p (r s n) -> p r s n", r=RING, s=SUB)
        key = [part(onehots, k * NQ * SUB * WIN, NQ * SUB * WIN, F16, GP).rearrange("p (q s w) -> p q s w", q=NQ, s=SUB)
               for k in range(2)]
        xres = [part(onehots, i * 512, D, F32) for i in range(2)]
        x1t = [part(onehots, 1024 + i * 512, D, F32) for i in range(2)]
        x2s = part(onehots, 2048, D, F32)
        x2 = [part(onehots, 2560 + i * 512, 512) for i in range(2)]
        x2T = part(onehots, 3584, 512).rearrange("p (b n) -> p b n", b=4)
        grow = part(onehots, 4096, 512)
        goh = part(onehots, 4608, P)

        keys = sb("keys", [P, 2, NG], F16)
        keyt = [sb(f"keyt{i}", [P, 2, GPT, 2], F16) for i in range(2)]
        iota = sb("iota", [P, P], F16)
        ident = sb("ident", [P, P], F16)
        ones = sb("ones", [P, P], F16)
        ltri = sb("ltri", [P, P], F16)
        bnd_i = sb("bnd_i", [GP, NQ, SUB], I32)
        bnd = sb("bnd", [GP, NQ, SUB], F32)
        rowf_ = sb("rowf_", [GP, 3, NQ], F32)
        cnt = sb("cnt", [GP, NQ, SUB], F32)
        row_i = sb("row_i", [GP, NQ], I32)
        lo_i = sb("lo_i", [GP, NQ, SUB], I32)
        vj = sb("vj", [GP, NQ, SUB], F32)
        deg8 = sb("deg8", [GP, NQ, BATCH], F32)
        deg = sb("deg", [P, NT], F32)
        rdeg = sb("rdeg", [P, NT], F32)
        viol = sb("viol", [P, 2], F32)
        violr = sb("violr", [P, 2], F32)
        flag = sb("flag", [P, 1], I32)
        stats = sb("stats", [P, QT, 6], F32)
        mv = sb("mv", [P, NT, 2], F32)
        sd = sb("sd", [P, NT], F32)
        rs = sb("rs", [P, NT], F32)
        nmr = sb("nmr", [P, NT], F32)
        epst = sb("epst", [P, 1], F32)
        wsplit = sb("wsplit", [P, 4, KB, 2, D], F16)
        wgate = sb("wgate", [P, KB, NE], F32)
        wgs = sb("wgs", [P, KB, 2, NE], F16)
        biasb = sb("biasb", [P, 2, D], F32)
        bgb = sb("bgb", [P, NE], F32)
        eb1T = sb("eb1T", [P, NE, HC], F32)
        ss = sb("ss", [P, 7 + NW], F32)
        ssum = sb("ssum", [P, 7], F32)
        ssall = sb("ssall", [P, 7], F32)
        bound = sb("bound", [P, 7], F32)
        p2 = sb("p2", [P, 7], I32)
        ip2 = sb("ip2", [P, 7], I32)
        scl = sb("scl", [P, 7], F32)
        inv = sb("inv", [P, 7], F32)
        cc = sb("cc", [P, 5], F32)
        meanhl = [sb(f"meanhl{i}", [P, 512], F16) for i in range(2)]
        mT = sb("mT", [P, 4, P], F16)
        nT = sb("nT", [P, 4, P], F16)
        tmp = sb("tmp", [P, D], F32)
        st2 = sb("st2", [P, 6], F32)
        mv2 = sb("mv2", [P, 2], F32)
        sd2 = sb("sd2", [P, 1], F32)
        rs2 = sb("rs2", [P, 1], F32)
        lg = sb("lg", [P, NE], F32)
        m8 = sb("m8", [P, 8], F32)
        i8 = sb("i8", [P, 8], U32)
        e01 = sb("e01", [P, 2], F32)
        ecap_i = sb("ecap_i", [P, NE], I32)
        ecap = sb("ecap", [P, NE], F32)
        sel = sb("sel", [P, 2, NE], F32)
        mask = sb("mask", [P, NE], F16)
        msum = sb("msum", [P, NE], F16)
        rk = sb("rk", [P, NE], F32)
        jk = sb("jk", [P, 2, NE], F32)
        posf = sb("posf", [P, 2], F32)
        posi = [[sb(f"posi{i}{k}", [P, 1], I32) for k in range(2)] for i in range(2)]
        posall = sb("posall", [P, NT, 2], F32)
        eall = sb("eall", [P, NT, 2], F16)
        posg = [[sb(f"posg{i}{k}", [P, 1], I32) for k in range(2)] for i in range(4)]
        diff = sb("diff", [P, NT], F32)
        zz = sb("zz", [P, NT], F32)
        zp = sb("zp", [P, NT], F32)
        past = part(onehots, 5120, 2 * NT, F32).rearrange("p (t k) -> p t k", k=2)
        wt = sb("wt", [P, 2, NT], F32)
        cntb = sb("cntb", [P, NE], F32)
        cti = sb("cti", [P, 2, NE], I32)
        nte = sb("nte", [P, NE], F32)
        cend = sb("cend", [P, NE], F32)
        pad_b = sb("pad_b", [P, 2, NE], I32)
        pad_bf = sb("pad_bf", [P, 2, NE], F32)
        pad_f = sb("pad_f", [P, 2, NE], F32)
        pad_i = sb("pad_i", [P, 2, NE], I32)
        fi_i = sb("fi_i", [1, NF], I32)
        ftab = sb("ftab", [1, 7, NF], F32)
        tab = sb("tab", [1, 3, NF], I32)
        gedge = sb("gedge", [P, 2], I32)
        gkey = sb("gkey", [P, 2], F32)
        gtile = sb("gtile", [P, 1], F32)
        zeros = sb("zeros", [P, D], F16)

        bank = [pb(f"bank{i}", [P, 512]) for i in range(8)]
        cps = bank[0:2]
        acc = bank[2:4]
        tpm, tpx, dps, gps = bank[4:8]
        lgp, rkp, cnp, dgp = gps[:, 0:8], gps[:, 8:16], gps[:, 16:24], gps[:, 24:25]
        hps = bank[0:4]
        yps = [b.rearrange("p (h c) -> p h c", h=2) for b in bank[4:6]]
        xtp = [b.rearrange("p (b n) -> p b n", b=2) for b in bank[6:8]]

        s_const = sem("s_const")
        s_coarse_raw = sem("s_coarse_raw")
        s_coarse = sem("s_coarse")
        s_x = [sem(f"s_xin{i}") for i in range(2)]
        s_erow = sem("s_erow")
        s_small = sem("s_small")
        s_wraw = [sem(f"s_wraw{i}") for i in range(2)]
        s_wraw_used = sem("s_wraw_used")
        s_row = sem("s_row")
        s_fine = [sem(f"s_fine{q}") for q in range(NQ)]
        s_lo = sem("s_lo")
        s_win = [sem(f"s_win{q}") for q in range(NQ)]
        s_key = sem("s_key")
        s_keyT = sem("s_keyT")
        s_keyc = sem("s_keyc")
        s_iota = sem("s_iota")
        s_dve = sem("s_dve")
        s_act = sem("s_act")
        s_pool = sem("s_pool")
        s_stats = sem("s_stats")
        s_sd = sem("s_sd")
        s_norm = sem("s_norm")
        s_xn = sem("s_xn")
        s_xs = sem("s_xs")
        s_ss = sem("s_ss")
        s_ssum = sem("s_ssum")
        s_ssall = sem("s_ssall")
        s_bound = sem("s_bound")
        s_scales_e = sem("s_scales_e")
        s_scales = sem("s_scales")
        s_wsplit = sem("s_wsplit")
        s_viol = sem("s_viol")
        s_violr = sem("s_violr")
        s_flag = sem("s_flag")
        s_deg = sem("s_deg")
        s_deg_out = sem("s_deg_out")
        s_deg_in = sem("s_deg_in")
        s_oh = sem("s_oh")
        s_cnt = sem("s_cnt")
        s_evac = sem("s_evac")
        s_acc = [sem(f"s_acc_l{i}") for i in range(2)]
        s_mean = [sem(f"s_mean_l{i}") for i in range(2)]
        s_t = [sem(f"s_t_l{i}") for i in range(2)]
        s_tc = [sem(f"s_tc_l{i}") for i in range(2)]
        s_dense = [sem(f"s_dense_l{i}") for i in range(2)]
        s_h = sem("s_h")
        s_adj_out = [sem(f"s_adj_out{i}") for i in range(2)]
        s_adj_in = [sem(f"s_adj_in{i}") for i in range(2)]
        s_xres = [sem(f"s_xres{i}") for i in range(2)]
        s_x1 = sem("s_x1")
        s_x1_out = [sem(f"s_x1_out{i}") for i in range(2)]
        s_var2 = sem("s_var2")
        s_sd2 = sem("s_sd2")
        s_x2 = sem("s_x2")
        s_x2t = sem("s_x2t")
        s_x2tc = sem("s_x2tc")
        s_logits = sem("s_logits")
        s_mask = sem("s_mask")
        s_rank = sem("s_rank")
        s_pos = sem("s_pos")
        s_scat = [sem(f"s_scat{i}") for i in range(2)]
        s_cntp = sem("s_cntp")
        s_pads = sem("s_pads")
        s_pads_out = sem("s_pads_out")
        s_tab = sem("s_tab")
        s_z = sem("s_z")
        s_win_w = [sem(f"s_win_w{i}") for i in range(2)]
        s_whl_out = [sem(f"s_whl_out{i}") for i in range(2)]
        s_late = sem("s_late")
        s_eb2 = sem("s_eb2")
        s_rows = [sem(f"s_rows{i}") for i in range(2)]
        s_xt = sem("s_xt")
        s_xtc = sem("s_xtc")
        s_hid = sem("s_hid")
        s_gel = sem("s_gel")
        s_g = sem("s_g")
        s_mm2 = sem("s_mm2")
        s_y = sem("s_y")
        s_y_out = [sem(f"s_y_out{i}") for i in range(2)]
        s_ready = sem("s_ready")
        s_idx = sem("s_idx")
        s_yg = [sem(f"s_yg{i}") for i in range(4)]
        s_xf = [sem(f"s_xf{i}") for i in range(4)]
        s_fin = sem("s_fin")
        s_out = [sem(f"s_out{i}") for i in range(4)]
        s_table = sem("s_table")
        s_alone_dve = sem("s_alone_dve")
        s_alone_pool = sem("s_alone_pool")
        s_dve2 = sem("s_dve2")
        s_dve3 = sem("s_dve3")
        s_gh = sem("s_gh")
        s_half = sem("s_half")
        s_gkey = sem("s_gkey")
        s_gedge = sem("s_gedge")
        s_goh = sem("s_goh")
        s_grow = sem("s_grow")
        s_gmm = sem("s_gmm")
        block = ctx.enter_context(nc.Block())

        def even(n):
            return [(n + 1) // 2, n // 2]

        def wchunk(e, w):
            if w < 2:
                return E1[bass.ds(e, 1), w * P:(w + 1) * P, :].rearrange("a p n -> (a p) n")
            return E2[bass.ds(e, 1), (w - 2) * 512:(w - 1) * 512, :].rearrange("a (c p) n -> p (a c) n", p=P)

        def wview(buf, w):
            return buf if w < 2 else buf.rearrange("p (c n) -> p c n", n=D)

        tables = [xs, hs]

        @block.sync
        def _(sp):
            with nc.allow_non_contiguous_dma(reason="every 128th destination"):
                sp.dma_start(coarse_d.rearrange("(n a) -> n a", a=1),
                             edges[0:COARSE * P * 2].rearrange("(n a) -> n a", a=2 * P)[:, 0:1]).then_inc(s_coarse_raw, 16)

            def store_degrees():
                sp.wait_ge(s_deg, 1)
                sp.dma_start(deg_d.rearrange("(q p d) -> p q d", p=GP, d=BATCH), deg8[:, :, :]).then_inc(s_deg_out, 16)
                sp.wait_ge(s_deg_out, 16)
                with nc.allow_non_contiguous_dma(reason="nodes onto partitions"):
                    sp.dma_start(deg[:, :], deg_d.rearrange("(t p) -> p t", p=P)).then_inc(s_deg_in, 16)

            def load_x(q):
                sp.dma_start(xraw[q % 2], x[q * QT * P:(q + 1) * QT * P, :].rearrange("(t p) c -> p t c", p=P)
                             ).then_inc(s_x[q % 2], 16)

            load_x(0)
            load_x(1)
            sp.wait_ge(s_coarse_raw, 16)
            sp.dma_start(crow, coarse_d.rearrange("(a n) -> a n", a=1).to_broadcast([GP, COARSE])
                         ).then_inc(s_coarse, 16)
            for i, n in ((0, E_ROWS), (1, 1)):
                sp.dma_start(erow[:, i * E_ROWS:i * E_ROWS + n, :],
                             edges[i * 2 * E_ROWS:i * 2 * E_ROWS + 2 * EPAD].rearrange("(p n e) -> p n e", p=P, e=2)[:, 0:n, :]
                             ).then_inc(s_erow, 16)
            for m, w in enumerate((W1l, W1r, W2l, W2r)):
                sp.dma_start(wsage[:, m], w.rearrange("(k p) c -> p k c", p=P)).then_inc(s_small, 16)
            for i, b in enumerate((b1, b2)):
                sp.dma_start(biasb[:, i, :], b.rearrange("(a c) -> a c", a=1).to_broadcast([P, D])
                             ).then_inc(s_small, 16)
            sp.dma_start(bgb[:, :], bg.rearrange("(a c) -> a c", a=1).to_broadcast([P, NE])).then_inc(s_small, 16)
            sp.dma_start(wgate[:, :, :], Wg.rearrange("(k p) e -> p k e", p=P)).then_inc(s_small, 16)
            with nc.allow_non_contiguous_dma(reason="hidden units onto partitions"):
                sp.dma_start(eb1T[:, :, :], eb1.rearrange("e (c p) -> p e c", p=P)).then_inc(s_small, 16)
            for q in range(2, NX):
                sp.wait_ge(s_xs, q - 1)
                load_x(q)
            for n in range(NW):
                if n >= 2:
                    sp.wait_ge(s_wraw_used, n - 1)
                sp.dma_start(wview(wraw[n % 2], n % 4), wchunk(n // 4, n % 4)).then_inc(s_wraw[n % 2], 16)
                if n == DEG_AT:
                    store_degrees()
            def general(layer):
                sp.wait_ge(s_h if layer else s_xs, NT if layer else NX)
                with sp.Fori(0, NT) as t:
                    sp.dma_start(table_d[bass.ds(t * P, P), :], tables[layer][:, bass.ds(t, 1), :].rearrange(
                        "p a c -> p (a c)")).then_inc(s_table, 16)
                sp.wait_ge(s_table, 16 * NT * (layer + 1))

                def tile(t, slot, first=False):
                    if layer:
                        load_res(t, slot, first)
                    with sp.Fori(0, ECH) as c:
                        n = (t + layer * NT) * ECH + c
                        sp.wait_ge(s_gmm, n + 1)
                        sp.dma_start(gedge[:, :], edges[bass.ds(c * 2 * P, 2 * P)].rearrange("(p e) -> p e", e=2)
                                     ).then_inc(s_gedge, 16)
                tile(0, 0, True)
                tile(1, 1, True)
                with sp.Fori(1, NT // 2) as i:
                    tile(2 * i, 0)
                    tile(2 * i + 1, 1)
                tile(NT - 1, 0)

            def load_res(t, slot, first):
                if not first:
                    sp.wait_ge(s_x1, t - 1)
                sp.dma_start(xres[slot], x[bass.ds(t * P, P), :]).then_inc(s_xres[slot], 16)

            sp.wait_ge(s_flag, 1)
            bad = sp.value_load(flag[0:1, 0:1], min_val=0, max_val=1)
            with sp.If(bad < 1):
                def store_adj(u, slot):
                    sp.wait_ge(s_evac, BPT * u + BPT)
                    sp.dma_start(adj_d[bass.ds(u, 1), :, :].rearrange("a p n -> (a p) n"), adj[slot]
                                 ).then_inc(s_adj_out[slot], 16)
                with sp.Fori(0, NT // 2) as i:
                    store_adj(2 * i, 0)
                    store_adj(2 * i + 1, 1)
                store_adj(NT - 1, 0)
            with sp.Else():
                general(0)
            sp.wait_ge(s_t[0], NT)
            for i in range(2):
                sp.wait_ge(s_whl_out[i], 16 * NW // 2)
            sp.dma_start(wts[:, 0:EARLY, :], split_d[0:EARLY].rearrange("e p w -> p e w")).then_inc(s_late, 16)
            with sp.If(bad < 1):
                for i in range(2):
                    sp.wait_ge(s_adj_out[i], 16 * even(NT)[i])

                def load_adj(t, slot, first=False):
                    if not first:
                        sp.wait_ge(s_acc[1], t - 1)
                    sp.dma_start(adj[slot], adj_d[bass.ds(t, 1), :, :].rearrange("a p n -> (a p) n")
                                 ).then_inc(s_adj_in[slot], 16)
                    load_res(t, slot, first)
                sp.wait_ge(s_acc[0], NT)
                load_adj(0, 0, True)
                load_adj(1, 1, True)
                with sp.Fori(1, NT // 2) as i:
                    load_adj(2 * i, 0)
                    load_adj(2 * i + 1, 1)
                load_adj(NT - 1, 0)
            with sp.Else():
                general(1)

            sp.wait_ge(s_t[1], NT)
            sp.wait_ge(s_acc[1], NT)
            sp.wait_ge(s_late, 16)
            sp.dma_start(eb2b, eb2.rearrange("e c -> (e c)").rearrange("(a n) -> a n", a=1).to_broadcast(
                [P, NE * D])).then_inc(s_eb2, 16)

            def load_rows(f, slot):
                r = sp.value_load(tab[0:1, 1, bass.ds(f, 1)], min_val=0, max_val=NE * CAPR - FT)
                sp.dma_start(xl[slot], xs_d[bass.ds(r, FT), :].rearrange("(h p) c -> p h c", p=P)
                             ).then_inc(s_rows[slot], 16)
            for e in range(EARLY, NE):
                sp.dma_start(wts[:, e, :], split_d[e]).then_inc(s_late, 16)
                sp.wait_ge(s_late, 16 * (e - EARLY + 2))
                if e == EARLY:
                    sp.wait_ge(s_tab, 1)
                    for i in range(2):
                        sp.wait_ge(s_scat[i], 32 * even(NT)[i])
                    sp.wait_ge(s_pads_out, 16 * 2 * NE)
                    load_rows(0, 0)
                    load_rows(1, 1)

            def step(f, slot, load=True):
                if load:
                    sp.wait_ge(s_xt, f)
                    load_rows(f + 1, 1 - slot)
                sp.wait_ge(s_y, f)
                sp.dma_start(y_d[bass.ds((f - 1) * FT, FT), :].rearrange("(h p) c -> p h c", p=P), yt[1 - slot]
                             ).then_inc(s_y_out[1 - slot], 16)
            step(1, 1)
            with sp.Fori(1, (NF - 1) // 2) as i:
                step(2 * i, 0)
                step(2 * i + 1, 1)
            step(NF - 1, 0, load=False)
            step(NF, 1, load=False)
            for i in range(2):
                sp.wait_ge(s_y_out[i], 16 * even(NF)[i])
                sp.wait_ge(s_x1_out[i], 16 * even(NT)[i])
            sp.wait_ge(s_mm2, NF * HC)
            sp.nop().then_inc(s_ready, 1)

            def load_x1(t, slot):
                sp.wait_ge(s_idx, t + 1)
                sp.dma_start(xf[slot], x1_d[bass.ds(t * P, P), :]).then_inc(s_xf[slot], 16)
            with sp.Fori(0, NT // 4) as i:
                for slot in range(4):
                    load_x1(4 * i + slot, slot)
            load_x1(NT - 1, 0)

        @block.gpsimd
        def _(pool):
            ch = Chain(pool, s_pool)
            pool.iota(iota_i[:, :], pattern=[[1, P]], base=0, channel_multiplier=0)
            pool.iota(bnd_i[:, :, :], pattern=[[BATCH * GP, NQ], [GRP, SUB]], base=0, channel_multiplier=BATCH)
            pool.iota(ecap_i[:, :], pattern=[[CAPR, NE]], base=0, channel_multiplier=0)
            pool.iota(pad_b[:, :, :], pattern=[[P, 2], [CAPR, NE]], base=0, channel_multiplier=1)
            pool.iota(fi_i[:, :], pattern=[[1, NF]], base=0, channel_multiplier=0)
            pool.memset(epst[:, :], EPS / XSCALE ** 2)
            pool.memset(ones[:, :], 1.0).then_inc(s_const, 1)
            ch.link(pool.memset(ident[:, :], 0.0))
            pool.affine_select(out=ident[:, :], in_=ident[:, :], compare_op=ALU.not_equal, fill=1.0, base=0,
                               pattern=[[-1, P]], channel_multiplier=1).then_inc(s_const, 1)
            pool.affine_select(out=ltri[:, :], in_=ones[:, :], compare_op=ALU.is_gt, fill=0.0, base=0,
                               pattern=[[1, P]], channel_multiplier=-1).then_inc(s_const, 1)
            pool.memset(msum[:, :], 0.0).then_inc(s_const, 1)

            def low_x(q):
                pool.wait_ge(s_xn, q + 1)
                t = slice(q * QT, (q + 1) * QT)
                pool.tensor_tensor(xs[:, t, D:2 * D], xraw[q % 2], xs[:, t, 0:D], ALU.subtract).then_inc(s_xs, 1)
            low_x(0)
            low_x(1)
            pool.wait_ge(s_row, 1)
            table = edges.rearrange("(n a) -> n a", a=1)
            for q in range(NQ):
                pool.indirect_dma_start(wfine[:, q, :, :].rearrange("p w e -> p (w e)"), None, table,
                                        bass.IndirectOffsetOnAxis(ap=row_i[:, q:q + 1], axis=0)
                                        ).then_inc(s_fine[q], 16)
            low_x(2)
            pool.wait_ge(s_lo, NQ)
            for q in range(NQ):
                for g in range(SUB):
                    pool.indirect_dma_start(wd[:, q, g, :, :].rearrange("p w e -> p (w e)"), None, table,
                                            bass.IndirectOffsetOnAxis(ap=lo_i[:, q, g:g + 1], axis=0)
                                            ).then_inc(s_win[q], 16)
                if q + 3 < NX:
                    low_x(q + 3)
                if q == 3:
                    pool.wait_ge(s_ssum, 1)
                    pool.partition_all_reduce(ssall[:, 0:4], ssum[:, 0:4], P, RADD).then_inc(s_ssall, 1)
            pool.wait_ge(s_viol, 1)
            pool.partition_all_reduce(violr[:, :], viol[:, :], P, RADD).then_inc(s_violr, 1)
            pool.wait_ge(s_ssum, 2)
            pool.partition_all_reduce(ssall[:, 4:7], ssum[:, 4:7], P, RADD).then_inc(s_ssall, 1)

            def load_w(e, w):
                pool.dma_start(wview(w_in[w % 2], w), wchunk(e, w)).then_inc(s_win_w[w % 2], 16)

            def split_w(e, w, first=False, last=False):
                n = 4 * e + w
                pool.wait_ge(s_win_w[w % 2], 32 * e + 16 * (w // 2) + 16)
                pool.nop().then_inc(s_alone_pool, 1)
                scale = scl[:, S_E1:S_E1 + 1] if w < 2 else scl[:, S_E2:S_E2 + 1]
                ch.link(pool.tensor_scalar(w_sc, w_in[w % 2], scale, None, ALU.mult))
                if not last:
                    load_w(e + w // 2, (w + 2) % 4)
                if not first:
                    pool.wait_ge(s_whl_out[w % 2], 32 * e + 16 * (w // 2))
                pool.nop().then_inc(s_alone_pool, 1)
                ch.link(pool.tensor_copy(w_hl[w % 2][:, 0:1024], w_sc))
                ch.link(pool.tensor_tensor(w_hl[w % 2][:, 1024:2048], w_sc, w_hl[w % 2][:, 0:1024], ALU.subtract))
                pool.dma_start(split_d[bass.ds(e, 1), :, w * 2048:(w + 1) * 2048].rearrange("a p n -> (a p) n"),
                               w_hl[w % 2]).then_inc(s_whl_out[w % 2], 16)

            pool.wait_ge(s_scales_e, 1)
            load_w(0, 0)
            load_w(0, 1)
            for w in range(4):
                split_w(0, w, first=w < 2)
            base = ch.n
            with pool.Fori(1, NE - 1) as e:
                ch.at(base + 12 * (e - 1))
                for w in range(4):
                    split_w(e, w)
            ch.at(base + 12 * (NE - 2))
            for w in range(4):
                split_w(NE - 1, w, last=w >= 2)

            pool.wait_ge(s_flag, 1)
            bad = pool.value_load(flag[0:1, 0:1], min_val=0, max_val=1)

            def gathers(t, layer):
                with pool.Fori(0, ECH) as c:
                    n = (t + layer * NT) * ECH + c
                    pool.wait_ge(s_gedge, 16 * n + 16)
                    pool.nop().then_inc(s_alone_pool, 1)
                    pool.indirect_dma_start(grow, None, table_d, bass.IndirectOffsetOnAxis(ap=gedge[:, 1:2], axis=0)
                                            ).then_inc(s_grow, 16)
                    pool.wait_ge(s_grow, 16 * n + 16)

            def scatter(p, slot):
                pool.wait_ge(s_pos, p + 1)
                pool.nop().then_inc(s_alone_pool, 1)
                for k in range(2):
                    pool.indirect_dma_start(xs_d, bass.IndirectOffsetOnAxis(ap=posi[slot][k][:, 0:1], axis=0),
                                            x2[slot], None).then_inc(s_scat[slot], 16)

            with pool.If(bad < 1):
                with pool.Fori(0, NT // 2) as i:
                    scatter(2 * i, 0)
                    scatter(2 * i + 1, 1)
                scatter(NT - 1, 0)
            with pool.Else():
                pool.wait_ge(s_table, 16 * NT)
                with pool.Fori(0, NT) as t:
                    gathers(t, 0)
                pool.wait_ge(s_table, 32 * NT)
                with pool.Fori(0, NT // 2) as i:
                    for slot in range(2):
                        gathers(2 * i + slot, 1)
                        scatter(2 * i + slot, slot)
                gathers(NT - 1, 1)
                scatter(NT - 1, 0)
            ch.link(pool.memset(zrow, 0.0))
            pool.wait_ge(s_pads, 1)
            for k in range(2):
                for e in range(NE):
                    pool.indirect_dma_start(xs_d, bass.IndirectOffsetOnAxis(ap=pad_i[:, k, e:e + 1], axis=0),
                                            zrow, None).then_inc(s_pads_out, 16)

            pool.wait_ge(s_ready, 1)
            base = ch.start + ch.n

            def gather(t, slot):
                for k in range(2):
                    ch.link(pool.tensor_copy(posg[slot][k][:, 0:1], posall[:, bass.ds(t, 1), k]))
                pool.nop().then_inc(s_idx, 1)
                for k in range(2):
                    pool.indirect_dma_start(yg[slot][k], None, y_d,
                                            bass.IndirectOffsetOnAxis(ap=posg[slot][k][:, 0:1], axis=0)
                                            ).then_inc(s_yg[slot], 16)
            for slot in range(4):
                gather(slot, slot)
            with pool.Fori(1, NT // 4) as i:
                ch.at(base + 8 * i)
                for slot in range(4):
                    pool.wait_ge(s_out[slot], 16 * i)
                    gather(4 * i + slot, slot)
            ch.at(base + 8 * (NT // 4))
            pool.wait_ge(s_out[0], 16 * (NT // 4))
            gather(NT - 1, 0)

        @block.scalar
        def _(act):
            ch = Chain(act, s_act)
            act.wait_ge(s_const, 4)
            act.activation(iota[:, :], iota_i[:, :], ACT.Copy).then_inc(s_iota, 1)
            act.activation(bnd[:, :, :], bnd_i[:, :, :], ACT.Copy).then_inc(s_iota, 1)
            act.activation(ecap[:, :], ecap_i[:, :], ACT.Copy).then_inc(s_iota, 1)
            act.activation(pad_bf[:, :, :], pad_b[:, :, :], ACT.Copy).then_inc(s_iota, 1)
            act.activation(ftab[:, 0, :], fi_i[:, :], ACT.Copy).then_inc(s_iota, 1)

            def norm_x(q):
                t = slice(q * QT, (q + 1) * QT)
                act.wait_ge(s_stats, q + 1)
                act.activation(sd[:, t], mv[:, t, 1], ACT.Sqrt, bias=epst[:, 0:1], scale=XSCALE ** -2
                               ).then_inc(s_sd, 1)
                act.wait_ge(s_norm, q + 1)
                for j in range(QT):
                    u = q * QT + j
                    last = act.activation(xraw[q % 2][:, j, :], xraw[q % 2][:, j, :], ACT.Identity,
                                          bias=nmr[:, u:u + 1], scale=rs[:, u:u + 1])
                ch.link(last)
                act.activation(xs[:, t, 0:D], xraw[q % 2], ACT.Copy).then_inc(s_xn, 1)

            def square(view, col):
                n = view.shape[1] * (view.shape[2] if len(view.shape) == 3 else 1)
                v = bank[7][:, 0:n]
                if len(view.shape) == 3:
                    v = v.rearrange("p (a b) -> p a b", a=view.shape[1])
                ch.link(act.activation(v, view, ACT.Square, accum_out=ss[:, col:col + 1]))

            def square_w(n):
                act.wait_ge(s_wraw[n % 2], 16 * (n // 2) + 16)
                act.activation(wraw[n % 2], wraw[n % 2], ACT.Square, accum_out=ss[:, 7 + n:8 + n]
                               ).then_inc(s_wraw_used, 1)

            norm_x(0)
            norm_x(1)
            act.wait_ge(s_small, 16 * 9)
            for m in range(4):
                square(wsage[:, m], m)
            square(wgate[:, :, :], 4)
            square(biasb[:, 0, :], 5)
            square(eb1T[:, :, :], 6)
            act.nop().then_inc(s_ss, 1)
            for q in range(2, NX):
                norm_x(q)
            for q in range(NQ):
                act.wait_ge(s_keyT, q + 1)
                for k in range(2):
                    act.activation(keys[:, k, q * SUB * GP:(q + 1) * SUB * GP].rearrange("p (g s) -> p s g", s=SUB),
                                   bank[2 * (q % 2) + k][:, 0:SUB * GP].rearrange("p (s g) -> p s g", s=SUB), ACT.Copy
                                   ).then_inc(s_keyc, 1)
                if q == 2:
                    act.wait_ge(s_ssall, 1)
                    act.activation(bound[:, 0:4], ssall[:, 0:4], ACT.Sqrt).then_inc(s_bound, 1)
                if q >= 2:
                    for n in range(SQ_EACH):
                        square_w(SQ_EACH * (q - 2) + n)

            def squares_rest():
                for n in range(SQ_EACH * (NQ - 2), NW):
                    square_w(n)
                act.nop().then_inc(s_ss, 1)

            def expert_bounds():
                act.wait_ge(s_ssall, 2)
                act.activation(bound[:, 4:7], ssall[:, 4:7], ACT.Sqrt).then_inc(s_bound, 1)

            def t_copy(p, layer):
                act.wait_ge(s_t[layer], p + 1)
                act.activation(mT[:, :, :], tpm[:, :].rearrange("p (b n) -> p b n", b=4), ACT.Copy
                               ).then_inc(s_tc[layer], 1)
                act.activation(nT[:, :, :], tpx[:, :].rearrange("p (b n) -> p b n", b=4), ACT.Copy
                               ).then_inc(s_tc[layer], 1)

            def evac(u, slot, j):
                act.wait_ge(s_cnt, BPT * u + j + 1)
                view = adj[slot].rearrange("p (a n) -> p n a", a=NT)[:, BATCH * j:BATCH * (j + 1), :]
                act.activation(view, cps[j % 2][:, 0:SUB * KW].rearrange("p (n a) -> p n a", n=BATCH), ACT.Copy
                               ).then_inc(s_evac, 1)

            def step1(t, slot, build=True, post=True):
                for j in range(BPT):
                    if build:
                        evac(t + 1, 1 - slot, j)
                    if post and j == T_AT:
                        t_copy(t - 1, 0)

            act.wait_ge(s_flag, 1)
            bad = act.value_load(flag[0:1, 0:1], min_val=0, max_val=1)
            with act.If(bad < 1):
                act.wait_ge(s_xs, NX)
                for j in range(BPT):
                    evac(0, 0, j)
                squares_rest()
                step1(0, 0, post=False)
                expert_bounds()
                act.wait_ge(s_acc[0], 1)
                act.wait_ge(s_adj_out[0], 16)
                step1(1, 1)
                with act.Fori(1, (NT - 1) // 2) as i:
                    for k in range(2):
                        act.wait_ge(s_acc[0], 2 * i + k)
                        act.wait_ge(s_adj_out[1 - k], 16 * (i + k))
                        step1(2 * i + k, k)
                step1(NT - 1, 0, build=False)
                t_copy(NT - 1, 0)
            with act.Else():
                squares_rest()
                expert_bounds()
                with act.Fori(0, NT) as t:
                    t_copy(t, 0)

            def post2(p):
                t_copy(p, 1)
                act.wait_ge(s_var2, p + 1)
                act.activation(sd2[:, :], mv2[:, 1:2], ACT.Sqrt, bias=epst[:, 0:1], scale=XSCALE ** -2
                               ).then_inc(s_sd2, 1)
                act.wait_ge(s_x2t, p + 1)
                act.activation(x2T, tpm[:, :].rearrange("p (b n) -> p b n", b=4), ACT.Copy).then_inc(s_x2tc, 1)

            def store_x1(p, slot):
                act.wait_ge(s_x1, p + 1)
                act.dma_start(x1_d[bass.ds(p * P, P), :], x1t[slot]).then_inc(s_x1_out[slot], 16)
            with act.Fori(0, NT // 2) as i:
                for slot in range(2):
                    post2(2 * i + slot)
                    store_x1(2 * i + slot, slot)
            post2(NT - 1)
            store_x1(NT - 1, 0)
            act.wait_ge(s_z, 1)
            act.activation(zz[:, :], diff[:, :], ACT.Exp).then_inc(s_z, 1)

            act.wait_ge(s_tab, 1)

            def xt_copy(f, slot):
                act.wait_ge(s_xt, f + 1)
                act.activation(xT[slot][:, 0:2, :], xtp[0], ACT.Copy).then_inc(s_xtc, 1)

            def step(f, slot, nxt=True, first=False):
                e = act.value_load(tab[0:1, 0, bass.ds(f, 1)], min_val=0, max_val=NE - 1)
                for c in range(HC):
                    act.wait_ge(s_hid, HC * f + c + 1)
                    if not (first and c < 2):
                        act.wait_ge(s_g, HC * f + c - 1)
                    act.activation(gel[c % 2], hps[c % 4][:, 0:FT], ACT.Gelu,
                                   bias=eb1T[:, bass.ds(e, 1), c], scale=cc[:, 3:4]).then_inc(s_gel, 1)
                    if nxt and c == XT_AT:
                        xt_copy(f + 1, 1 - slot)
            xt_copy(0, 0)
            step(0, 0, first=True)
            with act.Fori(0, (NF - 3) // 2) as i:
                step(2 * i + 1, 1)
                step(2 * i + 2, 0)
            step(NF - 2, 1)
            step(NF - 1, 0, nxt=False)

            def leave(t, slot):
                act.wait_ge(s_fin, t + 1)
                act.dma_start(out[bass.ds(t * P, P), :], of[slot]).then_inc(s_out[slot], 16)
            with act.Fori(0, NT // 4) as i:
                for slot in range(4):
                    leave(4 * i + slot, slot)
            leave(NT - 1, 0)
            for slot in range(4):
                act.wait_ge(s_out[slot], 16 * len(range(slot, NT, 4)))

        @block.tensor
        def _(pe):
            pe.wait_ge(s_const, 4)
            for q in range(NQ):
                pe.wait_ge(s_key, q + 1)
                if q >= 2:
                    pe.wait_ge(s_keyc, 2 * (q - 1))
                for k in range(2):
                    for g in range(SUB):
                        last = pe.matmul(bank[2 * (q % 2) + k][:, g * GP:(g + 1) * GP],
                                         key[k][:, q, g, :], ident[0:GP, 0:GP], start=True, stop=True)
                last.then_inc(s_keyT, 1)

            def count(u, j, first=False):
                n = BPT * u + j
                pe.wait_ge(s_oh, n + 1)
                if not first:
                    pe.wait_ge(s_evac, n - 1)
                for g in range(SUB):
                    last = pe.matmul(cps[j % 2][:, g * KW:(g + 1) * KW], oh1[:, j % RING, g, :], oh2[:, j % RING, g, :],
                                     start=True, stop=True)
                last.then_inc(s_cnt, 1)

            def sums(slot, table, a0, a1):
                for a in range(a0, a1):
                    for h in range(2):
                        last = pe.matmul(acc[slot][:, 0:D], adj[slot][:, a * P:(a + 1) * P],
                                         table[:, a, h * D:(h + 1) * D],
                                         start=(a == 0 and h == 0), stop=(a == NT - 1 and h == 1))
                return last

            def turn(p, slot, layer):
                pe.wait_ge(s_mean[layer], p + 1)
                for b in range(4):
                    pe.matmul(tpm[:, b * P:(b + 1) * P], meanhl[slot][:, b * P:(b + 1) * P], ident[:, :],
                              start=True, stop=True)
                for b in range(4):
                    last = pe.matmul(tpx[:, b * P:(b + 1) * P],
                                     tables[layer][:, bass.ds(p, 1), b * P:(b + 1) * P].rearrange("p a c -> p (a c)"),
                                     ident[:, :], start=True, stop=True)
                last.then_inc(s_t[layer], 1)

            def dense(p, layer):
                pe.wait_ge(s_tc[layer], 2 * p + 2)
                n = 0
                for m, rows in enumerate((mT, nT)):
                    for k in range(KB):
                        for ra, wb in ((0, 0), (0, 1), (1, 0)):
                            last = pe.matmul(dps[:, 0:D], rows[:, 2 * ra + k, :], wsplit[:, 2 * layer + m, k, wb, :],
                                             start=(n == 0), stop=(n == 11))
                            n += 1
                last.then_inc(s_dense[layer], 1)

            def step1(t, slot, build=True, post=True, reuse=True):
                pe.wait_ge(s_evac, BPT * t + BPT)
                if reuse:
                    pe.wait_ge(s_mean[0], t - 1)
                for j in range(BPT):
                    if build:
                        count(t + 1, j)
                    last = sums(slot, xs, 3 * j, 3 * j + 3 if j < BPT - 1 else NT)
                    if post and j == T_AT:
                        turn(t - 1, 1 - slot, 0)
                    if post and j == D_AT:
                        if reuse:
                            pe.wait_ge(s_h, t - 1)
                        dense(t - 1, 0)
                last.then_inc(s_acc[0], 1)

            pe.nop().then_inc(s_gmm, 1)
            pe.wait_ge(s_flag, 1)
            pe.wait_ge(s_xs, NX)
            bad = pe.value_load(flag[0:1, 0:1], min_val=0, max_val=1)

            def general(t, slot, layer):
                pe.matmul(acc[slot][:, 0:D], zeros[:, 0:P], zeros[:, 0:D], start=True, stop=False)
                if not layer:
                    pe.matmul(dgp, zeros[:, 0:P], zeros[:, 0:1], start=True, stop=False)
                with pe.Fori(0, ECH) as c:
                    n = (t + layer * NT) * ECH + c
                    pe.wait_ge(s_goh, n + 1)
                    pe.wait_ge(s_grow, 16 * n + 16)
                    if not layer:
                        pe.matmul(dgp, goh, ones[:, 0:1], start=False, stop=False)
                    pe.matmul(acc[slot][:, 0:D], goh, grow[:, 0:D], start=False, stop=False)
                    pe.matmul(acc[slot][:, 0:D], goh, grow[:, D:2 * D], start=False, stop=False).then_inc(s_gmm, 1)
                if not layer:
                    pe.matmul(dgp, zeros[:, 0:P], zeros[:, 0:1], start=False, stop=True)
                pe.matmul(acc[slot][:, 0:D], zeros[:, 0:P], zeros[:, 0:D], start=False, stop=True
                          ).then_inc(s_acc[layer], 1)

            with pe.If(bad < 1):
                for j in range(BPT):
                    count(0, j, first=j < 2)
                step1(0, 0, post=False, reuse=False)
                step1(1, 1, reuse=False)
                with pe.Fori(1, (NT - 1) // 2) as i:
                    step1(2 * i, 0)
                    step1(2 * i + 1, 1)
                step1(NT - 1, 0, build=False)
                turn(NT - 1, 0, 0)
                pe.wait_ge(s_h, NT - 1)
                dense(NT - 1, 0)
            with pe.Else():
                def tile(t, slot, first=False):
                    general(t, slot, 0)
                    turn(t, slot, 0)
                    if not first:
                        pe.wait_ge(s_h, t)
                    dense(t, 0)
                tile(0, 0, True)
                tile(1, 1)
                with pe.Fori(1, NT // 2) as i:
                    tile(2 * i, 0)
                    tile(2 * i + 1, 1)
                tile(NT - 1, 0)

            pe.wait_ge(s_h, NT)

            def turn_x2(p, slot):
                pe.wait_ge(s_x2, p + 1)
                for b in range(4):
                    last = pe.matmul(tpm[:, b * P:(b + 1) * P], x2[slot][:, b * P:(b + 1) * P], ident[:, :],
                                     start=True, stop=True)
                last.then_inc(s_x2t, 1)

            def gate(p, first=False):
                pe.wait_ge(s_x2tc, p + 1)
                if not first:
                    pe.wait_ge(s_pos, p)
                n = 0
                for k in range(KB):
                    for ra, wb in ((0, 0), (0, 1), (1, 0)):
                        last = pe.matmul(lgp, x2T[:, 2 * ra + k, :], wgs[:, k, wb, :], start=(n == 0), stop=(n == 5))
                        n += 1
                last.then_inc(s_logits, 1)

            def rank(p):
                pe.wait_ge(s_mask, p + 1)
                pe.matmul(rkp, ones[:, :], msum[:, :], start=True, stop=False)
                pe.matmul(rkp, ltri[:, :], mask[:, :], start=False, stop=True).then_inc(s_rank, 1)

            def free_dense(p, first):
                if not first:
                    pe.wait_ge(s_x1, p)

            def step2(t, slot, loads, post=True, reuse=True, first=False):
                pe.wait_ge(s_adj_in[slot], loads)
                if reuse:
                    pe.wait_ge(s_mean[1], t - 1)
                a = 0
                if post:
                    for stop, what in ((T2_AT, "turn"), (D2_AT, "dense"), (X2_AT, "x2"), (G2_AT, "gate")):
                        sums(slot, hs, a, stop)
                        a = stop
                        if what == "turn":
                            turn(t - 1, 1 - slot, 1)
                        elif what == "dense":
                            free_dense(t - 1, first)
                            dense(t - 1, 1)
                        elif what == "x2":
                            turn_x2(t - 1, 1 - slot)
                        else:
                            gate(t - 1, first)
                sums(slot, hs, a, NT).then_inc(s_acc[1], 1)
                if post:
                    rank(t - 1)

            def whole_post(p, slot, first=False):
                turn(p, slot, 1)
                free_dense(p, first)
                dense(p, 1)
                turn_x2(p, slot)
                gate(p, first)
                rank(p)

            with pe.If(bad < 1):
                step2(0, 0, 16, post=False, reuse=False)
                step2(1, 1, 16, reuse=False, first=True)
                with pe.Fori(1, (NT - 1) // 2) as i:
                    step2(2 * i, 0, 16 * i + 16)
                    step2(2 * i + 1, 1, 16 * i + 16)
                step2(NT - 1, 0, 16 * ((NT + 1) // 2))
                whole_post(NT - 1, 0)
            with pe.Else():
                def tile(t, slot, first=False):
                    general(t, slot, 1)
                    whole_post(t, slot, first)
                tile(0, 0, True)
                tile(1, 1)
                with pe.Fori(1, NT // 2) as i:
                    tile(2 * i, 0)
                    tile(2 * i + 1, 1)
                tile(NT - 1, 0)
            pe.wait_ge(s_pos, NT)
            pe.matmul(cnp, ones[:, :], msum[:, :], start=True, stop=True).then_inc(s_cntp, 1)

            pe.wait_ge(s_tab, 1)

            def turn_rows(f, slot, loads, first=False):
                pe.wait_ge(s_rows[slot], loads)
                if not first:
                    pe.wait_ge(s_xtc, 2 * f)
                for b in range(4):
                    for h in range(2):
                        last = pe.matmul(xtp[b // 2][:, b % 2, h * P:(h + 1) * P], xl[slot][:, h, b * P:(b + 1) * P],
                                         ident[:, :], start=True, stop=True)
                last.then_inc(s_xt, 1)

            def hidden(f, c, slot, e, first=False):
                if not first:
                    pe.wait_ge(s_gel, HC * f + c - 3)
                n = 0
                for k in range(KB):
                    for wa, rb in ((0, 0), (0, 1), (1, 0)):
                        o = k * 2048 + wa * 1024 + c * P
                        last = pe.matmul(hps[c % 4][:, 0:FT], wts[:, bass.ds(e, 1), o:o + P].rearrange(
                            "p a n -> p (a n)"), xT[slot][:, 2 * rb + k, :], start=(n == 0), stop=(n == 5))
                        n += 1
                last.then_inc(s_hid, 1)

            def output(f, c, slot, e, first=False):
                if c == 0 and not first:
                    pe.wait_ge(s_y, f - 1)
                pe.wait_ge(s_g, HC * f + c + 1)
                for h in range(2):
                    for ga, wb in ((0, 0), (0, 1), (1, 0)):
                        o = (2 + c // 4) * 2048 + wb * 1024 + (c % 4) * D
                        last = pe.matmul(yps[slot][:, h, :], ghl[c % 4][:, ga, h * P:(h + 1) * P],
                                         wts[:, bass.ds(e, 1), o:o + D].rearrange("p a n -> p (a n)"),
                                         start=(c == 0 and h == 0 and (ga, wb) == (0, 0)),
                                         stop=(c == HC - 1 and (ga, wb) == (1, 0)), skip_group_check=True)
                last.then_inc(s_mm2, 1)

            def expert_of(f):
                return pe.value_load(tab[0:1, 0, bass.ds(f, 1)], min_val=0, max_val=NE - 1)

            def step(f, slot, loads=None, nxt=True, prev=True, first=False, second=False):
                e = expert_of(f)
                ep = expert_of(f - 1) if prev else None
                need = pe.value_load(tab[0:1, 2, bass.ds(f, 1)], min_val=16, max_val=16 * NE)
                pe.wait_ge(s_late, need)
                pe.wait_ge(s_xtc, 2 * f + 2)
                for c in range(HC):
                    hidden(f, c, slot, e, first=first and c < 4)
                    if c >= 2:
                        output(f, c - 2, slot, e, first=first or second)
                    elif prev:
                        output(f - 1, HC - 2 + c, 1 - slot, ep)
                    if nxt and c == XT_AT - 1:
                        turn_rows(f + 1, 1 - slot, loads)
            turn_rows(0, 0, 16, first=True)
            step(0, 0, 16, prev=False, first=True)
            step(1, 1, 32, second=True)
            with pe.Fori(1, (NF - 1) // 2) as i:
                step(2 * i, 0, 16 * i + 16)
                step(2 * i + 1, 1, 16 * i + 32)
            step(NF - 1, 0, nxt=False)
            e = expert_of(NF - 1)
            for c in (HC - 2, HC - 1):
                output(NF - 1, c, 0, e)

        @block.vector
        def _(dve):
            ch = Chain(dve, s_dve)

            def norm_x(q):
                dve.wait_ge(s_x[q % 2], 16 * (q // 2 + 1))
                t = slice(q * QT, (q + 1) * QT)
                for j in range(QT):
                    last = dve.bn_stats(stats[:, j, :], xraw[q % 2][:, j, :])
                ch.link(last)
                for j in range(QT):
                    last = dve.bn_aggr(mv[:, q * QT + j, :], stats[:, j, :])
                last.then_inc(s_stats, 1)
                dve.wait_ge(s_sd, q + 1)
                ch.link(dve.reciprocal(rs[:, t], sd[:, t]))
                dve.scalar_tensor_tensor(out=nmr[:, t], in0=mv[:, t, 0], scalar=-1.0, in1=rs[:, t],
                                         op0=ALU.mult, op1=ALU.mult).then_inc(s_norm, 1)

            dve.memset(zeros[:, :], 0.0)
            norm_x(0)
            norm_x(1)
            dve.wait_ge(s_iota, 5)
            dve.wait_ge(s_coarse, 16)
            for q in range(NQ):
                ch.link(dve.tensor_scalar(junk[0:GP, 0:COARSE], crow, bnd[:, q, 0:1], 0.0, ALU.is_lt, ALU.add,
                                          accum_out=rowf_[:, 0, q:q + 1]))
            ch.link(dve.tensor_scalar(rowf_[:, 1, :], rowf_[:, 0, :], -1.0, 0.0, ALU.add, ALU.max))
            dve.tensor_scalar(row_i[:, :], rowf_[:, 1, :], 2.0 * P, None, ALU.mult).then_inc(s_row, 1)
            dve.tensor_scalar(rowf_[:, 2, :], rowf_[:, 1, :], float(P), None, ALU.mult)
            dve.wait_ge(s_erow, 32)
            ch.link(dve.tensor_tensor_reduce(out=junk, in0=erow[:, 0:E_ROWS, 0], in1=erow[:, 1:E_ROWS + 1, 0],
                                             scale=1.0, scalar=0.0, op0=ALU.subtract, op1=ALU.max,
                                             accum_out=viol[:, 0:1]))
            norm_x(2)
            for q in range(NQ):
                dve.wait_ge(s_fine[q], 16)
                for g in range(SUB):
                    ch.link(dve.tensor_scalar(junk[0:GP, 0:FW], wfine[:, q, :, 0], bnd[:, q, g:g + 1], 0.0,
                                              ALU.is_lt, ALU.add, accum_out=cnt[:, q, g:g + 1]))
                dve.tensor_scalar(lo_i[:, q, :], cnt[:, q, :], rowf_[:, 2, q:q + 1], 2.0, ALU.add, ALU.mult
                                  ).then_inc(s_lo, 1)
            dve.wait_ge(s_ss, 1)
            dve.tensor_tensor(ssum[:, S_W1:S_W1 + 1], ss[:, 0:1], ss[:, 1:2], ALU.add)
            dve.tensor_tensor(ssum[:, S_W2:S_W2 + 1], ss[:, 2:3], ss[:, 3:4], ALU.add)
            dve.tensor_copy(ssum[:, S_WG:S_H + 1], ss[:, 4:6]).then_inc(s_ssum, 1)
            norm_x(3)

            def scales(a, b, weights, result, length):
                v = slice(a, b)
                ch.link(dve.tensor_scalar(bound[:, v], bound[:, v], 1.01, 1e-15, ALU.mult, ALU.max))
                ch.link(dve.scalar_tensor_tensor(out=bound[:, result:result + 1], in0=bound[:, weights:weights + 1],
                                                 scalar=length, in1=bound[:, result:result + 1], op0=ALU.mult,
                                                 op1=ALU.add))
                ch.link(dve.tensor_scalar(p2[:, v], bound[:, v].bitcast(I32), 0x7F800000, None, ALU.bitwise_and))
                ch.link(dve.tensor_scalar(ip2[:, v], p2[:, v], -1.0, float(0x7F000000), ALU.mult, ALU.add))
                ch.link(dve.tensor_scalar(scl[:, v], ip2[:, v].bitcast(F32), 8192.0, None, ALU.mult))
                ch.link(dve.tensor_scalar(inv[:, v], p2[:, v].bitcast(F32), 1.0 / 8192.0, None, ALU.mult))

            def factor(i, a, b, k):
                ch.link(dve.scalar_tensor_tensor(out=cc[:, i:i + 1], in0=a, scalar=k, in1=b,
                                                 op0=ALU.mult, op1=ALU.mult))
            for q in range(NQ):
                dve.wait_ge(s_win[q], 16 * SUB)
                ch.link(dve.tensor_tensor(dl[:, q, :, :], wd[:, q, :, :, 0], bnd[:, q, :].rearrange(
                    "p (s a) -> p s a", a=1).to_broadcast([GP, SUB, WINX]), ALU.subtract))
                dve.tensor_scalar(sblk[:, q, :, :], wd[:, q, :, 0:WIN, 1], 7, None, ALU.logical_shift_right)
                ch.link(dve.tensor_scalar(dl[:, q, :, :], dl[:, q, :, :], -8.0, 64.0, ALU.max, ALU.min))
                dve.scalar_tensor_tensor(out=key[0][:, q, :, :], in0=sblk[:, q, :, :], scalar=-float(P),
                                         in1=wd[:, q, :, 0:WIN, 1], op0=ALU.mult, op1=ALU.add)
                dve.scalar_tensor_tensor(out=key[1][:, q, :, :], in0=dl[:, q, :, 0:WIN], scalar=float(NT),
                                         in1=sblk[:, q, :, :], op0=ALU.mult, op1=ALU.add).then_inc(s_key, 1)
                for g in range(SUB):
                    for d in range(GRP):
                        i = g * GRP + d
                        last = dve.tensor_scalar(junk[0:GP, i * WIN:(i + 1) * WIN], dl[:, q, g, 0:WIN], float(d), 0.0,
                                                 ALU.is_equal, ALU.add, accum_out=deg8[:, q, i:i + 1])
                ch.link(last)
                if q + 4 < NX:
                    norm_x(q + 4)
            dve.memset(viol[:, 1:2], 0.0)
            ch.link(dve.tensor_copy(vj[:, :, :], dl[:, :, :, WIN]))
            ch.link(dve.tensor_scalar(cnt[:, :, :], vj[:, :, :], float(GRP), 0.0, ALU.is_lt, ALU.add,
                                      accum_out=viol[0:GP, 1:2]))
            dve.nop().then_inc(s_viol, 1)
            dve.nop().then_inc(s_deg, 1)
            dve.wait_ge(s_bound, 1)
            scales(S_W1, S_H + 1, S_W1, S_H, 23.0)
            factor(0, scl[:, S_H:S_H + 1], inv[:, S_W1:S_W1 + 1], 1.0 / XSCALE)
            factor(1, inv[:, S_H:S_H + 1], inv[:, S_W2:S_W2 + 1], 1.0)
            ch.link(dve.tensor_scalar(cc[:, 2:3], inv[:, S_WG:S_WG + 1], 1.0 / XSCALE, None, ALU.mult))
            ch.link(dve.tensor_scalar(biasb[:, 0, :], biasb[:, 0, :], scl[:, S_H:S_H + 1], None, ALU.mult))
            for m in range(4):
                sc = scl[:, S_W1 + m // 2:S_W1 + m // 2 + 1]
                ch.link(dve.tensor_scalar(wsplit[:, m, :, 0, :], wsage[:, m], sc, None, ALU.mult))
                dve.scalar_tensor_tensor(out=wsplit[:, m, :, 1, :], in0=wsage[:, m], scalar=sc,
                                         in1=wsplit[:, m, :, 0, :], op0=ALU.mult, op1=ALU.subtract)
            sc = scl[:, S_WG:S_WG + 1]
            ch.link(dve.tensor_scalar(wgs[:, :, 0, :], wgate[:, :, :], sc, None, ALU.mult))
            ch.link(dve.scalar_tensor_tensor(out=wgs[:, :, 1, :], in0=wgate[:, :, :], scalar=sc, in1=wgs[:, :, 0, :],
                                             op0=ALU.mult, op1=ALU.subtract))
            dve.nop().then_inc(s_wsplit, 1)
            dve.wait_ge(s_violr, 1)
            ch.link(dve.tensor_tensor(viol[:, 0:1], violr[:, 0:1], violr[:, 1:2], ALU.add))
            dve.tensor_scalar(flag[:, :], viol[:, 0:1], 1.0, None, ALU.min).then_inc(s_flag, 1)
            dve.wait_ge(s_keyc, 2 * NQ)

            def expert_scales():
                dve.wait_ge(s_ss, 2)
                dve.tensor_copy(ssum[:, S_G:S_G + 1], ss[:, 6:7])
                sw = ss[:, 7:7 + NW].rearrange("p (e k w) -> p k e w", k=2, w=2)
                for k in range(2):
                    last = dve.tensor_reduce(ssum[:, S_E1 + k:S_E1 + k + 1], sw[:, k], mybir.AxisListType.XY, ALU.add)
                last.then_inc(s_ssum, 1)
                dve.wait_ge(s_deg_in, 16)
                ch.link(dve.tensor_scalar(deg[:, :], deg[:, :], 1.0, None, ALU.max))
                ch.link(dve.reciprocal(rdeg[:, :], deg[:, :]))
                dve.wait_ge(s_bound, 2)
                scales(S_E1, S_G + 1, S_E1, S_G, 16.1)
                ch.link(dve.tensor_scalar(cc[:, 3:4], inv[:, S_E1:S_E1 + 1], 1.0 / XSCALE, None, ALU.mult))
                factor(4, inv[:, S_G:S_G + 1], inv[:, S_E2:S_E2 + 1], 1.0)
                dve.nop().then_inc(s_scales_e, 1)

            def start_tile(u, slot):
                ch.link(dve.tensor_copy(keyt[slot][:, :, :, :], keys[:, :, bass.ds(u * GPT, GPT)].rearrange(
                    "p k (g a) -> p k g a", a=1).to_broadcast([P, 2, GPT, 2])))

            def onehots_of(u, slot, j, first=False):
                if not first:
                    dve.wait_ge(s_cnt, BPT * u + j - RING + 1)
                for k, (oh, width) in enumerate(((oh1, P), (oh2, KW))):
                    half = [P, SUB, width // 2, 2]
                    last = dve.tensor_tensor(
                        oh[:, j % RING, :, :].rearrange("p s (n a) -> p s n a", a=2),
                        iota[:, 0:width].rearrange("p (s n a) -> p s n a", s=1, a=2).to_broadcast(half),
                        keyt[slot][:, k, j * SUB:(j + 1) * SUB, :].rearrange("p s (n a) -> p s n a", n=1
                                                                             ).to_broadcast(half), ALU.is_equal)
                last.then_inc(s_oh, 1)

            def mean(p, slot, layer):
                dve.wait_ge(s_acc[layer], p + 1)
                r = rdeg[:, bass.ds(p, 1)]
                ch.link(dve.tensor_scalar(meanhl[slot][:, 0:D], acc[slot][:, 0:D], r, None, ALU.mult))
                dve.scalar_tensor_tensor(out=meanhl[slot][:, D:2 * D], in0=acc[slot][:, 0:D], scalar=r,
                                         in1=meanhl[slot][:, 0:D], op0=ALU.mult, op1=ALU.subtract
                                         ).then_inc(s_mean[layer], 1)

            def relu(p):
                dve.wait_ge(s_dense[0], p + 1)
                ch.link(dve.scalar_tensor_tensor(out=tmp[:, :], in0=dps[:, 0:D], scalar=cc[:, 0:1],
                                                 in1=biasb[:, 0, :], op0=ALU.mult, op1=ALU.add))
                hi = hs[:, bass.ds(p, 1), 0:D].rearrange("p a c -> p (a c)")
                lo = hs[:, bass.ds(p, 1), D:2 * D].rearrange("p a c -> p (a c)")
                ch.link(dve.tensor_scalar(hi, tmp[:, :], 0.0, None, ALU.max))
                dve.scalar_tensor_tensor(out=lo, in0=tmp[:, :], scalar=0.0, in1=hi, op0=ALU.max,
                                         op1=ALU.subtract).then_inc(s_h, 1)

            def step1(t, slot, build=True, post=True):
                if build:
                    start_tile(t + 1, 1 - slot)
                for j in range(BPT):
                    if build:
                        onehots_of(t + 1, 1 - slot, j)
                    if post and j == M_AT:
                        mean(t - 1, 1 - slot, 0)
                    if post and j == H_AT:
                        relu(t - 1)

            def general(t, layer):
                gbase = (t + layer * NT) * ECH
                dve.nop().then_inc(s_alone_dve, 1)
                with dve.Fori(0, ECH) as c:
                    n = gbase + c
                    dve.wait_ge(s_gedge, 16 * n + 16)
                    dve.tensor_scalar(gkey[:, 0:1], gedge[:, 0:1], gtile[:, 0:1], None, ALU.subtract).then_inc(s_gkey, 1)
                    dve.wait_ge(s_gkey, n + 1)
                    dve.tensor_scalar(goh, iota[:, 0:P], gkey[:, 0:1], None, ALU.is_equal).then_inc(s_goh, 1)
                dve.wait_ge(s_acc[layer], t + 1)

            def next_tile():
                ch.link(dve.tensor_scalar(gtile[:, 0:1], gtile[:, 0:1], float(P), None, ALU.add))

            def degree(t):
                ch.link(dve.tensor_scalar(gkey[:, 1:2], dgp, 1.0, None, ALU.max))
                ch.link(dve.reciprocal(rdeg[:, bass.ds(t, 1)], gkey[:, 1:2]))

            dve.wait_ge(s_flag, 1)
            bad = dve.value_load(flag[0:1, 0:1], min_val=0, max_val=1)
            base = ch.start + ch.n
            with dve.If(bad < 1):
                start_tile(0, 0)
                for j in range(BPT):
                    onehots_of(0, 0, j, first=j < RING)
                step1(0, 0, post=False)
                expert_scales()
                step1(1, 1)
                m = ch.start + ch.n
                with dve.Fori(1, (NT - 1) // 2) as i:
                    ch.at(m + 8 * (i - 1))
                    step1(2 * i, 0)
                    step1(2 * i + 1, 1)
                    assert ch.n == 8
                ch.at(m + 8 * ((NT - 1) // 2 - 1))
                step1(NT - 1, 0, build=False)
                mean(NT - 1, 0, 0)
                relu(NT - 1)
                fast_n = ch.start + ch.n
            with dve.Else():
                ch.at(base)
                expert_scales()
                ch.link(dve.memset(gtile[:, :], 0.0))

                def tile(t, slot):
                    general(t, 0)
                    degree(t)
                    mean(t, slot, 0)
                    relu(t)
                    next_tile()
                m = ch.start + ch.n
                with dve.Fori(0, NT // 2) as i:
                    ch.at(m + 12 * i)
                    tile(2 * i, 0)
                    tile(2 * i + 1, 1)
                    assert ch.n == 12
                ch.at(m + 12 * (NT // 2))
                tile(NT - 1, 0)
                ch.link(dve.memset(gtile[:, :], 0.0))

            ch2 = Chain(dve, s_dve2)

            def post2(p, slot, first=False):
                link = ch2.link
                dve.wait_ge(s_acc[1], p + 1)
                r = rdeg[:, bass.ds(p, 1)]
                link(dve.tensor_scalar(meanhl[slot][:, 0:D], acc[slot][:, 0:D], r, None, ALU.mult))
                dve.scalar_tensor_tensor(out=meanhl[slot][:, D:2 * D], in0=acc[slot][:, 0:D], scalar=r,
                                         in1=meanhl[slot][:, 0:D], op0=ALU.mult, op1=ALU.subtract
                                         ).then_inc(s_mean[1], 1)
                dve.wait_ge(s_dense[1], p + 1)
                if not first:
                    dve.wait_ge(s_x1_out[slot], 8 * (p - slot))
                link(dve.scalar_tensor_tensor(out=tmp[:, :], in0=dps[:, 0:D], scalar=cc[:, 1:2],
                                              in1=biasb[:, 1, :], op0=ALU.mult, op1=ALU.add))
                dve.wait_ge(s_xres[slot], 8 * (p - slot) + 16)
                dve.tensor_tensor(x1t[slot], tmp[:, :], xres[slot], ALU.add).then_inc(s_x1, 1)
                dve.wait_ge(s_x1, p + 1)
                link(dve.bn_stats(st2[:, :], x1t[slot]))
                dve.nop().then_inc(s_alone_dve, 1)
                dve.bn_aggr(mv2[:, :], st2[:, :]).then_inc(s_var2, 1)
                dve.wait_ge(s_sd2, p + 1)
                link(dve.reciprocal(rs2[:, :], sd2[:, :]))
                link(dve.tensor_scalar(x2s, x1t[slot], mv2[:, 0:1], rs2[:, 0:1], ALU.subtract, ALU.mult))
                if not first:
                    dve.wait_ge(s_scat[slot], 16 * (p - slot))
                link(dve.tensor_copy(x2[slot][:, 0:D], x2s))
                dve.tensor_tensor(x2[slot][:, D:2 * D], x2s, x2[slot][:, 0:D], ALU.subtract).then_inc(s_x2, 1)
                dve.wait_ge(s_logits, p + 1)
                link(dve.scalar_tensor_tensor(out=lg[:, :], in0=lgp, scalar=cc[:, 2:3], in1=bgb[:, :],
                                              op0=ALU.mult, op1=ALU.add))
                dve.nop().then_inc(s_alone_dve, 1)
                link(dve.max(m8[:, :], lg[:, :]))
                dve.nop().then_inc(s_alone_dve, 1)
                link(dve.max_index(i8[:, :], m8[:, :], lg[:, :]))
                dve.tensor_tensor(diff[:, bass.ds(p, 1)], m8[:, 1:2], m8[:, 0:1], ALU.subtract)
                link(dve.tensor_copy(e01[:, :], i8[:, 0:2]))
                for k in range(2):
                    last = dve.tensor_scalar(sel[:, k, :], iota[:, 0:NE], e01[:, k:k + 1], None, ALU.is_equal)
                link(last)
                dve.tensor_tensor(mask[:, :], sel[:, 0, :], sel[:, 1, :], ALU.add).then_inc(s_mask, 1)
                dve.wait_ge(s_rank, p + 1)
                link(dve.tensor_tensor(rk[:, :], rkp, ecap[:, :], ALU.add))
                for k in range(2):
                    last = dve.tensor_tensor_reduce(out=jk[:, k, :], in0=sel[:, k, :], in1=rk[:, :], scale=1.0,
                                                    scalar=0.0, op0=ALU.mult, op1=ALU.add,
                                                    accum_out=posf[:, k:k + 1])
                link(last)
                for k in range(2):
                    dve.tensor_copy(posi[slot][k][:, :], posf[:, k:k + 1])
                dve.tensor_copy(posall[:, bass.ds(p, 1), :], posf[:, :])
                dve.tensor_copy(eall[:, bass.ds(p, 1), :], e01[:, :])
                dve.tensor_tensor(msum[:, :], msum[:, :], mask[:, :], ALU.add).then_inc(s_pos, 1)
                dve.wait_ge(s_pos, p + 1)

            def layer2(tile):
                tile(0, 0, True)
                tile(1, 1, True)
                m = ch2.n
                per = m // 2
                with dve.Fori(1, NT // 2) as i:
                    ch2.at(m + 2 * per * (i - 1))
                    tile(2 * i, 0)
                    tile(2 * i + 1, 1)
                    assert ch2.n == 2 * per
                ch2.at(m + 2 * per * (NT // 2 - 1))
                tile(NT - 1, 0)
            with dve.If(bad < 1):
                layer2(post2)
            with dve.Else():
                ch2.at(0)

                def tile2(t, slot, first=False):
                    general(t, 1)
                    post2(t, slot, first)
                    ch2.link(dve.tensor_scalar(gtile[:, 0:1], gtile[:, 0:1], float(P), None, ALU.add))
                layer2(tile2)

            ch = Chain(dve, s_dve3)
            link = ch.link
            dve.nop().then_inc(s_z, 1)
            dve.wait_ge(s_cntp, 1)
            link(dve.tensor_copy(cntb[:, :], cnp))
            for k in range(2):
                last = dve.tensor_tensor(pad_f[:, k, :], pad_bf[:, k, :], cntb[:, :], ALU.add)
            link(last)
            dve.tensor_copy(pad_i[:, :, :], pad_f[:, :, :]).then_inc(s_pads, 1)
            link(dve.tensor_scalar(cti[:, 0, :], cntb[:, :], float(FT - 1), None, ALU.add))
            link(dve.tensor_scalar(cti[:, 1, :], cti[:, 0, :], FT.bit_length() - 1, None, ALU.logical_shift_right))
            link(dve.tensor_copy(nte[:, :], cti[:, 1, :]))
            link(dve.tensor_copy(cend[:, 0:1], nte[:, 0:1]))
            for e in range(1, NE):
                link(dve.tensor_tensor(cend[:, e:e + 1], cend[:, e - 1:e], nte[:, e:e + 1], ALU.add))
            tile_i, ge, ex, st, loc, rowf, lastf = (ftab[:, k, :] for k in range(7))
            link(dve.memset(ftab[:, 2:4, :], 0.0))
            for e in range(NE - 1):
                link(dve.tensor_scalar(ge, tile_i, cend[0:1, e:e + 1], None, ALU.is_ge))
                dve.tensor_tensor(ex, ex, ge, ALU.add)
                link(dve.scalar_tensor_tensor(out=st, in0=ge, scalar=nte[0:1, e:e + 1], in1=st, op0=ALU.mult,
                                              op1=ALU.add))
            link(dve.tensor_scalar(ge, tile_i, cend[0:1, NE - 1:NE], None, ALU.is_ge))
            link(dve.tensor_tensor(loc, tile_i, st, ALU.subtract))
            link(dve.tensor_scalar(loc, loc, float(FT), None, ALU.mult))
            link(dve.scalar_tensor_tensor(out=rowf, in0=ex, scalar=float(CAPR), in1=loc, op0=ALU.mult, op1=ALU.add))
            dve.tensor_copy(tab[:, 0, :], ex)
            link(dve.tensor_tensor(lastf, ge, loc, ALU.mult))
            link(dve.tensor_tensor(tab[:, 1, :], rowf, lastf, ALU.subtract))
            link(dve.tensor_scalar(lastf, ex, float(1 - EARLY), 0.0, ALU.add, ALU.max))
            link(dve.tensor_scalar(tab[:, 2, :], lastf, 16.0, 16.0, ALU.mult, ALU.add))
            dve.nop().then_inc(s_tab, 1)
            link(dve.tensor_scalar(nte[:, :], nte[:, :], float(FT), -float(CAPR), ALU.mult, ALU.add))
            for e in range(1, NE):
                link(dve.tensor_scalar(past[:, :, :], eall[:, :, :], float(e), nte[:, e - 1:e], ALU.is_ge, ALU.mult))
                link(dve.tensor_tensor(posall[:, :, :], posall[:, :, :], past[:, :, :], ALU.add))
            dve.wait_ge(s_z, 2)
            link(dve.tensor_scalar(zp[:, :], zz[:, :], 1.0, None, ALU.add))
            link(dve.reciprocal(wt[:, 0, :], zp[:, :]))
            link(dve.tensor_tensor(wt[:, 1, :], wt[:, 0, :], zz[:, :], ALU.mult))

            def xt_copy(f, slot):
                dve.wait_ge(s_xt, f + 1)
                dve.tensor_copy(xT[slot][:, 2:4, :], xtp[1]).then_inc(s_xtc, 1)

            def y_out(f, slot, stored):
                dve.wait_ge(s_mm2, HC * f + HC)
                if stored is not None:
                    dve.wait_ge(s_y_out[slot], stored)
                e = dve.value_load(tab[0:1, 0, bass.ds(f, 1)], min_val=0, max_val=NE - 1)
                for h in range(2):
                    last = dve.scalar_tensor_tensor(out=yt[slot][:, h, :], in0=yps[slot][:, h, :], scalar=cc[:, 4:5],
                                                    in1=eb2b[:, bass.ds(e, 1), :].rearrange("p a c -> p (a c)"),
                                                    op0=ALU.mult, op1=ALU.add)
                last.then_inc(s_y, 1)

            def step(f, slot, nxt=True, prev=True, first=False, stored=None):
                for c in range(HC):
                    n = HC * f + c
                    dve.wait_ge(s_gel, n + 1)
                    if not (first and c < 4):
                        dve.wait_ge(s_mm2, n - 3)
                    dve.tensor_scalar(ghl[c % 4][:, 0, :], gel[c % 2], scl[:, S_G:S_G + 1], None, ALU.mult
                                      ).then_inc(s_gh, 1)
                    dve.wait_ge(s_gh, n + 1)
                    dve.scalar_tensor_tensor(out=ghl[c % 4][:, 1, :], in0=gel[c % 2], scalar=scl[:, S_G:S_G + 1],
                                             in1=ghl[c % 4][:, 0, :], op0=ALU.mult, op1=ALU.subtract
                                             ).then_inc(s_g, 1)
                    if nxt and c == XT_AT:
                        xt_copy(f + 1, 1 - slot)
                    if prev and c == YT_AT + 1:
                        y_out(f - 1, 1 - slot, stored)
            dve.wait_ge(s_eb2, 16)
            xt_copy(0, 0)
            step(0, 0, prev=False, first=True)
            step(1, 1)
            step(2, 0)
            step(3, 1, stored=16)
            with dve.Fori(2, (NF - 1) // 2) as i:
                step(2 * i, 0, stored=16 * i - 16)
                step(2 * i + 1, 1, stored=16 * i)
            step(NF - 1, 0, nxt=False, stored=16 * ((NF - 1) // 2) - 16)
            y_out(NF - 1, 0, 16 * ((NF - 1) // 2))

            def final(t, slot, loads, left):
                dve.wait_ge(s_xf[slot], loads)
                dve.wait_ge(s_yg[slot], 2 * loads)
                if left is not None:
                    dve.wait_ge(s_out[slot], left)
                dve.scalar_tensor_tensor(out=xf[slot], in0=yg[slot][0], scalar=wt[:, 0, bass.ds(t, 1)], in1=xf[slot],
                                         op0=ALU.mult, op1=ALU.add).then_inc(s_half, 1)
                dve.wait_ge(s_half, t + 1)
                dve.scalar_tensor_tensor(out=of[slot], in0=yg[slot][1], scalar=wt[:, 1, bass.ds(t, 1)], in1=xf[slot],
                                         op0=ALU.mult, op1=ALU.add).then_inc(s_fin, 1)
            for slot in range(4):
                final(slot, slot, 16, None)
            with dve.Fori(1, NT // 4) as i:
                for slot in range(4):
                    final(4 * i + slot, slot, 16 * i + 16, 16 * i)
            final(NT - 1, 0, 16 * (NT // 4) + 16, 16 * (NT // 4))


_INS = ['x', 'edges', 'L0_gnn_W1_l', 'L0_gnn_b1', 'L0_gnn_W1_r', 'L0_gnn_W2_l', 'L0_gnn_b2', 'L0_gnn_W2_r',
        'L0_ffn_Wg', 'L0_ffn_bg', 'L0_ffn_W1', 'L0_ffn_b1', 'L0_ffn_W2', 'L0_ffn_b2']


def kernel(**inputs):
    import numpy as np
    import concourse.bacc as bacc
    from concourse.bass_utils import run_bass_kernel_spmd

    nc = bacc.Bacc("TRN2", target_bir_lowering=False, num_devices=1)
    arrays, args = {}, []
    pad = EPAD + E_ROWS - N_EDGES
    inputs["edges"] = np.stack([np.pad(inputs["dst"], (0, pad), constant_values=DST_PAD),
                                np.pad(inputs["src"], (0, pad))], axis=1).reshape(-1)
    for name in _INS:
        a = np.ascontiguousarray(inputs[name])
        if name == 'x':
            a = np.pad(a, ((0, NPAD - N_NODES), (0, 0)))
        arrays["in_" + name] = a
        args.append(nc.dram_tensor("in_" + name, a.shape, mybir.dt.from_np(a.dtype), kind="ExternalInput").ap())
    out = nc.dram_tensor("out_nodes", (NPAD, D), F32, kind="ExternalOutput").ap()
    build(nc, *args, out)
    r = run_bass_kernel_spmd(nc, [arrays], core_ids=[0])
    return r.results[0]["out_nodes"][:N_NODES]
```

```python
from contextlib import ExitStack

import concourse.bass as bass
from concourse import mybir

F32 = mybir.dt.float32
F16 = mybir.dt.float16
I32 = mybir.dt.int32
I16 = mybir.dt.int16
U32 = mybir.dt.uint32
ALU = mybir.AluOpType
ACT = mybir.ActivationFunctionType
AX_X = mybir.AxisListType.X
RADD = bass.bass_isa.ReduceOp.add

P = 128
N_NODES = 6250
D = 256
KB = D // P
N_EDGES = 206250
NT = -(-N_NODES // P)
NPAD = NT * P
GRP = 2
SUB = 4
BATCH = GRP * SUB
BPT = P // BATCH
GPT = P // GRP
NG = NT * GPT
NQ = 7
GP = NT * BPT // NQ
WIN = P
WINX = WIN + 1
FW = 448
KW = GRP * NT
COARSE = -(-(N_EDGES + WINX) // P)
E_ROWS = COARSE + 8
EPAD = E_ROWS * P
ECH = -(-N_EDGES // P)
DST_PAD = 8191
RING = 4
XSCALE = 1024.0
EPS = 1e-5

NE = 8
H = 1024
HC = H // P
FT = 256
CAPR = NPAD + FT
NF = NPAD * 2 // FT + NE
QT = 7
NX = NT // QT
EARLY = 3
T_AT, D_AT, M_AT, H_AT = 6, 9, 3, 12
R2_AT, T2_AT, D2_AT, X2_AT, G2_AT = 3, 8, 16, 35, 44
LOW_AT = (0, 3, 4, 6)
NORM_AT = (0, 3, 4)
LAG = 3
XT_AT, Y_AT, YW_AT = 4, 3, 5
WE = 4 * 2048
NW = 4 * NE

S_W1, S_W2, S_WG, S_H, S_E1, S_E2, S_G = range(7)


class Chain:

    def __init__(self, eng, sem):
        self.eng, self.sem, self.start, self.n = eng, sem, 0, 0

    def link(self, ins):
        ins.then_inc(self.sem, 1)
        self.n += 1
        self.eng.wait_ge(self.sem, self.start + self.n)

    def at(self, start):
        self.start, self.n = start, 0


def build(nc, x, edges, W1l, b1, W1r, W2l, b2, W2r, Wg, bg, E1, eb1, E2, eb2, out):
    def dram(name, shape, dt):
        return nc.dram_tensor(name, shape, dt, kind="Internal").ap()

    adj_d = dram("adj_d", (NT, P, NT * P), F16)
    coarse_d = dram("coarse_d", (COARSE,), I32)
    deg_d = dram("deg_d", (NPAD,), F32)
    split_d = dram("split_d", (NE, P, WE), F16)
    table_d = dram("table_d", (NPAD, 2 * D), F16)
    xs_d = dram("xs_d", (NE * CAPR + FT, 2 * D), F16)
    meta_d = dram("meta_d", (NE * CAPR + FT, 2), I32)

    with ExitStack() as ctx:
        def sb(name, shape, dt):
            return ctx.enter_context(nc.sbuf_tensor(name, shape, dt))

        def pb(name, shape, dt=F32):
            return ctx.enter_context(nc.psum_tensor(name, shape, dt))

        def sem(name):
            return ctx.enter_context(nc.semaphore(name))

        arena = sb("arena", [P, NE * WE], F16)

        def part(base, first, size, dt=F16, parts=P):
            n = size if dt in (F16, I16) else 2 * size
            v = base[0:parts, first:first + n]
            return v if dt == F16 else v.bitcast(dt)

        xs = part(arena, 0, NT * 512).rearrange("p (t c) -> p t c", c=512)
        wfine = part(arena, NT * 512 - 4 * NQ * FW, NQ * FW * 2, I32, GP).rearrange("p (q w e) -> p q w e", q=NQ, e=2)
        assert NT * 512 - 4 * NQ * FW >= 3 * QT * 512
        hs = part(arena, NT * 512, NT * 512).rearrange("p (t c) -> p t c", c=512)
        A0 = 2 * NT * 512
        adj = [part(arena, A0 + i * NT * P, NT * P) for i in range(2)]
        wts = arena[:, :].rearrange("p (e w) -> p e w", w=WE)
        o = NT * 512
        wd = part(arena, o, NQ * SUB * WINX * 2, I32, GP).rearrange("p (q s w e) -> p q s w e", q=NQ, s=SUB, e=2)
        o += 4 * NQ * SUB * WINX
        wraw = [part(arena, o + i * 2048, 1024, F32) for i in range(2)]
        o += 4096
        wsage = part(arena, o, 4 * KB * D, F32).rearrange("p (m k c) -> p m k c", m=4, k=KB)
        assert o + 8 * KB * D <= A0
        o = A0
        xraw = [part(arena, o + i * 2 * QT * D, QT * D, F32).rearrange("p (t c) -> p t c", c=D) for i in range(2)]
        o += 4 * QT * D
        erow = part(arena, o, 2 * (E_ROWS + 1), I32).rearrange("p (n e) -> p n e", e=2)
        assert o + 4 * (E_ROWS + 1) <= NE * WE and EARLY * WE <= NT * 512

        work = sb("work", [P, 2 * 6656], F16)
        w_in = [part(work, i * 2048, 1024, F32) for i in range(2)]
        w_sc = part(work, 4096, 1024, F32)
        w_hl = [part(work, 6144 + i * 2048, 2048) for i in range(2)]
        xl = [part(work, i * 1024, 1024).rearrange("p (h c) -> p h c", h=2) for i in range(2)]
        xT = [part(work, 2048 + i * 1024, 1024).rearrange("p (b n) -> p b n", b=4) for i in range(2)]
        gel = [part(work, 4096 + i * 512, FT, F32) for i in range(2)]
        ghl = [part(work, 5120 + i * 512, 2 * FT).rearrange("p (b n) -> p b n", b=2) for i in range(4)]
        yt = [part(work, 7168 + i * 1024, 2 * D, F32).rearrange("p (h c) -> p h c", h=2) for i in range(2)]
        eb2b = part(work, 9216, NE * D, F32).rearrange("p (e c) -> p e c", e=NE)
        etab = [part(work, 2048 + i * 2 * NE * NF, NE * NF, F32, 1).rearrange("p (e f) -> p e f", e=NE)
                for i in range(2)]
        zrow = part(work, 6144, 4 * D).rearrange("p (h c) -> p h c", h=2)
        crow = part(work, 0, COARSE, I32, GP)
        crow16 = part(work, 2 * COARSE, COARSE, I16, GP)
        fine16 = [part(work, (3 + i) * COARSE, FW, I16, GP) for i in range(2)]
        sblk = part(work, 0, NQ * SUB * WIN, I32, GP).rearrange("p (q s w) -> p q s w", q=NQ, s=SUB)
        dl = part(work, 2 * NQ * SUB * WIN, NQ * SUB * WINX, F16, GP).rearrange("p (q s w) -> p q s w", q=NQ, s=SUB)
        junk = part(work, NQ * SUB * (2 * WIN + WINX), SUB * FW)
        iota_i = part(work, NQ * SUB * (2 * WIN + WINX), P, I32)
        assert NQ * SUB * (2 * WIN + WINX) + SUB * FW <= 2 * 6656 and E_ROWS <= SUB * FW
        assert 5 * COARSE <= NQ * SUB * (2 * WIN + WINX) and FW <= COARSE
        onehots = sb("onehots", [P, 2 * NQ * SUB * WIN], F16)
        oh1 = part(onehots, 0, RING * SUB * P).rearrange("p (r s n) -> p r s n", r=RING, s=SUB)
        oh2 = part(onehots, RING * SUB * P, RING * SUB * KW).rearrange("p (r s n) -> p r s n", r=RING, s=SUB)
        key = [part(onehots, k * NQ * SUB * WIN, NQ * SUB * WIN, F16, GP).rearrange("p (q s w) -> p q s w", q=NQ, s=SUB)
               for k in range(2)]
        xres = [part(onehots, i * 512, D, F32) for i in range(2)]
        x1t = [part(onehots, 1024 + i * 512, D, F32) for i in range(2)]
        x2s = part(onehots, 2048, D, F32)
        x2 = [part(onehots, 2560 + i * 512, 512) for i in range(2)]
        x2T = part(onehots, 3584, 512).rearrange("p (b n) -> p b n", b=4)
        grow = part(onehots, 4096, 512)
        goh = part(onehots, 4608, P)

        keys = sb("keys", [P, 2, NG], F16)
        keyt = [sb(f"keyt{i}", [P, 2, GPT, 2], F16) for i in range(2)]
        iota = sb("iota", [P, P], F16)
        ident = sb("ident", [P, P], F16)
        ones = sb("ones", [P, P], F16)
        ltri = sb("ltri", [P, P], F16)
        bnd_i = sb("bnd_i", [GP, NQ, SUB], I32)
        bnd = sb("bnd", [GP, NQ, SUB], F32)
        rowf_ = sb("rowf_", [GP, 3, NQ], F32)
        cnt = sb("cnt", [GP, NQ, SUB], F32)
        row_i = sb("row_i", [GP, NQ], I32)
        lo_i = sb("lo_i", [GP, NQ, SUB], I32)
        vj = sb("vj", [GP, NQ, SUB], F32)
        deg8 = sb("deg8", [GP, NQ, BATCH], F32)
        deg = sb("deg", [P, NT], F32)
        rdeg = sb("rdeg", [P, NT], F32)
        viol = sb("viol", [P, 2], F32)
        violr = sb("violr", [P, 2], F32)
        flag = sb("flag", [P, 1], I32)
        stats = sb("stats", [P, QT, 6], F32)
        mv = sb("mv", [P, NT, 2], F32)
        sd = sb("sd", [P, NT], F32)
        rs = sb("rs", [P, NT], F32)
        nmr = sb("nmr", [P, NT], F32)
        epst = sb("epst", [P, 1], F32)
        wsplit = sb("wsplit", [P, 4, KB, 2, D], F16)
        wgate = sb("wgate", [P, KB, NE], F32)
        wgs = sb("wgs", [P, KB, 2, NE], F16)
        biasb = sb("biasb", [P, 2, D], F32)
        bgb = sb("bgb", [P, NE], F32)
        eb1T = sb("eb1T", [P, NE, HC], F32)
        ss = sb("ss", [P, 7 + NW], F32)
        ssum = sb("ssum", [P, 7], F32)
        ssall = sb("ssall", [P, 7], F32)
        bound = sb("bound", [P, 7], F32)
        p2 = sb("p2", [P, 7], I32)
        ip2 = sb("ip2", [P, 7], I32)
        scl = sb("scl", [P, 7], F32)
        inv = sb("inv", [P, 7], F32)
        cc = sb("cc", [P, 5], F32)
        meanhl = [sb(f"meanhl{i}", [P, 512], F16) for i in range(2)]
        mT = sb("mT", [P, 4, P], F16)
        nT = sb("nT", [P, 4, P], F16)
        tmp = sb("tmp", [P, D], F32)
        st2 = sb("st2", [P, 6], F32)
        mv2 = sb("mv2", [P, 2], F32)
        sd2 = sb("sd2", [P, 1], F32)
        rs2 = sb("rs2", [P, 1], F32)
        lg = sb("lg", [P, NE], F32)
        m8 = sb("m8", [P, 8], F32)
        i8 = sb("i8", [P, 8], U32)
        e01 = sb("e01", [P, 2], F32)
        ecap_i = sb("ecap_i", [P, NE], I32)
        ecap = sb("ecap", [P, NE], F32)
        sel = sb("sel", [P, 2, NE], F32)
        mask = sb("mask", [P, NE], F16)
        msum = sb("msum", [P, NE], F16)
        rk = sb("rk", [P, NE], F32)
        jk = sb("jk", [P, 2, NE], F32)
        posf = sb("posf", [P, 2], F32)
        posi = [[sb(f"posi{i}{k}", [P, 1], I32) for k in range(2)] for i in range(2)]
        diff = [sb(f"diff{i}", [P, 1], F32) for i in range(2)]
        zz = [sb(f"zz{i}", [P, 1], F32) for i in range(2)]
        zp = sb("zp", [P, 1], F32)
        w0 = sb("w0", [P, 1], F32)
        sq_back = sb("sq_back", [P, 1], F32)
        ids_i = sb("ids_i", [P, NT], I32)
        meta = [sb(f"meta{i}", [P, 2, 2], I32) for i in range(2)]
        metap = sb("metap", [P, 2, 2], I32)
        ml = [sb(f"ml{i}", [P, 2, 2], I32) for i in range(2)]
        cntb = sb("cntb", [P, NE], F32)
        cti = sb("cti", [P, 2, NE], I32)
        nte = sb("nte", [P, NE], F32)
        cend = sb("cend", [P, NE], F32)
        padf = sb("padf", [P, NE], F32)
        padi = sb("padi", [1, NE], I32)
        fi_i = sb("fi_i", [1, NF], I32)
        ftab = sb("ftab", [1, 7, NF], F32)
        tab = sb("tab", [1, 2, NF], I32)
        gedge = sb("gedge", [P, 2], I32)
        gkey = sb("gkey", [P, 2], F32)
        gtile = sb("gtile", [P, 1], F32)
        zeros = sb("zeros", [P, D], F16)

        bank = [pb(f"bank{i}", [P, 512]) for i in range(8)]
        cps = bank[0:2]
        acc = bank[2:4]
        tpm, tpx, dps, gps = bank[4:8]
        lgp, rkp, cnp, dgp = gps[:, 0:8], gps[:, 8:16], gps[:, 16:24], gps[:, 24:25]
        hps = bank[0:4]
        yps = [b.rearrange("p (h c) -> p h c", h=2) for b in bank[4:6]]
        xtp = [b.rearrange("p (b n) -> p b n", b=2) for b in bank[6:8]]

        s_const = sem("s_const")
        s_coarse_raw = sem("s_coarse_raw")
        s_coarse = sem("s_coarse")
        s_x = [sem(f"s_xin{i}") for i in range(2)]
        s_erow = sem("s_erow")
        s_small = sem("s_small")
        s_wraw = [sem(f"s_wraw{i}") for i in range(2)]
        s_wraw_used = sem("s_wraw_used")
        s_row = sem("s_row")
        s_fine = [sem(f"s_fine{q}") for q in range(NQ)]
        s_lo = sem("s_lo")
        s_win = [sem(f"s_win{q}") for q in range(NQ)]
        s_key = sem("s_key")
        s_keyT = sem("s_keyT")
        s_keyc = sem("s_keyc")
        s_iota = sem("s_iota")
        s_dve = sem("s_dve")
        s_act = sem("s_act")
        s_pool = sem("s_pool")
        s_stats = sem("s_stats")
        s_sd = sem("s_sd")
        s_norm = sem("s_norm")
        s_xn = sem("s_xn")
        s_xs = sem("s_xs")
        s_ss = sem("s_ss")
        s_ssum = sem("s_ssum")
        s_ssall = sem("s_ssall")
        s_bound = sem("s_bound")
        s_scales_e = sem("s_scales_e")
        s_wsplit = sem("s_wsplit")
        s_viol = sem("s_viol")
        s_violr = sem("s_violr")
        s_flag = sem("s_flag")
        s_deg = sem("s_deg")
        s_deg_out = sem("s_deg_out")
        s_deg_in = sem("s_deg_in")
        s_oh = sem("s_oh")
        s_cnt = sem("s_cnt")
        s_evac = sem("s_evac")
        s_acc = [sem(f"s_acc_l{i}") for i in range(2)]
        s_mean = [sem(f"s_mean_l{i}") for i in range(2)]
        s_t = [sem(f"s_t_l{i}") for i in range(2)]
        s_tc = [sem(f"s_tc_l{i}") for i in range(2)]
        s_dense = [sem(f"s_dense_l{i}") for i in range(2)]
        s_h = sem("s_h")
        s_adj_out = [sem(f"s_adj_out{i}") for i in range(2)]
        s_adj_in = [sem(f"s_adj_in{i}") for i in range(2)]
        s_xres = [sem(f"s_xres{i}") for i in range(2)]
        s_x1 = sem("s_x1")
        s_x1_out = [sem(f"s_x1_out{i}") for i in range(2)]
        s_var2 = sem("s_var2")
        s_sd2 = sem("s_sd2")
        s_x2 = sem("s_x2")
        s_x2t = sem("s_x2t")
        s_x2tc = sem("s_x2tc")
        s_logits = sem("s_logits")
        s_mask = sem("s_mask")
        s_rank = sem("s_rank")
        s_pos = sem("s_pos")
        s_scat = [sem(f"s_scat{i}") for i in range(2)]
        s_cntp = sem("s_cntp")
        s_pads = sem("s_pads")
        s_pads_out = sem("s_pads_out")
        s_padm_out = sem("s_padm_out")
        s_tab = sem("s_tab")
        s_win_w = [sem(f"s_win_w{i}") for i in range(2)]
        s_whl_out = [sem(f"s_whl_out{i}") for i in range(2)]
        s_early = sem("s_early")
        s_late = [sem(f"s_late{i}") for i in range(2)]
        s_exp = sem("s_exp")
        s_meta = [sem(f"s_meta{i}") for i in range(2)]
        s_zz = sem("s_zz")
        s_diff = sem("s_diff")
        s_back = sem("s_back")
        s_zrow = sem("s_zrow")
        s_none = sem("s_none")
        s_yh = sem("s_yh")
        s_add = [sem(f"s_add{i}") for i in range(2)]
        s_eb2 = sem("s_eb2")
        s_rows = [sem(f"s_rows{i}") for i in range(2)]
        s_xt = sem("s_xt")
        s_xtc = sem("s_xtc")
        s_hid = sem("s_hid")
        s_gel = sem("s_gel")
        s_g = sem("s_g")
        s_mm2 = sem("s_mm2")
        s_y = sem("s_y")
        s_table = sem("s_table")
        s_alone_dve = sem("s_alone_dve")
        s_alone_pool = sem("s_alone_pool")
        s_alone_sp = sem("s_alone_sp")
        s_dve2 = sem("s_dve2")
        s_dve3 = sem("s_dve3")
        s_gh = sem("s_gh")
        s_gkey = sem("s_gkey")
        s_gedge = sem("s_gedge")
        s_goh = sem("s_goh")
        s_grow = sem("s_grow")
        s_growd = sem("s_growd")
        s_gmm = sem("s_gmm")
        block = ctx.enter_context(nc.Block())

        def even(n):
            return [(n + 1) // 2, n // 2]

        def wchunk(e, w):
            if w < 2:
                return E1[bass.ds(e, 1), w * P:(w + 1) * P, :].rearrange("a p n -> (a p) n")
            return E2[bass.ds(e, 1), (w - 2) * 512:(w - 1) * 512, :].rearrange("a (c p) n -> p (a c) n", p=P)

        def wview(buf, w):
            return buf if w < 2 else buf.rearrange("p (c n) -> p c n", n=D)

        tables = [xs, hs]

        @block.sync
        def _(sp):
            with nc.allow_non_contiguous_dma(reason="every 128th destination"):
                sp.dma_start(coarse_d.rearrange("(n a) -> n a", a=1),
                             edges[0:COARSE * P * 2].rearrange("(n a) -> n a", a=2 * P)[:, 0:1]).then_inc(s_coarse_raw, 16)

            def load_pair(e, k):
                for i in range(2):
                    sp.dma_start(wview(wraw[i], 2 * k + i), wchunk(e, 2 * k + i)).then_inc(s_wraw[i], 16)

            def load_x(q):
                sp.dma_start(xraw[q % 2], x[q * QT * P:(q + 1) * QT * P, :].rearrange("(t p) c -> p t c", p=P)
                             ).then_inc(s_x[q % 2], 16)

            load_x(0)
            load_x(1)
            sp.wait_ge(s_coarse_raw, 16)
            sp.dma_start(crow, coarse_d.rearrange("(a n) -> a n", a=1).to_broadcast([GP, COARSE])
                         ).then_inc(s_coarse, 16)
            for i, n in ((0, E_ROWS), (1, 1)):
                sp.dma_start(erow[:, i * E_ROWS:i * E_ROWS + n, :],
                             edges[i * 2 * E_ROWS:i * 2 * E_ROWS + 2 * EPAD].rearrange("(p n e) -> p n e", p=P, e=2)[:, 0:n, :]
                             ).then_inc(s_erow, 16)
            for m, w in enumerate((W1l, W1r, W2l, W2r)):
                sp.dma_start(wsage[:, m], w.rearrange("(k p) c -> p k c", p=P)).then_inc(s_small, 16)
            for i, b in enumerate((b1, b2)):
                sp.dma_start(biasb[:, i, :], b.rearrange("(a c) -> a c", a=1).to_broadcast([P, D])
                             ).then_inc(s_small, 16)
            sp.dma_start(bgb[:, :], bg.rearrange("(a c) -> a c", a=1).to_broadcast([P, NE])).then_inc(s_small, 16)
            sp.dma_start(wgate[:, :, :], Wg.rearrange("(k p) e -> p k e", p=P)).then_inc(s_small, 16)
            with nc.allow_non_contiguous_dma(reason="hidden units onto partitions"):
                sp.dma_start(eb1T[:, :, :], eb1.rearrange("e (c p) -> p e c", p=P)).then_inc(s_small, 16)
            for q in range(2, NX):
                sp.wait_ge(s_xs, q - 1)
                load_x(q)
            load_pair(0, 0)
            sp.wait_ge(s_deg, 1)
            sp.dma_start(deg_d.rearrange("(q p d) -> p q d", p=GP, d=BATCH), deg8[:, :, :]).then_inc(s_deg_out, 16)
            sp.wait_ge(s_deg_out, 16)
            with nc.allow_non_contiguous_dma(reason="nodes onto partitions"):
                sp.dma_start(deg[:, :], deg_d.rearrange("(t p) -> p t", p=P)).then_inc(s_deg_in, 16)

            def general(layer):
                sp.wait_ge(s_h if layer else s_xs, NT if layer else NX)
                with sp.Fori(0, NT) as t:
                    sp.dma_start(table_d[bass.ds(t * P, P), :], tables[layer][:, bass.ds(t, 1), :].rearrange(
                        "p a c -> p (a c)")).then_inc(s_table, 16)
                sp.wait_ge(s_table, 16 * NT * (layer + 1))

                def tile(t, slot, first=False):
                    if layer:
                        load_res(t, slot, first)
                    with sp.Fori(0, ECH) as c:
                        n = (t + layer * NT) * ECH + c
                        sp.wait_ge(s_gmm, n + 1)
                        sp.dma_start(gedge[:, :], edges[bass.ds(c * 2 * P, 2 * P)].rearrange("(p e) -> p e", e=2)
                                     ).then_inc(s_gedge, 16)
                tile(0, 0, True)
                tile(1, 1, True)
                with sp.Fori(1, NT // 2) as i:
                    tile(2 * i, 0)
                    tile(2 * i + 1, 1)
                tile(NT - 1, 0)

            def load_res(t, slot, first=False):
                if not first:
                    sp.wait_ge(s_x1, t - 1)
                    sp.nop().then_inc(s_alone_sp, 1)
                sp.dma_start(xres[slot], x[bass.ds((NT - 1 - t) * P, P), :]).then_inc(s_xres[slot], 16)

            sp.wait_ge(s_flag, 1)
            bad = sp.value_load(flag[0:1, 0:1], min_val=0, max_val=1)
            with sp.If(bad < 1):
                def store_adj(u, slot):
                    sp.wait_ge(s_evac, BPT * u + BPT)
                    sp.dma_start(adj_d[bass.ds(u, 1), :, :].rearrange("a p n -> (a p) n"), adj[slot]
                                 ).then_inc(s_adj_out[slot], 16)
                store_adj(0, 0)
                store_adj(1, 1)
                with sp.Fori(1, NE) as i:
                    store_adj(2 * i, 0)
                    sp.wait_ge(s_wraw_used, 4 * i - 2)
                    load_pair(i - 1, 1)
                    store_adj(2 * i + 1, 1)
                    sp.wait_ge(s_wraw_used, 4 * i)
                    load_pair(i, 0)
                store_adj(2 * NE, 0)
                sp.wait_ge(s_wraw_used, 4 * NE - 2)
                load_pair(NE - 1, 1)
                store_adj(2 * NE + 1, 1)
                with sp.Fori(NE + 1, NT // 2 - 1) as i:
                    store_adj(2 * i, 0)
                    store_adj(2 * i + 1, 1)
                store_adj(NT - 3, 0)
            with sp.Else():
                with sp.Fori(1, NE) as i:
                    sp.wait_ge(s_wraw_used, 4 * i - 2)
                    load_pair(i - 1, 1)
                    sp.wait_ge(s_wraw_used, 4 * i)
                    load_pair(i, 0)
                sp.wait_ge(s_wraw_used, 4 * NE - 2)
                load_pair(NE - 1, 1)
                general(0)
            sp.wait_ge(s_zrow, 1)
            sp.dma_start(xs_d[NE * CAPR:NE * CAPR + FT, :].rearrange("(h p) c -> p h c", p=P), zrow).then_inc(s_none, 16)
            sp.dma_start(meta_d[NE * CAPR:NE * CAPR + FT, :].rearrange("(h p) c -> p h c", p=P), metap[:, :, :]
                         ).then_inc(s_none, 16)
            sp.dma_start(out[NPAD:NPAD + FT, :].rearrange("(h p) c -> p h c", p=P), zrow.bitcast(F32)
                         ).then_inc(s_none, 16)
            def load_early(e):
                sp.dma_start(wts[:, e, :], split_d[e]).then_inc(s_early, 16)
            for i in range(2):
                sp.wait_ge(s_whl_out[i], 16 * NW // 2)
            with sp.If(bad < 1):
                def load_adj(t, slot):
                    sp.wait_ge(s_acc[1], t - 1)
                    sp.nop().then_inc(s_alone_sp, 1)
                    sp.dma_start(adj[slot], adj_d[bass.ds(NT - 1 - t, 1), :, :].rearrange("a p n -> (a p) n")
                                 ).then_inc(s_adj_in[slot], 16)
                    load_res(t, slot)
                sp.wait_ge(s_acc[0], NT)
                load_res(0, 0, True)
                load_res(1, 1, True)
                sp.wait_ge(s_adj_out[0], 16 * (NT // 2))
                sp.wait_ge(s_adj_out[1], 16 * (NT // 2 - 1))
                sp.wait_ge(s_t[0], NT)
                for e in range(EARLY):
                    load_early(e)
                    load_adj(2 * e + 2, 0)
                    load_adj(2 * e + 3, 1)
                with sp.Fori(EARLY + 1, NT // 2) as i:
                    load_adj(2 * i, 0)
                    load_adj(2 * i + 1, 1)
                load_adj(NT - 1, 0)
            with sp.Else():
                sp.wait_ge(s_t[0], NT)
                for e in range(EARLY):
                    load_early(e)
                general(1)

            sp.wait_ge(s_t[1], NT)
            sp.wait_ge(s_acc[1], NT)
            sp.wait_ge(s_early, 16 * EARLY)
            sp.nop().then_inc(s_exp, EARLY)
            sp.dma_start(eb2b, eb2.rearrange("e c -> (e c)").rearrange("(a n) -> a n", a=1).to_broadcast(
                [P, NE * D])).then_inc(s_eb2, 16)

            def load_rows(f, slot):
                r = sp.value_load(tab[0:1, 1, bass.ds(f, 1)], min_val=0, max_val=NE * CAPR)
                sp.dma_start(xl[slot], xs_d[bass.ds(r, FT), :].rearrange("(h p) c -> p h c", p=P)
                             ).then_inc(s_rows[slot], 16)
            def load_meta(f, slot):
                sp.nop().then_inc(s_alone_sp, 1)
                r = sp.value_load(tab[0:1, 1, bass.ds(f, 1)], min_val=0, max_val=NE * CAPR)
                sp.dma_start(ml[slot][:, :, :], meta_d[bass.ds(r, FT), :].rearrange("(h p) c -> p h c", p=P)
                             ).then_inc(s_meta[slot], 16)
            sp.wait_ge(s_pads, 1)
            for i in range(NE):
                r = sp.value_load(padi[0:1, i:i + 1], min_val=0, max_val=NE * CAPR - FT)
                sp.dma_start(xs_d[bass.ds(r, FT), :].rearrange("(h p) c -> p h c", p=P), zrow).then_inc(s_pads_out, 16)
            for i in range(2):
                sp.wait_ge(s_scat[i], 64 * even(NT)[i])
            sp.wait_ge(s_none, 16 * 3)
            sp.wait_ge(s_pads_out, 16 * NE)
            sp.wait_ge(s_tab, 1)
            load_rows(0, 0)
            load_rows(1, 1)
            sp.wait_ge(s_padm_out, 16 * NE)
            load_meta(0, 0)
            load_meta(1, 1)

            def step(f, slot, added=None, load=True):
                if load:
                    sp.wait_ge(s_xt, f)
                    load_rows(f + 1, 1 - slot)
                if added is not None:
                    sp.wait_ge(s_add[slot], added)
                    load_meta(f, slot)
            step(1, 1)
            with sp.Fori(1, (NF - 1) // 2) as i:
                step(2 * i, 0, 32 * i)
                step(2 * i + 1, 1, 32 * i)
            step(NF - 1, 0, 32 * ((NF - 1) // 2), load=False)

        @block.gpsimd
        def _(pool):
            ch = Chain(pool, s_pool)
            pool.iota(iota_i[:, :], pattern=[[1, P]], base=0, channel_multiplier=0)
            pool.iota(bnd_i[:, :, :], pattern=[[BATCH * GP, NQ], [GRP, SUB]], base=0, channel_multiplier=BATCH)
            pool.iota(ecap_i[:, :], pattern=[[CAPR, NE]], base=0, channel_multiplier=0)
            pool.iota(ids_i[:, :], pattern=[[P, NT]], base=0, channel_multiplier=1)
            ch.link(pool.memset(metap[:, :, :], 0))
            pool.iota(metap[:, :, 0], pattern=[[P, 2]], base=NPAD, channel_multiplier=1)
            pool.iota(fi_i[:, :], pattern=[[1, NF]], base=0, channel_multiplier=0)
            pool.memset(epst[:, :], EPS / XSCALE ** 2)
            pool.memset(ones[:, :], 1.0).then_inc(s_const, 1)
            ch.link(pool.memset(ident[:, :], 0.0))
            pool.affine_select(out=ident[:, :], in_=ident[:, :], compare_op=ALU.not_equal, fill=1.0, base=0,
                               pattern=[[-1, P]], channel_multiplier=1).then_inc(s_const, 1)
            pool.affine_select(out=ltri[:, :], in_=ones[:, :], compare_op=ALU.is_gt, fill=0.0, base=0,
                               pattern=[[1, P]], channel_multiplier=-1).then_inc(s_const, 1)
            pool.memset(msum[:, :], 0.0).then_inc(s_const, 1)

            def low_x(q):
                pool.wait_ge(s_xn, q + 1)
                t = slice(q * QT, (q + 1) * QT)
                pool.tensor_tensor(xs[:, t, D:2 * D], xraw[q % 2], xs[:, t, 0:D], ALU.subtract).then_inc(s_xs, 1)
            low_x(0)
            low_x(1)
            pool.wait_ge(s_row, 1)
            table = edges.rearrange("(n a) -> n a", a=1)
            for q in range(NQ):
                pool.indirect_dma_start(wfine[:, q, :, :].rearrange("p w e -> p (w e)"), None, table,
                                        bass.IndirectOffsetOnAxis(ap=row_i[:, q:q + 1], axis=0)
                                        ).then_inc(s_fine[q], 16)
            for q in range(NQ):
                pool.wait_ge(s_lo, q + 1)
                for g in range(SUB):
                    pool.indirect_dma_start(wd[:, q, g, :, :].rearrange("p w e -> p (w e)"), None, table,
                                            bass.IndirectOffsetOnAxis(ap=lo_i[:, q, g:g + 1], axis=0)
                                            ).then_inc(s_win[q], 16)
                if q in LOW_AT:
                    low_x(2 + LOW_AT.index(q))
            pool.wait_ge(s_ssum, 1)
            pool.partition_all_reduce(ssall[:, 0:4], ssum[:, 0:4], P, RADD).then_inc(s_ssall, 1)
            pool.wait_ge(s_viol, 1)
            pool.partition_all_reduce(violr[:, :], viol[:, :], P, RADD).then_inc(s_violr, 1)
            low_x(NX - 1)
            pool.wait_ge(s_ssum, 2)
            pool.partition_all_reduce(ssall[:, 4:7], ssum[:, 4:7], P, RADD).then_inc(s_ssall, 1)

            def load_w(e, w):
                pool.dma_start(wview(w_in[w % 2], w), wchunk(e, w)).then_inc(s_win_w[w % 2], 16)

            def split_w(e, w, first=False, last=False):
                n = 4 * e + w
                pool.wait_ge(s_win_w[w % 2], 32 * e + 16 * (w // 2) + 16)
                pool.nop().then_inc(s_alone_pool, 1)
                scale = scl[:, S_E1:S_E1 + 1] if w < 2 else scl[:, S_E2:S_E2 + 1]
                ch.link(pool.tensor_scalar(w_sc, w_in[w % 2], scale, None, ALU.mult))
                if not last:
                    load_w(e + w // 2, (w + 2) % 4)
                if not first:
                    pool.wait_ge(s_whl_out[w % 2], 32 * e + 16 * (w // 2))
                pool.nop().then_inc(s_alone_pool, 1)
                ch.link(pool.tensor_copy(w_hl[w % 2][:, 0:1024], w_sc))
                ch.link(pool.tensor_tensor(w_hl[w % 2][:, 1024:2048], w_sc, w_hl[w % 2][:, 0:1024], ALU.subtract))
                pool.dma_start(split_d[bass.ds(e, 1), :, w * 2048:(w + 1) * 2048].rearrange("a p n -> (a p) n"),
                               w_hl[w % 2]).then_inc(s_whl_out[w % 2], 16)

            pool.wait_ge(s_scales_e, 1)
            load_w(0, 0)
            load_w(0, 1)
            for w in range(4):
                split_w(0, w, first=w < 2)
            base = ch.n
            with pool.Fori(1, NE - 1) as e:
                ch.at(base + 12 * (e - 1))
                for w in range(4):
                    split_w(e, w)
            ch.at(base + 12 * (NE - 2))
            for w in range(4):
                split_w(NE - 1, w, last=w >= 2)

            pool.wait_ge(s_flag, 1)
            bad = pool.value_load(flag[0:1, 0:1], min_val=0, max_val=1)

            def gathers(t, layer):
                with pool.Fori(0, ECH) as c:
                    n = (t + layer * NT) * ECH + c
                    pool.wait_ge(s_gedge, 16 * n + 16)
                    pool.nop().then_inc(s_alone_pool, 1)
                    pool.indirect_dma_start(grow, None, table_d, bass.IndirectOffsetOnAxis(ap=gedge[:, 1:2], axis=0)
                                            ).then_inc(s_grow, 16)
                    pool.wait_ge(s_grow, 16)
                    pool.inc_swdge_sem([s_grow], [16], mode="sub")
                    pool.nop().then_inc(s_growd, 1)

            def scatter(p, slot):
                pool.wait_ge(s_pos, p + 1)
                pool.nop().then_inc(s_alone_pool, 1)
                for k in range(2):
                    where = bass.IndirectOffsetOnAxis(ap=posi[slot][k][:, 0:1], axis=0)
                    pool.indirect_dma_start(xs_d, where, x2[slot], None).then_inc(s_scat[slot], 16)
                    pool.indirect_dma_start(meta_d, where, meta[slot][:, k, :], None).then_inc(s_scat[slot], 16)

            pool.wait_ge(s_whl_out[0], 16 * NW // 2)
            pool.memset(zrow, 0.0).then_inc(s_zrow, 1)
            with pool.If(bad < 1):
                with pool.Fori(0, NT // 2) as i:
                    scatter(2 * i, 0)
                    scatter(2 * i + 1, 1)
            with pool.Else():
                for i in range(2):
                    pool.wait_ge(s_whl_out[i], 16 * NW // 2)
                pool.wait_ge(s_table, 16 * NT)
                with pool.Fori(0, NT) as t:
                    gathers(t, 0)
                pool.wait_ge(s_table, 32 * NT)
                with pool.Fori(0, NT // 2) as i:
                    for slot in range(2):
                        gathers(2 * i + slot, 1)
                        scatter(2 * i + slot, slot)
                        pool.wait_ge(s_scat[slot], 64 * i + 64)
                        pool.nop().then_inc(s_alone_pool, 1)
                gathers(NT - 1, 1)

            def load_late(e):
                pool.dma_start(wts[:, e, :], split_d[e]).then_inc(s_late[(e - EARLY) % 2], 16)
            pool.wait_ge(s_t[1], NT)
            pool.wait_ge(s_acc[1], NT)
            load_late(EARLY)
            scatter(NT - 1, 0)
            pool.wait_ge(s_exp, EARLY)
            for i in range(2):
                pool.wait_ge(s_rows[i], 16)
                pool.wait_ge(s_meta[i], 16)
            for e in range(EARLY, NE):
                if e < NE - 1:
                    load_late(e + 1)
                pool.wait_ge(s_late[(e - EARLY) % 2], 16 * ((e - EARLY) // 2 + 1))
                pool.nop().then_inc(s_exp, 1)
            for i in range(2):
                pool.wait_ge(s_x1_out[i], 16 * even(NT)[i])
            pool.wait_ge(s_none, 16 * 3)

            def add(f, slot, before=None):
                pool.wait_ge(s_y, 2 * f + 2)
                if before is not None:
                    pool.wait_ge(s_add[1 - slot], before)
                pool.nop().then_inc(s_alone_pool, 1)
                for h in range(2):
                    pool.indirect_dma_start(out, bass.IndirectOffsetOnAxis(ap=ml[slot][:, h, 0:1], axis=0),
                                            yt[slot][:, h, :], None, compute_op=ALU.add).then_inc(s_add[slot], 16)
            add(0, 0)
            add(1, 1, 32)
            with pool.Fori(1, NF // 2) as i:
                add(2 * i, 0, 32 * i)
                add(2 * i + 1, 1, 32 * i + 32)
            add(NF - 1, 0, 32 * (NF // 2))
            for i in range(2):
                pool.wait_ge(s_add[i], 32 * even(NF)[i])

        @block.scalar
        def _(act):
            ch = Chain(act, s_act)
            act.wait_ge(s_const, 4)
            act.activation(iota[:, :], iota_i[:, :], ACT.Copy).then_inc(s_iota, 1)
            act.activation(bnd[:, :, :], bnd_i[:, :, :], ACT.Copy).then_inc(s_iota, 1)
            act.activation(ecap[:, :], ecap_i[:, :], ACT.Copy).then_inc(s_iota, 1)
            act.activation(ftab[:, 0, :], fi_i[:, :], ACT.Copy).then_inc(s_iota, 1)

            def norm_x(q):
                t = slice(q * QT, (q + 1) * QT)
                act.wait_ge(s_stats, q + 1)
                act.activation(sd[:, t], mv[:, t, 1], ACT.Sqrt, bias=epst[:, 0:1], scale=XSCALE ** -2
                               ).then_inc(s_sd, 1)
                act.wait_ge(s_norm, q + 1)
                for j in range(QT):
                    u = q * QT + j
                    last = act.activation(xraw[q % 2][:, j, :], xraw[q % 2][:, j, :], ACT.Identity,
                                          bias=nmr[:, u:u + 1], scale=rs[:, u:u + 1])
                ch.link(last)
                act.activation(xs[:, t, 0:D], xraw[q % 2], ACT.Copy).then_inc(s_xn, 1)

            def square(view, col):
                n = view.shape[1] * (view.shape[2] if len(view.shape) == 3 else 1)
                v = bank[7][:, 0:n]
                if len(view.shape) == 3:
                    v = v.rearrange("p (a b) -> p a b", a=view.shape[1])
                ch.link(act.activation(v, view, ACT.Square, accum_out=ss[:, col:col + 1]))

            def square_pair(e, k):
                for i in range(2):
                    w = 2 * k + i
                    act.wait_ge(s_wraw[i], 32 * e + 16 * k + 16)
                    act.activation(wraw[i], wraw[i], ACT.Square, accum_out=ss[:, bass.ds(4 * e + w + 7, 1)]
                                   ).then_inc(s_wraw_used, 1)

            norm_x(0)
            norm_x(1)
            act.wait_ge(s_small, 16 * 9)
            for m in range(4):
                square(wsage[:, m], m)
            square(wgate[:, :, :], 4)
            square(biasb[:, 0, :], 5)
            square(eb1T[:, :, :], 6)
            act.nop().then_inc(s_ss, 1)
            def key_copy(q):
                act.wait_ge(s_keyT, q + 1)
                for k in range(2):
                    act.activation(keys[:, k, q * SUB * GP:(q + 1) * SUB * GP].rearrange("p (g s) -> p s g", s=SUB),
                                   bank[2 * (q % 2) + k][:, 0:SUB * GP].rearrange("p (s g) -> p s g", s=SUB), ACT.Copy
                                   ).then_inc(s_keyc, 1)
            copied = 0
            for q in range(2, NX):
                norm_x(q)
                while q >= 4 and copied < min(NQ, 2 * (q - 3)):
                    key_copy(copied)
                    copied += 1
            for q in range(copied, NQ):
                key_copy(q)
            act.wait_ge(s_ssall, 1)
            act.activation(bound[:, 0:4], ssall[:, 0:4], ACT.Sqrt).then_inc(s_bound, 1)

            def expert_bounds():
                act.wait_ge(s_wraw_used, NW)
                act.nop().then_inc(s_ss, 1)
                act.wait_ge(s_ssall, 2)
                act.activation(bound[:, 4:7], ssall[:, 4:7], ACT.Sqrt).then_inc(s_bound, 1)

            def t_copy(p, layer):
                act.wait_ge(s_t[layer], p + 1)
                act.activation(mT[:, :, :], tpm[:, :].rearrange("p (b n) -> p b n", b=4), ACT.Copy
                               ).then_inc(s_tc[layer], 1)
                act.activation(nT[:, :, :], tpx[:, :].rearrange("p (b n) -> p b n", b=4), ACT.Copy
                               ).then_inc(s_tc[layer], 1)

            def evac(u, slot, j):
                act.wait_ge(s_cnt, BPT * u + j + 1)
                view = adj[slot].rearrange("p (a n) -> p n a", a=NT)[:, BATCH * j:BATCH * (j + 1), :]
                act.activation(view, cps[j % 2][:, 0:SUB * KW].rearrange("p (n a) -> p n a", n=BATCH), ACT.Copy
                               ).then_inc(s_evac, 1)

            def step1(t, slot, build=True, post=True):
                for j in range(BPT):
                    if build:
                        evac(t + 1, 1 - slot, j)
                    if post and j == T_AT:
                        t_copy(t - 1, 0)

            act.wait_ge(s_flag, 1)
            bad = act.value_load(flag[0:1, 0:1], min_val=0, max_val=1)
            with act.If(bad < 1):
                act.wait_ge(s_xs, NX)
                for j in range(BPT):
                    evac(0, 0, j)
                step1(0, 0, post=False)
                act.wait_ge(s_acc[0], 1)
                act.wait_ge(s_adj_out[0], 16)
                step1(1, 1)

                def pair(i, squares):
                    for k in range(2):
                        if squares:
                            square_pair(i - 1, k)
                        act.wait_ge(s_acc[0], 2 * i + k)
                        act.wait_ge(s_adj_out[1 - k], 16 * (i + k))
                        step1(2 * i + k, k)
                with act.Fori(1, NE + 1) as i:
                    pair(i, True)
                expert_bounds()
                with act.Fori(NE + 1, (NT - 1) // 2) as i:
                    pair(i, False)
                step1(NT - 1, 0, build=False)
                t_copy(NT - 1, 0)
            with act.Else():
                with act.Fori(0, NE) as e:
                    square_pair(e, 0)
                    square_pair(e, 1)
                expert_bounds()
                with act.Fori(0, NT) as t:
                    t_copy(t, 0)

            def post2(p, slot, last=False):
                t_copy(p, 1)
                act.wait_ge(s_var2, p + 1)
                act.activation(sd2[:, :], mv2[:, 1:2], ACT.Sqrt, bias=epst[:, 0:1], scale=XSCALE ** -2
                               ).then_inc(s_sd2, 1)
                act.wait_ge(s_x1, p + 1)
                act.dma_start(out[bass.ds((NT - 1 - p) * P, P), :], x1t[slot]).then_inc(s_x1_out[slot], 16)
                act.wait_ge(s_x2t, p + 1)
                act.activation(x2T, tpm[:, :].rearrange("p (b n) -> p b n", b=4), ACT.Copy).then_inc(s_x2tc, 1)
                act.wait_ge(s_diff, p + 1)
                act.activation(zz[slot][:, :], diff[slot][:, :], ACT.Exp).then_inc(s_zz, 1)
                if not last:
                    act.activation(sq_back[:, :], epst[:, 0:1], ACT.Sqrt).then_inc(s_back, 1)
                    act.wait_ge(s_back, p + 1)
            with act.Fori(0, NT // 2) as i:
                for slot in range(2):
                    post2(2 * i + slot, slot)
            post2(NT - 1, 0, last=True)

            act.wait_ge(s_pads, 1)
            for i in range(NE):
                r = act.value_load(padi[0:1, i:i + 1], min_val=0, max_val=NE * CAPR - FT)
                act.dma_start(meta_d[bass.ds(r, FT), :].rearrange("(h p) c -> p h c", p=P), metap[:, :, :]
                              ).then_inc(s_padm_out, 16)

            act.wait_ge(s_tab, 1)

            def xt_copy(f, slot):
                act.wait_ge(s_xt, f + 1)
                act.activation(xT[slot][:, 0:2, :], xtp[0], ACT.Copy).then_inc(s_xtc, 1)

            def step(f, slot, nxt=True, first=False):
                e = act.value_load(tab[0:1, 0, bass.ds(f, 1)], min_val=0, max_val=NE - 1)
                for c in range(HC):
                    act.wait_ge(s_hid, HC * f + c + 1)
                    if not (first and c < 2):
                        act.wait_ge(s_g, HC * f + c - 1)
                    act.activation(gel[c % 2], hps[c % 4][:, 0:FT], ACT.Gelu,
                                   bias=eb1T[:, bass.ds(e, 1), c], scale=cc[:, 3:4]).then_inc(s_gel, 1)
                    if nxt and c == XT_AT:
                        xt_copy(f + 1, 1 - slot)
            xt_copy(0, 0)
            step(0, 0, first=True)
            with act.Fori(0, (NF - 3) // 2) as i:
                step(2 * i + 1, 1)
                step(2 * i + 2, 0)
            step(NF - 2, 1)
            step(NF - 1, 0, nxt=False)

        @block.tensor
        def _(pe):
            pe.wait_ge(s_const, 4)
            for q in range(NQ):
                pe.wait_ge(s_key, q + 1)
                if q >= 2:
                    pe.wait_ge(s_keyc, 2 * (q - 1))
                for k in range(2):
                    for g in range(SUB):
                        last = pe.matmul(bank[2 * (q % 2) + k][:, g * GP:(g + 1) * GP],
                                         key[k][:, q, g, :], ident[0:GP, 0:GP], start=True, stop=True)
                last.then_inc(s_keyT, 1)

            def count(u, j, first=False):
                n = BPT * u + j
                pe.wait_ge(s_oh, n + 1)
                if not first:
                    pe.wait_ge(s_evac, n - 1)
                for g in range(SUB):
                    last = pe.matmul(cps[j % 2][:, g * KW:(g + 1) * KW], oh1[:, j % RING, g, :], oh2[:, j % RING, g, :],
                                     start=True, stop=True)
                last.then_inc(s_cnt, 1)

            def sums(slot, layer, a0, a1):
                table, into = tables[layer], acc[(slot + layer) % 2]
                for a in range(a0, a1):
                    for h in range(2):
                        last = pe.matmul(into[:, 0:D], adj[slot][:, a * P:(a + 1) * P],
                                         table[:, a, h * D:(h + 1) * D],
                                         start=(a == 0 and h == 0), stop=(a == NT - 1 and h == 1))
                return last

            def turn(p, slot, layer):
                own = NT - 1 - p if layer else p
                pe.wait_ge(s_mean[layer], p + 1)
                for b in range(4):
                    pe.matmul(tpm[:, b * P:(b + 1) * P], meanhl[slot][:, b * P:(b + 1) * P], ident[:, :],
                              start=True, stop=True)
                for b in range(4):
                    last = pe.matmul(tpx[:, b * P:(b + 1) * P],
                                     tables[layer][:, bass.ds(own, 1), b * P:(b + 1) * P].rearrange("p a c -> p (a c)"),
                                     ident[:, :], start=True, stop=True)
                last.then_inc(s_t[layer], 1)

            def dense(p, layer):
                pe.wait_ge(s_tc[layer], 2 * p + 2)
                if not layer:
                    pe.wait_ge(s_wsplit, 1)
                n = 0
                for m, rows in enumerate((mT, nT)):
                    for k in range(KB):
                        for ra, wb in ((0, 0), (0, 1), (1, 0)):
                            last = pe.matmul(dps[:, 0:D], rows[:, 2 * ra + k, :], wsplit[:, 2 * layer + m, k, wb, :],
                                             start=(n == 0), stop=(n == 11))
                            n += 1
                last.then_inc(s_dense[layer], 1)

            def step1(t, slot, build=True, post=True, reuse=True):
                pe.wait_ge(s_evac, BPT * t + BPT)
                if reuse:
                    pe.wait_ge(s_mean[0], t - 1)
                for j in range(BPT):
                    if build:
                        count(t + 1, j)
                    last = sums(slot, 0, 3 * j, 3 * j + 3 if j < BPT - 1 else NT)
                    if post and j == T_AT:
                        turn(t - 1, 1 - slot, 0)
                    if post and j == D_AT:
                        if reuse:
                            pe.wait_ge(s_h, t - 1)
                        dense(t - 1, 0)
                last.then_inc(s_acc[0], 1)

            pe.nop().then_inc(s_gmm, 1)
            pe.wait_ge(s_flag, 1)
            pe.wait_ge(s_xs, NX)
            pe.wait_ge(s_keyc, 2 * NQ)
            bad = pe.value_load(flag[0:1, 0:1], min_val=0, max_val=1)

            def general(t, slot, layer):
                into = acc[(slot + layer) % 2]
                pe.matmul(into[:, 0:D], zeros[:, 0:P], zeros[:, 0:D], start=True, stop=False)
                if not layer:
                    pe.matmul(dgp, zeros[:, 0:P], zeros[:, 0:1], start=True, stop=False)
                with pe.Fori(0, ECH) as c:
                    n = (t + layer * NT) * ECH + c
                    pe.wait_ge(s_goh, n + 1)
                    pe.wait_ge(s_growd, n + 1)
                    if not layer:
                        pe.matmul(dgp, goh, ones[:, 0:1], start=False, stop=False)
                    pe.matmul(into[:, 0:D], goh, grow[:, 0:D], start=False, stop=False)
                    pe.matmul(into[:, 0:D], goh, grow[:, D:2 * D], start=False, stop=False).then_inc(s_gmm, 1)
                if not layer:
                    pe.matmul(dgp, zeros[:, 0:P], zeros[:, 0:1], start=False, stop=True)
                pe.matmul(into[:, 0:D], zeros[:, 0:P], zeros[:, 0:D], start=False, stop=True
                          ).then_inc(s_acc[layer], 1)

            with pe.If(bad < 1):
                for j in range(BPT):
                    count(0, j, first=j < 2)
                step1(0, 0, post=False, reuse=False)
                step1(1, 1, reuse=False)
                with pe.Fori(1, (NT - 1) // 2) as i:
                    step1(2 * i, 0)
                    step1(2 * i + 1, 1)
                step1(NT - 1, 0, build=False)
            with pe.Else():
                def tile(t, slot, first=False):
                    general(t, slot, 0)
                    turn(t, slot, 0)
                    if not first:
                        pe.wait_ge(s_h, t)
                    dense(t, 0)
                tile(0, 0, True)
                tile(1, 1)
                with pe.Fori(1, NT // 2) as i:
                    tile(2 * i, 0)
                    tile(2 * i + 1, 1)
                tile(NT - 1, 0)


            def turn_x2(p, slot):
                pe.wait_ge(s_x2, p + 1)
                for b in range(4):
                    last = pe.matmul(tpm[:, b * P:(b + 1) * P], x2[slot][:, b * P:(b + 1) * P], ident[:, :],
                                     start=True, stop=True)
                last.then_inc(s_x2t, 1)

            def gate(p, first=False):
                pe.wait_ge(s_x2tc, p + 1)
                if not first:
                    pe.wait_ge(s_pos, p)
                n = 0
                for k in range(KB):
                    for ra, wb in ((0, 0), (0, 1), (1, 0)):
                        last = pe.matmul(lgp, x2T[:, 2 * ra + k, :], wgs[:, k, wb, :], start=(n == 0), stop=(n == 5))
                        n += 1
                last.then_inc(s_logits, 1)

            def rank(p):
                pe.wait_ge(s_mask, p + 1)
                pe.matmul(rkp, ones[:, :], msum[:, :], start=True, stop=False)
                pe.matmul(rkp, ltri[:, :], mask[:, :], start=False, stop=True).then_inc(s_rank, 1)

            def free_dense(p, first):
                if not first:
                    pe.wait_ge(s_x1, p)

            def step2(t, slot, loads=None, place=True, first=False):
                if loads is not None:
                    pe.wait_ge(s_adj_in[slot], loads)
                    pe.wait_ge(s_mean[1], t - 1)
                a = 0
                for stop, what in ((R2_AT, "rank"), (T2_AT, "turn"), (D2_AT, "dense"), (X2_AT, "x2"), (G2_AT, "gate")):
                    sums(slot, 1, a, stop)
                    a = stop
                    if what == "rank" and place:
                        rank(t - 2)
                    elif what == "turn":
                        turn(t - 1, 1 - slot, 1)
                    elif what == "dense":
                        free_dense(t - 1, first)
                        dense(t - 1, 1)
                    elif what == "x2":
                        turn_x2(t - 1, 1 - slot)
                    elif what == "gate":
                        gate(t - 1, first)
                sums(slot, 1, a, NT).then_inc(s_acc[1], 1)

            def whole_post(p, slot, first=False):
                turn(p, slot, 1)
                free_dense(p, first)
                dense(p, 1)
                turn_x2(p, slot)
                gate(p, first)
                rank(p)

            with pe.If(bad < 1):
                pe.wait_ge(s_h, NT - 1)
                sums(0, 1, 0, T2_AT)
                turn(NT - 1, 0, 0)
                sums(0, 1, T2_AT, D2_AT)
                dense(NT - 1, 0)
                sums(0, 1, D2_AT, NT - 1)
                pe.wait_ge(s_h, NT)
                sums(0, 1, NT - 1, NT).then_inc(s_acc[1], 1)
                step2(1, 1, place=False, first=True)
                with pe.Fori(1, (NT - 1) // 2) as i:
                    step2(2 * i, 0, 16 * i)
                    step2(2 * i + 1, 1, 16 * i)
                step2(NT - 1, 0, 16 * ((NT - 1) // 2))
                rank(NT - 2)
                whole_post(NT - 1, 0)
            with pe.Else():
                pe.wait_ge(s_h, NT)

                def tile(t, slot, first=False):
                    general(t, slot, 1)
                    whole_post(t, slot, first)
                tile(0, 0, True)
                tile(1, 1)
                with pe.Fori(1, NT // 2) as i:
                    tile(2 * i, 0)
                    tile(2 * i + 1, 1)
                tile(NT - 1, 0)
            pe.wait_ge(s_pos, NT)
            pe.matmul(cnp, ones[:, :], msum[:, :], start=True, stop=True).then_inc(s_cntp, 1)

            pe.wait_ge(s_tab, 1)

            def turn_rows(f, slot, loads, first=False):
                pe.wait_ge(s_rows[slot], loads)
                if not first:
                    pe.wait_ge(s_xtc, 2 * f)
                for b in range(4):
                    for h in range(2):
                        last = pe.matmul(xtp[b // 2][:, b % 2, h * P:(h + 1) * P], xl[slot][:, h, b * P:(b + 1) * P],
                                         ident[:, :], start=True, stop=True)
                last.then_inc(s_xt, 1)

            def hidden(f, c, slot, e, first=False):
                if not first:
                    pe.wait_ge(s_gel, HC * f + c - 3)
                n = 0
                for k in range(KB):
                    w = [wts[:, bass.ds(e, 1), o:o + P].rearrange("p a n -> p (a n)")
                         for o in (k * 2048 + c * P, k * 2048 + 1024 + c * P)]
                    for wa, rb in ((0, 0), (0, 1), (1, 0)):
                        last = pe.matmul(hps[c % 4][:, 0:FT], w[wa], xT[slot][:, 2 * rb + k, :],
                                         start=(n == 0), stop=(n == 5))
                        n += 1
                last.then_inc(s_hid, 1)

            def output(f, c, slot, e, first=False):
                if c == 0 and not first:
                    pe.wait_ge(s_yh, 2 * f - 2)
                pe.wait_ge(s_g, HC * f + c + 1)
                for wb, parts in ((0, (0, 1)), (1, (0,))):
                    o = (2 + c // 4) * 2048 + wb * 1024 + (c % 4) * D
                    w = wts[:, bass.ds(e, 1), o:o + D].rearrange("p a n -> p (a n)")
                    for h in range(2):
                        for ga in parts:
                            last = pe.matmul(yps[slot][:, h, :], ghl[c % 4][:, ga, h * P:(h + 1) * P], w,
                                             start=(c == 0 and h == 0 and (ga, wb) == (0, 0)),
                                             stop=(c == HC - 1 and wb == 1), skip_group_check=True)
                last.then_inc(s_mm2, 1)

            before = pe.alloc_register("expert_before")

            def step(f, slot, loads=None, nxt=True, prev=True, first=False, second=False):
                ep = pe.snap(before, min_val=0, max_val=NE - 1) if prev else None
                e = pe.value_load(tab[0:1, 0, bass.ds(f, 1)], min_val=0, max_val=NE - 1)
                pe.wait_ge(s_exp, e + 1)
                pe.wait_ge(s_xtc, 2 * f + 2)
                for c in range(HC):
                    hidden(f, c, slot, e, first=first and c < 4)
                    if c >= LAG:
                        output(f, c - LAG, slot, e, first=first or second)
                    elif prev:
                        output(f - 1, HC - LAG + c, 1 - slot, ep)
                    if nxt and c == XT_AT - 1:
                        turn_rows(f + 1, 1 - slot, loads)
                pe.reg_mov(before, e)
            turn_rows(0, 0, 16, first=True)
            step(0, 0, 16, prev=False, first=True)
            step(1, 1, 32, second=True)
            with pe.Fori(1, (NF - 1) // 2) as i:
                step(2 * i, 0, 16 * i + 16)
                step(2 * i + 1, 1, 16 * i + 32)
            step(NF - 1, 0, nxt=False)
            e = pe.snap(before, min_val=0, max_val=NE - 1)
            for c in range(HC - LAG, HC):
                output(NF - 1, c, 0, e)

        @block.vector
        def _(dve):
            ch = Chain(dve, s_dve)

            def norm_x(q):
                dve.wait_ge(s_x[q % 2], 16 * (q // 2 + 1))
                t = slice(q * QT, (q + 1) * QT)
                for j in range(QT):
                    last = dve.bn_stats(stats[:, j, :], xraw[q % 2][:, j, :])
                ch.link(last)
                for j in range(QT):
                    last = dve.bn_aggr(mv[:, q * QT + j, :], stats[:, j, :])
                last.then_inc(s_stats, 1)
                dve.wait_ge(s_sd, q + 1)
                ch.link(dve.reciprocal(rs[:, t], sd[:, t]))
                dve.scalar_tensor_tensor(out=nmr[:, t], in0=mv[:, t, 0], scalar=-1.0, in1=rs[:, t],
                                         op0=ALU.mult, op1=ALU.mult).then_inc(s_norm, 1)

            dve.memset(zeros[:, :], 0.0)
            norm_x(0)
            norm_x(1)
            dve.wait_ge(s_iota, 4)
            dve.wait_ge(s_coarse, 16)
            ch.link(dve.tensor_copy(crow16, crow))
            for q in range(NQ):
                ch.link(dve.tensor_scalar(junk[0:GP, 0:COARSE], crow16, bnd[:, q, 0:1], 0.0, ALU.is_lt, ALU.add,
                                          accum_out=rowf_[:, 0, q:q + 1]))
            ch.link(dve.tensor_scalar(rowf_[:, 1, :], rowf_[:, 0, :], -1.0, 0.0, ALU.add, ALU.max))
            dve.tensor_scalar(row_i[:, :], rowf_[:, 1, :], 2.0 * P, None, ALU.mult).then_inc(s_row, 1)
            dve.tensor_scalar(rowf_[:, 2, :], rowf_[:, 1, :], float(P), None, ALU.mult)
            dve.wait_ge(s_erow, 32)
            ch.link(dve.tensor_tensor_reduce(out=junk[:, 0:E_ROWS], in0=erow[:, 0:E_ROWS, 0], in1=erow[:, 1:E_ROWS + 1, 0],
                                             scale=1.0, scalar=0.0, op0=ALU.subtract, op1=ALU.max,
                                             accum_out=viol[:, 0:1]))
            norm_x(2)
            for q in range(NQ):
                dve.wait_ge(s_fine[q], 16)
                ch.link(dve.tensor_copy(fine16[q % 2], wfine[:, q, :, 0]))
                for g in range(SUB):
                    last = dve.tensor_scalar(junk[0:GP, g * FW:(g + 1) * FW], fine16[q % 2], bnd[:, q, g:g + 1], 0.0,
                                             ALU.is_lt, ALU.add, accum_out=cnt[:, q, g:g + 1])
                ch.link(last)
                dve.tensor_scalar(lo_i[:, q, :], cnt[:, q, :], rowf_[:, 2, q:q + 1], 2.0, ALU.add, ALU.mult
                                  ).then_inc(s_lo, 1)
            dve.wait_ge(s_ss, 1)
            dve.tensor_tensor(ssum[:, S_W1:S_W1 + 1], ss[:, 0:1], ss[:, 1:2], ALU.add)
            dve.tensor_tensor(ssum[:, S_W2:S_W2 + 1], ss[:, 2:3], ss[:, 3:4], ALU.add)
            dve.tensor_copy(ssum[:, S_WG:S_H + 1], ss[:, 4:6]).then_inc(s_ssum, 1)
            norm_x(3)

            def scales(a, b, weights, result, length):
                v = slice(a, b)
                ch.link(dve.tensor_scalar(bound[:, v], bound[:, v], 1.01, 1e-15, ALU.mult, ALU.max))
                ch.link(dve.scalar_tensor_tensor(out=bound[:, result:result + 1], in0=bound[:, weights:weights + 1],
                                                 scalar=length, in1=bound[:, result:result + 1], op0=ALU.mult,
                                                 op1=ALU.add))
                ch.link(dve.tensor_scalar(p2[:, v], bound[:, v].bitcast(I32), 0x7F800000, None, ALU.bitwise_and))
                ch.link(dve.tensor_scalar(ip2[:, v], p2[:, v], -1.0, float(0x7F000000), ALU.mult, ALU.add))
                ch.link(dve.tensor_scalar(scl[:, v], ip2[:, v].bitcast(F32), 8192.0, None, ALU.mult))
                ch.link(dve.tensor_scalar(inv[:, v], p2[:, v].bitcast(F32), 1.0 / 8192.0, None, ALU.mult))

            def factor(i, a, b, k):
                ch.link(dve.scalar_tensor_tensor(out=cc[:, i:i + 1], in0=a, scalar=k, in1=b,
                                                 op0=ALU.mult, op1=ALU.mult))
            def degrees(q):
                for i in range(BATCH):
                    last = dve.tensor_scalar(junk[0:GP, i * WIN:(i + 1) * WIN], dl[:, q, i // GRP, 0:WIN],
                                             float(i % GRP), 0.0, ALU.is_equal, ALU.add, accum_out=deg8[:, q, i:i + 1])
                ch.link(last)
            for q in range(NQ):
                if q > 0:
                    degrees(q - 1)
                dve.wait_ge(s_win[q], 16 * SUB)
                ch.link(dve.tensor_tensor(dl[:, q, :, :], wd[:, q, :, :, 0], bnd[:, q, :].rearrange(
                    "p (s a) -> p s a", a=1).to_broadcast([GP, SUB, WINX]), ALU.subtract))
                dve.tensor_scalar(sblk[:, q, :, :], wd[:, q, :, 0:WIN, 1], 7, None, ALU.logical_shift_right)
                ch.link(dve.tensor_scalar(dl[:, q, :, :], dl[:, q, :, :], -8.0, 64.0, ALU.max, ALU.min))
                dve.scalar_tensor_tensor(out=key[0][:, q, :, :], in0=sblk[:, q, :, :], scalar=-float(P),
                                         in1=wd[:, q, :, 0:WIN, 1], op0=ALU.mult, op1=ALU.add)
                dve.scalar_tensor_tensor(out=key[1][:, q, :, :], in0=dl[:, q, :, 0:WIN], scalar=float(NT),
                                         in1=sblk[:, q, :, :], op0=ALU.mult, op1=ALU.add).then_inc(s_key, 1)
                if q in NORM_AT:
                    norm_x(4 + NORM_AT.index(q))
            dve.memset(viol[:, 1:2], 0.0)
            ch.link(dve.tensor_copy(vj[:, :, :], dl[:, :, :, WIN]))
            ch.link(dve.tensor_scalar(cnt[:, :, :], vj[:, :, :], float(GRP), 0.0, ALU.is_lt, ALU.add,
                                      accum_out=viol[0:GP, 1:2]))
            dve.nop().then_inc(s_viol, 1)
            degrees(NQ - 1)
            dve.nop().then_inc(s_deg, 1)
            dve.wait_ge(s_violr, 1)
            ch.link(dve.tensor_tensor(viol[:, 0:1], violr[:, 0:1], violr[:, 1:2], ALU.add))
            dve.tensor_scalar(flag[:, :], viol[:, 0:1], 1.0, None, ALU.min).then_inc(s_flag, 1)
            dve.wait_ge(s_keyc, 2 * NQ)

            def conv_scales():
                dve.wait_ge(s_bound, 1)
                scales(S_W1, S_H + 1, S_W1, S_H, 23.0)
                factor(0, scl[:, S_H:S_H + 1], inv[:, S_W1:S_W1 + 1], 1.0 / XSCALE)
                factor(1, inv[:, S_H:S_H + 1], inv[:, S_W2:S_W2 + 1], 1.0)
                ch.link(dve.tensor_scalar(cc[:, 2:3], inv[:, S_WG:S_WG + 1], 1.0 / XSCALE, None, ALU.mult))
                ch.link(dve.tensor_scalar(biasb[:, 0, :], biasb[:, 0, :], scl[:, S_H:S_H + 1], None, ALU.mult))

            def conv_weights(m):
                sc = scl[:, S_W1 + m // 2:S_W1 + m // 2 + 1]
                ch.link(dve.tensor_scalar(wsplit[:, m, :, 0, :], wsage[:, m], sc, None, ALU.mult))
                dve.scalar_tensor_tensor(out=wsplit[:, m, :, 1, :], in0=wsage[:, m], scalar=sc,
                                         in1=wsplit[:, m, :, 0, :], op0=ALU.mult, op1=ALU.subtract)

            def conv_rest():
                sc = scl[:, S_WG:S_WG + 1]
                ch.link(dve.tensor_scalar(wgs[:, :, 0, :], wgate[:, :, :], sc, None, ALU.mult))
                ch.link(dve.scalar_tensor_tensor(out=wgs[:, :, 1, :], in0=wgate[:, :, :], scalar=sc, in1=wgs[:, :, 0, :],
                                                 op0=ALU.mult, op1=ALU.subtract))
                dve.nop().then_inc(s_wsplit, 1)
                dve.wait_ge(s_deg_in, 16)
                ch.link(dve.tensor_scalar(deg[:, :], deg[:, :], 1.0, None, ALU.max))
                ch.link(dve.reciprocal(rdeg[:, :], deg[:, :]))

            def expert_scales():
                dve.wait_ge(s_ss, 2)
                dve.tensor_copy(ssum[:, S_G:S_G + 1], ss[:, 6:7])
                sw = ss[:, 7:7 + NW].rearrange("p (e k w) -> p k e w", k=2, w=2)
                for k in range(2):
                    last = dve.tensor_reduce(ssum[:, S_E1 + k:S_E1 + k + 1], sw[:, k], mybir.AxisListType.XY, ALU.add)
                last.then_inc(s_ssum, 1)
                dve.wait_ge(s_bound, 2)
                scales(S_E1, S_G + 1, S_E1, S_G, 16.1)
                ch.link(dve.tensor_scalar(cc[:, 3:4], inv[:, S_E1:S_E1 + 1], 1.0 / XSCALE, None, ALU.mult))
                factor(4, inv[:, S_G:S_G + 1], inv[:, S_E2:S_E2 + 1], 1.0)
                dve.nop().then_inc(s_scales_e, 1)

            def start_tile(u, slot):
                ch.link(dve.tensor_copy(keyt[slot][:, :, :, :], keys[:, :, bass.ds(u * GPT, GPT)].rearrange(
                    "p k (g a) -> p k g a", a=1).to_broadcast([P, 2, GPT, 2])))

            def onehots_of(u, slot, j, first=False):
                if not first:
                    dve.wait_ge(s_cnt, BPT * u + j - RING + 1)
                for k, (oh, width) in enumerate(((oh1, P), (oh2, KW))):
                    half = [P, SUB, width // 2, 2]
                    last = dve.tensor_tensor(
                        oh[:, j % RING, :, :].rearrange("p s (n a) -> p s n a", a=2),
                        iota[:, 0:width].rearrange("p (s n a) -> p s n a", s=1, a=2).to_broadcast(half),
                        keyt[slot][:, k, j * SUB:(j + 1) * SUB, :].rearrange("p s (n a) -> p s n a", n=1
                                                                             ).to_broadcast(half), ALU.is_equal)
                last.then_inc(s_oh, 1)

            def mean(p, slot, layer):
                dve.wait_ge(s_acc[layer], p + 1)
                r = rdeg[:, bass.ds(p, 1)]
                ch.link(dve.tensor_scalar(meanhl[slot][:, 0:D], acc[slot][:, 0:D], r, None, ALU.mult))
                dve.scalar_tensor_tensor(out=meanhl[slot][:, D:2 * D], in0=acc[slot][:, 0:D], scalar=r,
                                         in1=meanhl[slot][:, 0:D], op0=ALU.mult, op1=ALU.subtract
                                         ).then_inc(s_mean[layer], 1)

            def relu(p):
                dve.wait_ge(s_dense[0], p + 1)
                ch.link(dve.scalar_tensor_tensor(out=tmp[:, :], in0=dps[:, 0:D], scalar=cc[:, 0:1],
                                                 in1=biasb[:, 0, :], op0=ALU.mult, op1=ALU.add))
                hi = hs[:, bass.ds(p, 1), 0:D].rearrange("p a c -> p (a c)")
                lo = hs[:, bass.ds(p, 1), D:2 * D].rearrange("p a c -> p (a c)")
                ch.link(dve.tensor_scalar(hi, tmp[:, :], 0.0, None, ALU.max))
                dve.scalar_tensor_tensor(out=lo, in0=tmp[:, :], scalar=0.0, in1=hi, op0=ALU.max,
                                         op1=ALU.subtract).then_inc(s_h, 1)

            def step1(t, slot, build=True, post=True):
                if build:
                    start_tile(t + 1, 1 - slot)
                for j in range(BPT):
                    if build:
                        onehots_of(t + 1, 1 - slot, j)
                    if post and j == M_AT:
                        mean(t - 1, 1 - slot, 0)
                    if post and j == H_AT:
                        relu(t - 1)

            def general(t, layer):
                gbase = (t + layer * NT) * ECH
                dve.nop().then_inc(s_alone_dve, 1)
                with dve.Fori(0, ECH) as c:
                    n = gbase + c
                    dve.wait_ge(s_gedge, 16 * n + 16)
                    dve.tensor_scalar(gkey[:, 0:1], gedge[:, 0:1], gtile[:, 0:1], None, ALU.subtract).then_inc(s_gkey, 1)
                    dve.wait_ge(s_gkey, n + 1)
                    dve.tensor_scalar(goh, iota[:, 0:P], gkey[:, 0:1], None, ALU.is_equal).then_inc(s_goh, 1)
                dve.wait_ge(s_acc[layer], t + 1)

            def next_tile():
                ch.link(dve.tensor_scalar(gtile[:, 0:1], gtile[:, 0:1], float(P), None, ALU.add))

            def degree(t):
                ch.link(dve.tensor_scalar(gkey[:, 1:2], dgp, 1.0, None, ALU.max))
                ch.link(dve.reciprocal(rdeg[:, bass.ds(t, 1)], gkey[:, 1:2]))

            dve.wait_ge(s_flag, 1)
            bad = dve.value_load(flag[0:1, 0:1], min_val=0, max_val=1)
            base = ch.start + ch.n
            with dve.If(bad < 1):
                start_tile(0, 0)
                for j in range(BPT):
                    onehots_of(0, 0, j, first=j < RING)
                start_tile(1, 1)
                for j in range(BPT):
                    onehots_of(1, 1, j)
                    if j == 1:
                        conv_scales()
                    if j in (4, 6, 8, 10):
                        conv_weights(j // 2 - 2)
                    if j == 12:
                        conv_rest()
                step1(1, 1)

                def steps(a, b):
                    m = ch.start + ch.n
                    with dve.Fori(a, b) as i:
                        ch.at(m + 8 * (i - a))
                        step1(2 * i, 0)
                        step1(2 * i + 1, 1)
                        assert ch.n == 8
                    ch.at(m + 8 * (b - a))
                steps(1, NE + 1)
                expert_scales()
                steps(NE + 1, (NT - 1) // 2)
                step1(NT - 1, 0, build=False)
                mean(NT - 1, 0, 0)
                relu(NT - 1)
                fast_n = ch.start + ch.n
            with dve.Else():
                ch.at(base)
                conv_scales()
                for m in range(4):
                    conv_weights(m)
                conv_rest()
                expert_scales()
                ch.link(dve.memset(gtile[:, :], 0.0))

                def tile(t, slot):
                    general(t, 0)
                    degree(t)
                    mean(t, slot, 0)
                    relu(t)
                    next_tile()
                m = ch.start + ch.n
                with dve.Fori(0, NT // 2) as i:
                    ch.at(m + 12 * i)
                    tile(2 * i, 0)
                    tile(2 * i + 1, 1)
                    assert ch.n == 12
                ch.at(m + 12 * (NT // 2))
                tile(NT - 1, 0)
                ch.link(dve.memset(gtile[:, :], float((NT - 1) * P)))

            ch2 = Chain(dve, s_dve2)
            PER2 = 30

            def mean2(p, slot):
                link = ch2.link
                dve.wait_ge(s_acc[1], p + 1)
                dve.nop().then_inc(s_alone_dve, 1)
                r = rdeg[:, bass.ds(NT - 1 - p, 1)]
                link(dve.tensor_scalar(meanhl[slot][:, 0:D], acc[1 - slot][:, 0:D], r, None, ALU.mult))
                dve.scalar_tensor_tensor(out=meanhl[slot][:, D:2 * D], in0=acc[1 - slot][:, 0:D], scalar=r,
                                         in1=meanhl[slot][:, 0:D], op0=ALU.mult, op1=ALU.subtract
                                         ).then_inc(s_mean[1], 1)

            def gate2(p, slot, first=False):
                link = ch2.link
                dve.wait_ge(s_dense[1], p + 1)
                if not first:
                    dve.wait_ge(s_x1_out[slot], 8 * (p - slot))
                link(dve.scalar_tensor_tensor(out=tmp[:, :], in0=dps[:, 0:D], scalar=cc[:, 1:2],
                                              in1=biasb[:, 1, :], op0=ALU.mult, op1=ALU.add))
                dve.wait_ge(s_xres[slot], 8 * (p - slot) + 16)
                dve.tensor_tensor(x1t[slot], tmp[:, :], xres[slot], ALU.add).then_inc(s_x1, 1)
                dve.wait_ge(s_x1, p + 1)
                link(dve.bn_stats(st2[:, :], x1t[slot]))
                dve.nop().then_inc(s_alone_dve, 1)
                dve.bn_aggr(mv2[:, :], st2[:, :]).then_inc(s_var2, 1)
                dve.wait_ge(s_sd2, p + 1)
                link(dve.reciprocal(rs2[:, :], sd2[:, :]))
                link(dve.tensor_scalar(x2s, x1t[slot], mv2[:, 0:1], rs2[:, 0:1], ALU.subtract, ALU.mult))
                if not first:
                    dve.wait_ge(s_scat[slot], 32 * (p - slot))
                link(dve.tensor_copy(x2[slot][:, 0:D], x2s))
                dve.tensor_tensor(x2[slot][:, D:2 * D], x2s, x2[slot][:, 0:D], ALU.subtract).then_inc(s_x2, 1)
                dve.wait_ge(s_logits, p + 1)
                link(dve.scalar_tensor_tensor(out=lg[:, :], in0=lgp, scalar=cc[:, 2:3], in1=bgb[:, :],
                                              op0=ALU.mult, op1=ALU.add))
                dve.nop().then_inc(s_alone_dve, 1)
                link(dve.max(m8[:, :], lg[:, :]))
                dve.nop().then_inc(s_alone_dve, 1)
                link(dve.max_index(i8[:, :], m8[:, :], lg[:, :]))
                dve.tensor_tensor(diff[slot][:, :], m8[:, 1:2], m8[:, 0:1], ALU.subtract).then_inc(s_diff, 1)
                link(dve.tensor_copy(e01[:, :], i8[:, 0:2]))
                for k in range(2):
                    last = dve.tensor_scalar(sel[:, k, :], iota[:, 0:NE], e01[:, k:k + 1], None, ALU.is_equal)
                link(last)
                dve.tensor_tensor(mask[:, :], sel[:, 0, :], sel[:, 1, :], ALU.add).then_inc(s_mask, 1)

            def place2(p, slot):
                link = ch2.link
                dve.wait_ge(s_rank, p + 1)
                link(dve.tensor_tensor(rk[:, :], rkp, ecap[:, :], ALU.add))
                for k in range(2):
                    last = dve.tensor_tensor_reduce(out=jk[:, k, :], in0=sel[:, k, :], in1=rk[:, :], scale=1.0,
                                                    scalar=0.0, op0=ALU.mult, op1=ALU.add,
                                                    accum_out=posf[:, k:k + 1])
                link(last)
                for k in range(2):
                    dve.tensor_copy(posi[slot][k][:, :], posf[:, k:k + 1])
                dve.tensor_copy(meta[slot][:, :, 0], ids_i[:, bass.ds(NT - 1 - p, 1)].to_broadcast([P, 2]))
                dve.wait_ge(s_zz, p + 1)
                link(dve.tensor_scalar(zp[:, :], zz[slot][:, :], 1.0, None, ALU.add))
                link(dve.reciprocal(w0[:, :], zp[:, :]))
                wm = meta[slot][:, :, :].bitcast(F32)
                dve.tensor_copy(wm[:, 0, 1:2], w0[:, :])
                dve.tensor_tensor(wm[:, 1, 1:2], w0[:, :], zz[slot][:, :], ALU.mult)
                dve.tensor_tensor(msum[:, :], msum[:, :], mask[:, :], ALU.add).then_inc(s_pos, 1)
                dve.wait_ge(s_pos, p + 1)


            def rest2(p, slot, first=False):
                gate2(p, slot, first)
                mean2(p + 1, 1 - slot)
                place2(p, slot)
            with dve.If(bad < 1):
                mean2(0, 0)
                rest2(0, 0, True)
                rest2(1, 1, True)
                m = ch2.n
                with dve.Fori(1, NT // 2) as i:
                    ch2.at(m + PER2 * (i - 1))
                    rest2(2 * i, 0)
                    rest2(2 * i + 1, 1)
                    assert ch2.n == PER2, ch2.n
                ch2.at(m + PER2 * (NT // 2 - 1))
                gate2(NT - 1, 0)
                place2(NT - 1, 0)
            with dve.Else():
                ch2.at(0)

                def tile2(t, slot, first=False):
                    general(t, 1)
                    mean2(t, slot)
                    gate2(t, slot, first)
                    place2(t, slot)
                    ch2.link(dve.tensor_scalar(gtile[:, 0:1], gtile[:, 0:1], -float(P), None, ALU.add))
                tile2(0, 0, True)
                tile2(1, 1, True)
                m = ch2.n
                with dve.Fori(1, NT // 2) as i:
                    ch2.at(m + (PER2 + 2) * (i - 1))
                    tile2(2 * i, 0)
                    tile2(2 * i + 1, 1)
                    assert ch2.n == PER2 + 2, ch2.n
                ch2.at(m + (PER2 + 2) * (NT // 2 - 1))
                tile2(NT - 1, 0)

            ch = Chain(dve, s_dve3)
            link = ch.link
            dve.wait_ge(s_cntp, 1)
            link(dve.tensor_copy(cntb[:, :], cnp))
            link(dve.tensor_tensor(padf[:, :], ecap[:, :], cntb[:, :], ALU.add))
            dve.tensor_copy(padi[:, :], padf[0:1, :]).then_inc(s_pads, 1)
            link(dve.tensor_scalar(cti[:, 0, :], cntb[:, :], float(FT - 1), None, ALU.add))
            link(dve.tensor_scalar(cti[:, 1, :], cti[:, 0, :], FT.bit_length() - 1, None, ALU.logical_shift_right))
            link(dve.tensor_copy(nte[:, :], cti[:, 1, :]))
            link(dve.tensor_copy(cend[:, 0:1], nte[:, 0:1]))
            for e in range(1, NE):
                link(dve.tensor_tensor(cend[:, e:e + 1], cend[:, e - 1:e], nte[:, e:e + 1], ALU.add))
            tile_i, ge, ex, st, loc, rowf, lastf = (ftab[:, k, :] for k in range(7))
            ended, before_it = etab
            every = [1, NE, NF]
            link(dve.tensor_tensor(ended, tile_i.rearrange("p (e f) -> p e f", e=1).to_broadcast(every),
                                   cend[0:1, :].rearrange("p (e f) -> p e f", f=1).to_broadcast(every), ALU.is_ge))
            link(dve.tensor_tensor(before_it, ended, nte[0:1, :].rearrange("p (e f) -> p e f", f=1
                                                                           ).to_broadcast(every), ALU.mult))
            dve.tensor_reduce(ex, ended.rearrange("p e f -> p f e"), AX_X, ALU.add)
            link(dve.tensor_reduce(st, before_it.rearrange("p e f -> p f e"), AX_X, ALU.add))
            link(dve.tensor_scalar(ge, tile_i, cend[0:1, NE - 1:NE], None, ALU.is_ge))
            link(dve.tensor_tensor(loc, tile_i, st, ALU.subtract))
            link(dve.tensor_scalar(loc, loc, float(FT), None, ALU.mult))
            link(dve.scalar_tensor_tensor(out=rowf, in0=ex, scalar=float(CAPR), in1=loc, op0=ALU.mult, op1=ALU.add))
            link(dve.tensor_scalar(tab[:, 0, :], ex, float(NE - 1), None, ALU.min))
            link(dve.tensor_scalar(lastf, rowf, -1.0, float(NE * CAPR), ALU.mult, ALU.add))
            link(dve.tensor_tensor(lastf, lastf, ge, ALU.mult))
            link(dve.tensor_tensor(tab[:, 1, :], rowf, lastf, ALU.add))
            dve.nop().then_inc(s_tab, 1)

            def xt_copy(f, slot):
                dve.wait_ge(s_xt, f + 1)
                dve.tensor_copy(xT[slot][:, 2:4, :], xtp[1]).then_inc(s_xtc, 1)

            def y_bias(f, slot, h, e, stored):
                if not h:
                    dve.wait_ge(s_mm2, HC * f + HC)
                    if stored is not None:
                        dve.wait_ge(s_add[slot], stored)
                dve.scalar_tensor_tensor(out=yt[slot][:, h, :], in0=yps[slot][:, h, :], scalar=cc[:, 4:5],
                                         in1=eb2b[:, bass.ds(e, 1), :].rearrange("p a c -> p (a c)"),
                                         op0=ALU.mult, op1=ALU.add).then_inc(s_yh, 1)

            def y_weight(f, slot, h):
                if not h:
                    dve.wait_ge(s_meta[slot], 8 * (f - slot) + 16)
                dve.wait_ge(s_yh, 2 * f + h + 1)
                wm = ml[slot][:, :, :].bitcast(F32)
                dve.tensor_scalar(yt[slot][:, h, :], yt[slot][:, h, :], wm[:, h, 1:2], None, ALU.mult
                                  ).then_inc(s_y, 1)

            def expert_of(f):
                return dve.value_load(tab[0:1, 0, bass.ds(f, 1)], min_val=0, max_val=NE - 1)

            def step(f, slot, nxt=True, prev=True, first=False, stored=None):
                for c in range(HC):
                    n = HC * f + c
                    dve.wait_ge(s_gel, n + 1)
                    if not (first and c < 4):
                        dve.wait_ge(s_mm2, n - 3)
                    dve.tensor_scalar(ghl[c % 4][:, 0, :], gel[c % 2], scl[:, S_G:S_G + 1], None, ALU.mult
                                      ).then_inc(s_gh, 1)
                    dve.wait_ge(s_gh, n + 1)
                    dve.scalar_tensor_tensor(out=ghl[c % 4][:, 1, :], in0=gel[c % 2], scalar=scl[:, S_G:S_G + 1],
                                             in1=ghl[c % 4][:, 0, :], op0=ALU.mult, op1=ALU.subtract
                                             ).then_inc(s_g, 1)
                    if nxt and c == XT_AT:
                        xt_copy(f + 1, 1 - slot)
                    if prev:
                        if c == 0:
                            ep = expert_of(f - 1)
                        if c - Y_AT in (0, 1):
                            y_bias(f - 1, 1 - slot, c - Y_AT, ep, stored)
                        if c - YW_AT in (0, 1):
                            y_weight(f - 1, 1 - slot, c - YW_AT)
            dve.wait_ge(s_eb2, 16)
            xt_copy(0, 0)
            step(0, 0, prev=False, first=True)
            step(1, 1)
            step(2, 0)
            step(3, 1, stored=32)
            with dve.Fori(2, (NF - 1) // 2) as i:
                step(2 * i, 0, stored=32 * i - 32)
                step(2 * i + 1, 1, stored=32 * i)
            step(NF - 1, 0, nxt=False, stored=32 * ((NF - 1) // 2) - 32)
            ep = expert_of(NF - 1)
            for h in range(2):
                y_bias(NF - 1, 0, h, ep, 32 * ((NF - 1) // 2))
            for h in range(2):
                y_weight(NF - 1, 0, h)


_INS = ['x', 'edges', 'L0_gnn_W1_l', 'L0_gnn_b1', 'L0_gnn_W1_r', 'L0_gnn_W2_l', 'L0_gnn_b2', 'L0_gnn_W2_r',
        'L0_ffn_Wg', 'L0_ffn_bg', 'L0_ffn_W1', 'L0_ffn_b1', 'L0_ffn_W2', 'L0_ffn_b2']


def kernel(**inputs):
    import numpy as np
    import concourse.bacc as bacc
    from concourse.bass_utils import run_bass_kernel_spmd

    nc = bacc.Bacc("TRN2", target_bir_lowering=False, num_devices=1)
    arrays, args = {}, []
    pad = EPAD + E_ROWS - N_EDGES
    inputs["edges"] = np.stack([np.pad(inputs["dst"], (0, pad), constant_values=DST_PAD),
                                np.pad(inputs["src"], (0, pad))], axis=1).reshape(-1)
    for name in _INS:
        a = np.ascontiguousarray(inputs[name])
        if name == 'x':
            a = np.pad(a, ((0, NPAD - N_NODES), (0, 0)))
        arrays["in_" + name] = a
        args.append(nc.dram_tensor("in_" + name, a.shape, mybir.dt.from_np(a.dtype), kind="ExternalInput").ap())
    out = nc.dram_tensor("out_nodes", (NPAD + FT, D), F32, kind="ExternalOutput").ap()
    build(nc, *args, out)
    r = run_bass_kernel_spmd(nc, [arrays], core_ids=[0])
    return r.results[0]["out_nodes"][:N_NODES]
```
